# Optimizing a Trainium2 kernel written in Bass

```python
import numpy as np
import jax
import jax.numpy as jnp

def _softmax(x, axis=-1):
    return jax.nn.softmax(x, axis=axis)

def _gelu(x):
    return jax.nn.gelu(x, approximate=True)

def _silu(x):
    return jax.nn.silu(x)

def _sigmoid(x):
    return jax.nn.sigmoid(x)

def _layernorm(x, axis=-1, eps=1e-05):
    m = jnp.mean(x, axis=axis, keepdims=True)
    v = jnp.var(x, axis=axis, keepdims=True)
    return (x - m) / jnp.sqrt(v + eps)

def _scatter_add(tgt, idx, src, axis=0):
    return tgt.at[idx].add(src)

def _segment_sum(src, seg, n):
    return jax.ops.segment_sum(src, seg, n)
kernel_name = 'mk_audio_tower_d1_tok_audfeat256_r4_86b171'

def setup_inputs(seed: int=0):
    np.random.seed(seed)
    _w = jnp.asarray

    def _rec_inputs():
        import jax
        import jax.numpy as jnp
        _rk = jax.random.key(seed)
        x = -0.000154596 + 0.999967 * jax.random.normal(jax.random.fold_in(_rk, 1), (16, 750, 64), jnp.float32)
        return x
    x = _rec_inputs()

    def _L0_tok_setup():
        import jax, jax.numpy as jnp
        import numpy as np
        RATIO = 0.5
        key = jax.random.key(seed)
        k1, k2 = jax.random.split(key)
        B, N, F = (32, 4096, 64)
        inputs = jax.random.normal(k1, (B, N, F), dtype=jnp.float32)
        score_proj = jax.random.normal(k2, (F, 1), dtype=jnp.float32) * (1.0 / np.sqrt(F))
        return {'inputs': inputs, 'score_proj': score_proj}
    _L0_tok_all = _L0_tok_setup()
    _L0_tok_in = {k: v for k, v in _L0_tok_all.items() if k in ('score_proj',)}
    del _L0_tok_all

    def _L0_attn_setup():
        import jax, jax.numpy as jnp
        import numpy as np
        B, N, C, H = (1024, 64, 64, 8)
        key = jax.random.key(seed)
        ks = jax.random.split(key, 6)
        return {'x': jax.random.normal(ks[0], (B, N, C), dtype=jnp.float32), 'qkv_w': jax.random.normal(ks[1], (C, 3 * C), dtype=jnp.float32) * 0.02, 'qkv_b': jax.random.normal(ks[2], (3 * C,), dtype=jnp.float32) * 0.02, 'proj_w': jax.random.normal(ks[3], (C, C), dtype=jnp.float32) * 0.02, 'proj_b': jax.random.normal(ks[4], (C,), dtype=jnp.float32) * 0.02, 'rpb_table': jax.random.normal(ks[5], (2 * N - 1, H), dtype=jnp.float32) * 0.02}
    _L0_attn_all = _L0_attn_setup()
    _L0_attn_in = {k: v for k, v in _L0_attn_all.items() if k in ('qkv_w', 'qkv_b', 'proj_w', 'proj_b', 'rpb_table')}
    del _L0_attn_all

    def _L0_ffn_setup():
        import jax, jax.numpy as jnp
        import numpy as np
        DIM = 64
        HEADS = 8
        NUM_KEYS = 64
        NUM_KV = NUM_KEYS ** 2
        PK_TOPK = 16
        FINAL_TOPK = 16
        DIM_KEY = DIM // 2
        P = 2

        def _pk(x, Wq_pk, pk_keys):
            b, n, _ = x.shape
            q = (x @ Wq_pk).reshape(b, n, P, HEADS, DIM_KEY).transpose(2, 0, 1, 3, 4)
            sim = jnp.einsum('pbnhd,pkhd->pbnhk', q, pk_keys)
            scores, idx = jax.lax.top_k(sim, PK_TOPK)
            idx0 = idx[0]
            idx1 = idx[1] * NUM_KEYS
            index = (idx0[..., :, None] + idx1[..., None, :]).reshape(b, n, HEADS, PK_TOPK * PK_TOPK)
            score = (scores[0][..., :, None] + scores[1][..., None, :]).reshape(b, n, HEADS, PK_TOPK * PK_TOPK)
            final_scores, pk_idx = jax.lax.top_k(score, FINAL_TOPK)
            final_indices = jnp.take_along_axis(index, pk_idx, axis=-1)
            final_scores = jax.nn.softmax(final_scores, axis=-1)
            return (final_scores, final_indices)
        key = jax.random.key(seed)
        ks = jax.random.split(key, 7)
        b, n = (2, 256)
        std = 0.02
        x = jax.random.normal(ks[0], (b, n, DIM), dtype=jnp.float32)
        Wq_pk = jax.random.normal(ks[1], (DIM, P * HEADS * DIM_KEY), dtype=jnp.float32) * std
        pk_keys = jax.random.normal(ks[2], (P, NUM_KEYS, HEADS, DIM_KEY), dtype=jnp.float32) * std
        Wq = jax.random.normal(ks[3], (DIM, HEADS * DIM), dtype=jnp.float32) * std
        keys_table = jax.random.normal(ks[4], (NUM_KV * HEADS, DIM), dtype=jnp.float32) * std
        values_table = jax.random.normal(ks[5], (NUM_KV * HEADS, DIM), dtype=jnp.float32) * std
        Wo = jax.random.normal(ks[6], (DIM * HEADS, DIM), dtype=jnp.float32) * std
        return {'x': x, 'Wq_pk': Wq_pk, 'pk_keys': pk_keys, 'Wq': Wq, 'keys_table': keys_table, 'values_table': values_table, 'Wo': Wo}
    _L0_ffn_all = _L0_ffn_setup()
    _L0_ffn_in = {k: v for k, v in _L0_ffn_all.items() if k in ('Wq_pk', 'pk_keys', 'Wq', 'keys_table', 'values_table', 'Wo')}
    del _L0_ffn_all
    return {'x': x, 'L0_tok_score_proj': _L0_tok_in['score_proj'], 'L0_attn_qkv_w': _L0_attn_in['qkv_w'], 'L0_attn_qkv_b': _L0_attn_in['qkv_b'], 'L0_attn_proj_w': _L0_attn_in['proj_w'], 'L0_attn_proj_b': _L0_attn_in['proj_b'], 'L0_attn_rpb_table': _L0_attn_in['rpb_table'], 'L0_ffn_Wq_pk': _L0_ffn_in['Wq_pk'], 'L0_ffn_pk_keys': _L0_ffn_in['pk_keys'], 'L0_ffn_Wq': _L0_ffn_in['Wq'], 'L0_ffn_keys_table': _L0_ffn_in['keys_table'], 'L0_ffn_values_table': _L0_ffn_in['values_table'], 'L0_ffn_Wo': _L0_ffn_in['Wo']}

def reference(x, L0_tok_score_proj, L0_attn_qkv_w, L0_attn_qkv_b, L0_attn_proj_w, L0_attn_proj_b, L0_attn_rpb_table, L0_ffn_Wq_pk, L0_ffn_pk_keys, L0_ffn_Wq, L0_ffn_keys_table, L0_ffn_values_table, L0_ffn_Wo):
    import jax
    import jax.numpy as jnp

    def _L0_tok_ref(inputs, score_proj):
        import jax, jax.numpy as jnp
        import numpy as np
        RATIO = 0.5
        N = inputs.shape[1]
        k = max(int(N * RATIO), 1)
        scores = jnp.einsum('bnf,fo->bn', inputs, score_proj)
        _, top_idx = jax.lax.top_k(scores, k)
        sel_feat = jnp.take_along_axis(inputs, top_idx[:, :, None], axis=1)
        sel_scores = jnp.take_along_axis(scores, top_idx, axis=1)
        gate = jax.nn.sigmoid(sel_scores)[:, :, None]
        return sel_feat * gate

    def _L0_attn_ref(x, qkv_w, qkv_b, proj_w, proj_b, rpb_table):
        import jax, jax.numpy as jnp
        import numpy as np
        B, N, C, H = (1024, 64, 64, 8)
        Bw, Nw, Cd = x.shape
        nh = rpb_table.shape[1]
        dh = Cd // nh
        scale = dh ** (-0.5)
        qkv = (x @ qkv_w + qkv_b).reshape(Bw, Nw, 3, nh, dh)
        q, k, v = (qkv[:, :, 0], qkv[:, :, 1], qkv[:, :, 2])
        attn = jnp.einsum('bnhd,bmhd->bhnm', q * scale, k)
        coords = jnp.arange(Nw)
        rel_idx = coords[:, None] - coords[None, :] + (Nw - 1)
        bias = jnp.transpose(rpb_table[rel_idx], (2, 0, 1))
        attn = jax.nn.softmax(attn + bias[None], axis=-1)
        out = jnp.einsum('bhnm,bmhd->bnhd', attn, v).reshape(Bw, Nw, Cd)
        return out @ proj_w + proj_b

    def _L0_ffn_ref(x, Wq_pk, pk_keys, Wq, keys_table, values_table, Wo):
        import jax, jax.numpy as jnp
        import numpy as np
        DIM = 64
        HEADS = 8
        NUM_KEYS = 64
        NUM_KV = NUM_KEYS ** 2
        PK_TOPK = 16
        FINAL_TOPK = 16
        DIM_KEY = DIM // 2
        P = 2

        def _pk(x, Wq_pk, pk_keys):
            b, n, _ = x.shape
            q = (x @ Wq_pk).reshape(b, n, P, HEADS, DIM_KEY).transpose(2, 0, 1, 3, 4)
            sim = jnp.einsum('pbnhd,pkhd->pbnhk', q, pk_keys)
            scores, idx = jax.lax.top_k(sim, PK_TOPK)
            idx0 = idx[0]
            idx1 = idx[1] * NUM_KEYS
            index = (idx0[..., :, None] + idx1[..., None, :]).reshape(b, n, HEADS, PK_TOPK * PK_TOPK)
            score = (scores[0][..., :, None] + scores[1][..., None, :]).reshape(b, n, HEADS, PK_TOPK * PK_TOPK)
            final_scores, pk_idx = jax.lax.top_k(score, FINAL_TOPK)
            final_indices = jnp.take_along_axis(index, pk_idx, axis=-1)
            final_scores = jax.nn.softmax(final_scores, axis=-1)
            return (final_scores, final_indices)
        b, n, d = x.shape
        q = (x @ Wq).reshape(b, n, HEADS, DIM) * DIM ** (-0.5)
        kv_scores, indices = _pk(x, Wq_pk, pk_keys)
        offsets = jnp.arange(HEADS, dtype=indices.dtype) * NUM_KV
        ind = indices + offsets[None, None, :, None]
        k = jnp.einsum('bnhk,bnhkd->bnhd', kv_scores, keys_table[ind])
        v = jnp.einsum('bnhk,bnhkd->bnhd', kv_scores, values_table[ind])
        sim = jnp.einsum('bihd,bjhd->bhij', q, k)
        neg = -jnp.finfo(sim.dtype).max
        causal = jnp.tril(jnp.ones((n, n), dtype=bool))
        sim = jnp.where(causal, sim, neg)
        attn = jax.nn.softmax(sim, axis=-1)
        out = jnp.einsum('bhij,bjhd->bhid', attn, v)
        out = out.transpose(0, 2, 1, 3).reshape(b, n, HEADS * DIM)
        return out @ Wo
    h = _L0_tok_ref(x, L0_tok_score_proj)
    h = h + _L0_attn_ref(_layernorm(h, axis=-1), L0_attn_qkv_w, L0_attn_qkv_b, L0_attn_proj_w, L0_attn_proj_b, L0_attn_rpb_table)
    h = h + _L0_ffn_ref(_layernorm(h, axis=-1), L0_ffn_Wq_pk, L0_ffn_pk_keys, L0_ffn_Wq, L0_ffn_keys_table, L0_ffn_values_table, L0_ffn_Wo)
    return h

_drawn_inputs = setup_inputs


def setup_inputs(seed=0):
    import zlib

    import numpy as np

    out = dict(_drawn_inputs(seed))
    spreads = {}
    factors = {'L0_attn_qkv_w': 8.0,
     'L0_attn_qkv_b': 8.0,
     'L0_attn_proj_w': 8.0,
     'L0_attn_rpb_table': 31.384,
     'L0_ffn_Wq_pk': 8.0,
     'L0_ffn_pk_keys': 8.0,
     'L0_ffn_Wq': 64.0,
     'L0_ffn_keys_table': 64.0,
     'L0_ffn_values_table': 8.0,
     'L0_ffn_Wo': 8.0}
    for name, (base, spread) in spreads.items():
        noise = np.random.default_rng([zlib.crc32(name.encode()), seed]).standard_normal(out[name].shape)
        drawn = base * np.exp(spread * noise) if base else spread * noise
        out[name] = jnp.asarray(drawn.astype(out[name].dtype))
    for name, factor in factors.items():
        out[name] = (out[name] * factor).astype(out[name].dtype)
    return out
```

```python
BATCH, TOKENS, PICKED, DIM, HEADS = 16, 750, 375, 64, 8
TP = 125
NT = PICKED // TP
XT = TOKENS // TP
DH = DIM // HEADS
LAST_REL = 126
KEYS, KEY_DIM, TOPK = 64, 32, 16
CAND = sum(17 // (i + 1) for i in range(17))
SLOTS = 256
PER_HEAD = SLOTS // HEADS
COMBOS = 4
TIE = 1e-37
SPAN = 100.0
SHIFT = SPAN / 2
SWAP_HEADS = (3, 7)
BIG = 1e30


def table_slot(h):
    return 3 if h in SWAP_HEADS else h


def select_steps():
    s = [("V", ("score_mul",), .45), ("V", ("score",), .45), ("A", ("eneg",), .2), ("T", ("rowbc",), .4),
         ("V", ("den",), .1), ("V", ("gate",), .1), ("V", ("xg",), .45)]
    s += [("V", ("rank", t), 1.) for t in range(XT)] + [("V", ("ranks",), .1)]
    s += [("V", ("hot", t), .3) for t in range(XT)]
    s += [("T", ("pick",), 2.), ("A", ("h1",), .4)]
    s += norm_steps(1)
    s += [("T", ("v",), .3), ("A", ("v",), .4)]
    for g in range(2):
        s += [("T", ("q", g), .7), ("A", ("q", g), .5), ("T", ("k", g), .7), ("A", ("k", g), .5)]
        for n in range(12):
            s += [("T", ("qk", g, n), .9), ("V", ("low", g, n), .5), ("A", ("p", g, n), .6), ("T", ("pt", g, n), .3),
                  ("A" if n % 2 else "V", ("ptc", g, n), .5)]
        s += [("T", ("pv_end", g), .4), ("V", ("rz", g), .1), ("V", ("o1", g), .25)]
    s += [("T", ("o1t",), .2), ("A", ("o1t",), .5), ("T", ("proj",), .3), ("V", ("h2",), .3)]
    s += norm_steps(2)
    return s


def norm_steps(i):
    return [("V", ("sum", i), .3), ("V", ("mean", i), .1), ("V", ("cen", i), .3), ("V", ("sq", i), .3),
            ("V", ("var", i), .3), ("V", ("veps", i), .1), ("G", ("rstd", i), .3), ("V", ("xn", i), .3),
            ("T", ("xnt", i), .2), ("A", ("xnt", i), .5)]


def topk_steps(g):
    s = []
    for p in range(2):
        s += [("T", ("qpk", g, p), .7), ("A", ("qpk", g, p), .5)]
    for it in range(NT):
        s += [("T", ("sim", g, it), .9), ("A", ("sim", g, it), .7)]
    for it in range(NT):
        for what in ("max_a", "cut_a", "max_b", "cut_b"):
            s += [("V", (what, g, it, q), .13) for q in range(8)]
        s += [("V", ("max_c", g, it), .6)]
        s += [("V", ("cand", g, it, i), .12) for i in range(7)]
        for what in ("cmax_a", "ccut_a", "cmax_b", "ccut_b"):
            s += [("V", (what, g, it, q), .12) for q in range(4)]
        s += [("V", ("cmax_c", g, it), .3)]
    s += [("V", ("mid", g), .1), ("V", ("floor", g), .1), ("V", ("thr", g), .1), ("V", ("diff", g), .3),
          ("A", ("wexp", g), .4), ("V", ("zk", g), .3), ("V", ("rzk", g), .1),
          ("V", ("off1", g), .1), ("V", ("off0", g), .1)]
    s += [("G", ("shift", g, it), 1.5) for it in range(NT)] + [("G", ("clamp", g, it), 1.) for it in range(NT)]
    return s


def head_steps(h):
    s = [("T", ("kvt", h), .2), ("V", ("kvn", h), .5), ("T", ("knt", h), .2), ("A", ("knt", h), .5)]
    if h % 2 == 0:
        s += [("T", ("q2", h // 2), .7), ("A", ("q2", h // 2), .5)]
    for r in range(2):
        s += [("T", ("qk2", h, r), .7), ("V", ("low2", h, r), .5), ("A", ("p2", h, r), .7), ("T", ("pt2", h, r), .3),
              ("A" if r else "V", ("ptc2", h, r), .5)]
    s += [("T", ("pv2", h), .7), ("V", ("rz2", h), .1), ("V", ("o2", h), .3)]
    if h % 2:
        s += [("T", ("o2t", h // 2), .2), ("A", ("o2t", h // 2), .5), ("T", ("wo", h // 2), .4), ("V", ("acc", h // 2), .3)]
    return s


FRONT = select_steps() + topk_steps(0) + [("G", ("keep_xn2",), .8)] + topk_steps(1)
BACK = [("G", ("keep_h2",), .4)] + [x for h in range(HEADS) for x in head_steps(h)]


def order(steps, engine):
    return [name for e, name, _ in steps if e == engine]


SEQ = {"front": {e: order(FRONT, e) for e in "TVAG"}, "back": {e: order(BACK, e) for e in "TVAG"}}
COUNT = {(t, e): {name: i + 1 for i, name in enumerate(SEQ[t][e])} for t in SEQ for e in "TVAG"}


def place(timeline, thread, steps, first, last, batch):
    total, at = sum(c for _, _, c in steps), 0.0
    for engine, name, cost in steps:
        timeline[min(int(first + at / total * (last - first)), last)].append((thread, engine, name, batch))
        at += cost


def timeline_of(kind):
    line = [[] for _ in range(SLOTS)]
    keep = [("G", ("keep_xn2",), .8)]
    place(line, "front", keep + topk_steps(1), 0, 76, 0)
    if kind != "last":
        place(line, "front", select_steps(), 77, 165, 1)
        place(line, "front", topk_steps(0), 166, 236, 1)
    if kind != "first":
        place(line, "back", head_steps(HEADS - 1), 1, 26, -1)
        line[27].append(("back", "S", ("store",), -1))
    place(line, "back", BACK[:1], 29, 29, 0)
    for h in range(HEADS - 1):
        place(line, "back", head_steps(h), PER_HEAD * (h + 1) + 3, PER_HEAD * (h + 2) - 1, 0)
    for n in range(1, HEADS * COMBOS + (kind != "last")):
        for engine, slot in (("G", -2), ("T", 1), ("A", 2), ("V", 4)):
            line[max(8 * (n - 1) + slot, 0)].insert(0, ("combo", engine, ("combo", n % (HEADS * COMBOS)), n // (HEADS * COMBOS)))
    return line


def build_kernel(nc, x, score_proj, qkv_w, qkv_b, proj_w, proj_b, rpb, wq_pk, pk_keys, wq, kv_table, wo, out):
    from contextlib import ExitStack
    import concourse.bass as bass
    from concourse import mybir

    F32, F16, BF16 = mybir.dt.float32, mybir.dt.float16, mybir.dt.bfloat16
    ALU, ACT, AX = mybir.AluOpType, mybir.ActivationFunctionType, mybir.AxisListType

    with ExitStack() as ctx:
        def sb(name, shape, dt=F32):
            return ctx.enter_context(nc.sbuf_tensor(name, shape, dt))

        def sem(name):
            return ctx.enter_context(nc.semaphore(name))

        table = sb("table", [128, 7, COMBOS, 8, 2 * DIM])
        sel = sb("sel", [128, 8, 128], F16)
        ident = sb("ident", [128, 128])
        identb = sb("identb", [128, 128], BF16)
        flip = sb("flip", [127, 127])
        causal = sb("causal", [TP, TP], BF16)
        ties = sb("ties", [TP, 11 * TP], BF16)
        ranks_row = sb("ranks_row", [TP, PICKED])
        neg_lo = sb("neg_lo", [128, 1])
        w_score = sb("w_score", [TP, DIM])
        w_qk = sb("w_qk", [65, 2, 2, 4, 32])
        w_v = sb("w_v", [65, DIM])
        w_proj = sb("w_proj", [65, DIM])
        w_pk = sb("w_pk", [64, 512])
        w_q2 = sb("w_q2", [64, 512])
        w_o = sb("w_o", [128, 4, DIM])
        w_keys = sb("w_keys", [128, 4, 4, KEYS])
        hankel = sb("hankel", [TP, HEADS, 126])
        rel_tab = sb("rel_tab", [127, HEADS])

        xin = sb("xin", [TP, XT, DIM])
        xw = sb("xw", [TP, XT, DIM])
        xg = sb("xg", [TP, XT, DIM])
        junk = sb("junk", [TP, TOKENS], BF16)
        small = sb("small", [TP, 64])
        score, eneg, den, gate, rank = (small[:, 6 * i:6 * i + 6] for i in range(5))
        attn = sb("attn", [128, 2250])
        hot = attn[0:TP, :].rearrange("p (t r) -> p t r", t=XT)
        qT, kT = attn[:, 0:375], attn[:, 375:750]
        prob = attn[0:TP, 750:1500].rearrange("p (n r) -> p n r", n=2)
        probT = attn[0:TP, 1500:2250].rearrange("p (n r) -> p n r", n=2)
        h1 = sb("h1", [TP, NT, DIM])
        h2 = sb("h2", [TP, NT, DIM])
        cen = sb("cen", [TP, NT, DIM])
        sq = sb("sq", [TP, NT, DIM])
        xn = sb("xn", [TP, NT, DIM])
        stat = sb("stat", [TP, 5, NT])
        half = sb("half", [TP, NT])
        xnT = sb("xnT", [65, PICKED])
        vtok = sb("vtok", [TP, NT, DIM])
        low = sb("low", [TP, 2])
        zsum = sb("zsum", [TP, 24])
        rz = sb("rz", [TP, 24])
        o1 = sb("o1", [TP, NT, DIM])
        xn2 = sb("xn2", [64, PICKED])
        xn2k = sb("xn2k", [64, PICKED])
        qpkT = sb("qpkT", [128, 2, PICKED])
        sims = sb("sims", [TP, 2, NT, 4, 2, KEYS])
        left = sb("left", [TP, 8, KEYS])
        top = sb("top", [TP, NT, 8, 17])
        cand = sb("cand", [TP, 4, CAND])
        best = sb("best", [TP, NT, 4, 17])
        cut = sb("cut", [TP, 3, NT * 4])
        wk = sb("wk", [TP, NT * 4, TOPK])
        wke = sb("wke", [TP, NT * 4, TOPK])
        zk = sb("zk", [TP, NT * 4])
        rzk = sb("rzk", [TP, 2, NT * 4])
        off = sb("off", [TP, NT * 4, 2])

        quarter = sb("quarter", [TP, 2, NT, 2 * KEYS])
        hi = sb("hi", [128, PICKED], F16)
        halves = sb("halves", [128, 2, PICKED], F16)
        weight = sb("weight", [128, 4, PICKED])
        kvT = sb("kvT", [128, PICKED])
        kv = sb("kv", [TP, NT, 128])
        knT = sb("knT", [128, PICKED])
        q2T = sb("q2T", [128, PICKED])
        prob2 = sb("prob2", [TP, 2, PICKED])
        prob2T = sb("prob2T", [TP, 2, NT, TP])
        low2 = sb("low2", [TP, NT])
        z2 = sb("z2", [TP, NT])
        rz2 = sb("rz2", [TP, NT])
        o2 = sb("o2", [TP, NT, 128])
        o2T = knT
        result = sb("result", [TP, NT, DIM])
        shift = sb("shift", [128, 1])

        ext = kvT[0:HEADS, 0:250]

        banks = [ctx.enter_context(nc.psum_tensor(f"bank{i}", [128, 512], F32)) for i in range(8)]
        s_bank, kv_bank, fa, fb, combo_bank, back_bank = banks[0:3], banks[3], banks[4], banks[5], banks[6], banks[7]
        fa2 = [fa, fb]

        done = {(t, e): sem(f"{t}_{e}") for t in ("front", "back") for e in "TVAG"}
        combo_done = {e: sem(f"combo_{e}") for e in "GTAV"}
        pair_scores, pair_exps, pair_weights, pair_sums = sem("pair_scores"), sem("pair_exps"), sem("pair_weights"), sem("pair_sums")
        kv_copied = sem("kv_copied")
        x_loaded, stored = sem("x_loaded"), sem("stored")
        weights_loaded, bias_loaded, hankel_loaded, swap_loaded = sem("weights_loaded"), sem("bias_loaded"), sem("hankel_loaded"), sem("swap_loaded")
        table_loaded = [sem(f"table_loaded{h}") for h in range(HEADS)]
        const_pool, zeroed, const_dve, const_pe, const_act = sem("const_pool"), sem("zeroed"), sem("const_dve"), sem("const_pe"), sem("const_act")
        const_dve0 = sem("const_dve0")
        CONSTS = 24

        def reached(thread, engine, *step, b):
            return done[thread, engine], b * len(SEQ[thread][engine]) + COUNT[thread, engine][step]

        def wait(eng, s, value):
            if isinstance(value, int) and value <= 0:
                return
            eng.wait_ge(s, value)

        def wait_alone(eng, s, value):
            if not isinstance(value, int):
                value = eng.to_reg(value)
                eng.wait_ge(const_pool, CONSTS)
            wait(eng, s, value)

        def after_alone(eng, thread, engine, *step, b):
            wait_alone(eng, *reached(thread, engine, *step, b=b))

        def after(eng, thread, engine, *step, b):
            wait(eng, *reached(thread, engine, *step, b=b))

        def load_table(eng, h, s):
            rows = kv_table[h * 4096:(h + 1) * 4096, :].rearrange("(g b ah a t) c -> a g b ah (t c)", g=2, b=32, ah=2, a=4, t=8)
            for a in range(4):
                for g in range(2):
                    eng.dma_start(table[32 * a:32 * a + 32, table_slot(h), 2 * g:2 * g + 2].rearrange("p ah t c -> p ah (t c)"),
                                  rows[a, g]).then_inc(s, 16)

        block = ctx.enter_context(nc.Block())
        TL = {kind: timeline_of(kind) for kind in ("first", "mid", "last")}
        N_TABLE = 8 * 16
        N_WEIGHTS = 16 * 18
        first_batch, last_batch = 0, BATCH - 1

        def side(kind, slot, engine, steps, b):
            for thread, e, name, ahead in TL[kind][slot]:
                if e == engine:
                    steps[thread, name[0]](b + ahead, *name[1:])

        def prologue(engine, steps):
            for e, name, _ in select_steps() + topk_steps(0):
                if e == engine:
                    steps["front", name[0]](0, *name[1:])
            if engine in "GTAV":
                steps["combo", "combo"](0, 0)

        def run(eng, engine, steps, dense, flush, start=None):
            prologue(engine, steps)
            dense_batch(engine, steps, dense, flush, "first", first_batch)
            with eng.Fori(1, last_batch) as b:
                dense_batch(engine, steps, dense, flush, "mid", b)
            dense_batch(engine, steps, dense, flush, "last", last_batch)
            for e, name, _ in head_steps(HEADS - 1):
                if e == engine:
                    steps["back", name[0]](last_batch, *name[1:])

        def dense_batch(engine, steps, dense, flush, kind, b):
            for u in range(SLOTS):
                dense(b, u)
                side(kind, u, engine, steps, b)
            flush(b)

        @block.sync
        def _(sp):
            def load_x(b):
                if not isinstance(b, int) or b > 0:
                    after(sp, "front", "V", "xg", b=b - 1)
                sp.dma_start(xin[:, :, :], x[b].rearrange("(t p) f -> p t f", p=TP)).then_inc(x_loaded, 16)

            def store(b):
                after(sp, "back", "V", "acc", 3, b=b)
                sp.dma_start(out[b].rearrange("(t p) f -> p t f", p=TP), result[:, :, :]).then_inc(stored, 16)

            load_x(0)
            s = weights_loaded
            sp.dma_start(w_score[:, :], score_proj.rearrange("f o -> (o f)").partition_broadcast(TP)).then_inc(s, 16)
            sp.dma_start(rel_tab[:, :], rpb).then_inc(s, 16)
            sp.wait_ge(zeroed, 2)
            qkv = qkv_w.rearrange("c (k g h d) -> c k g h d", k=3, g=2, h=4)
            qkvb = qkv_b.rearrange("(o k g h d) -> o k g h d", o=1, k=3, g=2, h=4)
            for k in range(2):
                for g in range(2):
                    sp.dma_start(w_qk[0:64, k, g, :, 0:DH], qkv[:, k, g]).then_inc(s, 16)
                    sp.dma_start(w_qk[64:65, k, g, :, 0:DH], qkvb[:, k, g]).then_inc(s, 16)
            sp.dma_start(w_v[0:64, :], qkv_w[:, 128:192]).then_inc(s, 16)
            sp.dma_start(w_v[64:65, :], qkv_b.rearrange("(o n) -> o n", o=1)[:, 128:192]).then_inc(s, 16)
            sp.dma_start(w_proj[0:64, :], proj_w).then_inc(s, 16)
            sp.dma_start(w_proj[64:65, :], proj_b.rearrange("(o n) -> o n", o=1)).then_inc(s, 16)
            sp.dma_start(w_pk[:, :], wq_pk).then_inc(s, 16)
            sp.dma_start(w_q2[:, :], wq).then_inc(s, 16)
            sp.dma_start(w_o[:, :, :], wo.rearrange("(j p) n -> p j n", p=128)).then_inc(s, 16)
            sp.dma_start(attn[0:64, 0:512].rearrange("p (q n) -> p q n", q=2), pk_keys.rearrange("q k h d -> k q (h d)")).then_inc(s, 16)
            sp.wait_ge(const_dve, 1)
            for h in range(HEADS):
                row = ext[h:h + 1, :]
                sp.dma_start(hankel[:, h, :], bass.AP(row.tensor, row.offset, [row.ap[0], [1, TP], [1, 126]])).then_inc(hankel_loaded, 16)
            for h in range(HEADS - 1):
                load_table(sp, h, table_loaded[h])

            def batch(kind, b):
                if kind != "last":
                    load_x(b + 1)
                if kind != "first":
                    store(b - 1)
                sp.wait_ge(pair_sums, b * SLOTS + 4 * PER_HEAD)
                load_table(sp, 7, swap_loaded)
                if kind != "last":
                    sp.wait_ge(pair_sums, b * SLOTS + SLOTS)
                    load_table(sp, 3, swap_loaded)

            batch("first", 0)
            with sp.Fori(1, last_batch) as b:
                batch("mid", b)
            batch("last", last_batch)
            store(last_batch)
            sp.wait_ge(stored, 16 * BATCH)

        @block.gpsimd
        def _(pool):
            g = nc.gpsimd
            g.memset(w_qk[:, :, :, :, :], 0.0).then_inc(zeroed, 1)
            g.memset(w_keys[:, :, :, :], 0.0).then_inc(zeroed, 1)
            n = [0]

            def made(ins):
                n[0] += 1
                ins.then_inc(const_pool, 1)
                pool.wait_ge(const_pool, n[0])

            for m in (ident, identb, flip, causal, sel):
                made(g.memset(m[:], 0.0))
            made(g.memset(ties[:, 0:6 * TP], -TIE))
            made(g.memset(ties[:, 6 * TP:], 0.0))
            made(g.memset(neg_lo[:, :], 0.0))
            made(g.memset(neg_lo[32:64, :], -1.0))
            made(g.memset(neg_lo[96:128, :], -1.0))
            made(g.memset(half[:, :], -0.5))
            made(g.memset(shift[:, :], -SHIFT))
            made(g.memset(xnT[64:65, :], 1.0))
            made(g.memset(ext[:, 0:123], 0.0))
            for m in (ident, identb):
                made(g.affine_select(out=m[:, :], in_=m[:, :], compare_op=ALU.not_equal, fill=1.0, base=0,
                                     pattern=[[-1, 128]], channel_multiplier=1))
            made(g.affine_select(out=flip[:, :], in_=flip[:, :], compare_op=ALU.not_equal, fill=1.0, base=-126,
                                 pattern=[[1, 127]], channel_multiplier=1))
            made(g.affine_select(out=causal[:, :], in_=causal[:, :], compare_op=ALU.is_ge, fill=BIG, base=0,
                                 pattern=[[-1, TP]], channel_multiplier=1))
            tri = ties[:, 5 * TP:6 * TP]
            made(g.affine_select(out=tri, in_=tri, compare_op=ALU.is_gt, fill=0.0, base=0,
                                 pattern=[[-1, TP]], channel_multiplier=1))
            for r in (0, 32):
                v = sel[r:r + 32].rearrange("p t (a b) -> p t a b", a=4)
                made(g.affine_select(out=v, in_=v, compare_op=ALU.not_equal, fill=1.0, base=0,
                                     pattern=[[0, 8], [0, 4], [-1, 32]], channel_multiplier=1))
            for r in (64, 96):
                v = sel[r:r + 32].rearrange("p t (a b) -> p t a b", a=4)
                made(g.affine_select(out=v, in_=v, compare_op=ALU.not_equal, fill=1.0, base=0,
                                     pattern=[[-1, 8], [-8, 4], [0, 32]], channel_multiplier=1))
            made(g.iota(ranks_row[:, :], [[1, PICKED]], base=0, channel_multiplier=0, allow_small_or_imprecise_dtypes=True))

            def rstd(b, i):
                after(pool, "front", "V", "veps", i, b=b)
                g.tensor_tensor(stat[:, 4, :], stat[:, 3, :], half[:, :], ALU.pow).then_inc(done["front", "G"], 1)

            def shift_scores(b, gr, it):
                after(pool, "front", "V", "off0", gr, b=b)
                v = sims[:, gr, it].rearrange("p h q k -> p (h q) k")
                o = off[:, 4 * it:4 * it + 4, :].rearrange("p h q -> p (h q)").unsqueeze(2).broadcast_to([TP, 8, KEYS])
                g.tensor_tensor(v, v, o, ALU.add).then_inc(done["front", "G"], 1)

            def clamp(b, gr, it):
                after_alone(pool, "front", "G", "shift", gr, it, b=b)
                v = sims[:, gr, it].rearrange("p h q k -> p (h q k)")
                g.tensor_scalar(v, v, -60000.0, None, ALU.max).then_inc(done["front", "G"], 1)

            def combo(b, n):
                h, c = n // COMBOS, n % COMBOS
                gk, ah = c // 2, c % 2
                after(pool, "front", "G", "clamp", h // 4, NT - 1, b=b)
                wait_alone(pool, combo_done["T"], b * HEADS * COMBOS + n - 1)
                cols = sims[:, h // 4, :, h % 4].rearrange("p t q (g k) -> p t (q g) k", g=2)
                cols = cols[:, :, gk:2 + ah + 1:2 + ah - gk, :].unsqueeze(3).broadcast_to([TP, NT, 2, 2, 32])
                g.tensor_copy(quarter[:, n % 2].rearrange("p t (q d k) -> p t q d k", q=2, d=2), cols).then_inc(combo_done["G"], 1)

            def keep_xn2(b):
                after(pool, "front", "A", "xnt", 2, b=b)
                after(pool, "front", "T", "qpk", 1, 1, b=b - 1)
                after_alone(pool, "back", "T", "q2", 3, b=b - 1)
                g.tensor_copy(xn2k[:, :], xn2[:, :]).then_inc(done["front", "G"], 1)

            def keep_h2(b):
                after(pool, "front", "V", "h2", b=b)
                wait_alone(pool, stored, b * 16)
                g.tensor_copy(result[:, :, :], h2[:, :, :]).then_inc(done["back", "G"], 1)

            run(pool, "G", {("front", "rstd"): rstd, ("front", "shift"): shift_scores, ("front", "clamp"): clamp,
                            ("combo", "combo"): combo, ("front", "keep_xn2"): keep_xn2, ("back", "keep_h2"): keep_h2},
                lambda b, u: None, lambda b: None)

        @block.tensor
        def _(pe):
            mm, tr = nc.tensor.matmul, nc.tensor.transpose
            fT, bT = done["front", "T"], done["back", "T"]

            pe.wait_ge(weights_loaded, N_WEIGHTS)
            pe.wait_ge(const_pool, CONSTS)
            mm(fa[0:HEADS, 0:127], rel_tab[:, :], flip[:, :], start=True, stop=True).then_inc(const_pe, 1)
            for q in range(2):
                for gr in range(2):
                    last = tr(fb[:, (q * 2 + gr) * 64:(q * 2 + gr) * 64 + 64], attn[0:64, q * 256 + gr * 128:q * 256 + gr * 128 + 128], ident[0:64, 0:64])
            last.then_inc(const_pe, 1)
            pe.wait_ge(const_dve, 2)
            pe.wait_ge(const_act, 1)
            pe.wait_ge(hankel_loaded, 16 * HEADS)

            def rowbc(b):
                after(pe, "front", "V", "score", b=b)
                after(pe, "front", "A", "sim", 1, 2, b=b - 1)
                for t in range(XT):
                    last = tr(fa2[t // 3][0:TP, t % 3 * TP:t % 3 * TP + TP], score[:, t:t + 1].broadcast_to([TP, TP]), ident[0:TP, 0:TP])
                last.then_inc(fT, 1)

            def pick(b):
                after(pe, "front", "V", "hot", XT - 1, b=b)
                for it in range(NT):
                    for t in range(XT):
                        last = mm(fa[0:TP, it * DIM:it * DIM + DIM], hot[:, t, it * TP:it * TP + TP], xg[:, t, :], start=(t == 0), stop=(t == XT - 1))
                last.then_inc(fT, 1)

            def xnt(b, i):
                after_alone(pe, "front", "V", "xn", i, b=b)
                for it in range(NT):
                    last = tr(fb[0:64, it * TP:it * TP + TP], xn[:, it, :], ident[0:TP, 0:TP])
                last.then_inc(fT, 1)

            def v(b):
                after(pe, "front", "A", "xnt", 1, b=b)
                for it in range(NT):
                    last = mm(fa[0:TP, it * DIM:it * DIM + DIM], xnT[:, it * TP:it * TP + TP], w_v[:, :], start=True, stop=True)
                last.then_inc(fT, 1)

            def qk_proj(which, bank):
                def f(b, gr):
                    if which == 0:
                        if gr == 0:
                            after(pe, "front", "A", "v", b=b)
                        else:
                            after(pe, "front", "V", "o1", 0, b=b)
                    elif gr == 1:
                        after(pe, "front", "A", "ptc", 0, 11, b=b)
                    mm(bank[:, 0:PICKED], w_qk[:, which, gr].rearrange("p h d -> p (h d)"), xnT[:, :], start=True, stop=True).then_inc(fT, 1)
                return f

            def pv(gr, n):
                hh, it = n // NT, n % NT
                o = fa[0:TP, 384 + it * 32 + hh * DH:384 + it * 32 + hh * DH + DH]
                col = (gr * 4 + hh) * DH
                for jt in range(NT):
                    last = mm(o, probT[:, n % 2, jt * TP:jt * TP + TP], vtok[:, jt, col:col + DH], start=(jt == 0), stop=(jt == NT - 1))
                return last

            def qk(b, gr, n):
                hh, it = n // NT, n % NT
                if n == 0:
                    after(pe, "front", "A", "k", gr, b=b)
                else:
                    after(pe, "front", "A", "p", gr, n - 1, b=b)
                if n >= 2:
                    after(pe, "front", "A" if n % 2 else "V", "ptc", gr, n - 2, b=b)
                    pv(gr, n - 2)
                k0 = 32 * hh
                last = mm(fa[0:TP, 0:PICKED], qT[k0:k0 + DH, it * TP:it * TP + TP], kT[k0:k0 + DH, :], start=True, stop=True)
                if it == 0:
                    last = mm(fa[0:TP, 249:375], flip[0:TP, 2:127], hankel[:, gr * 4 + hh, :], start=False, stop=True, skip_group_check=True)
                elif it == 1:
                    last = mm(fa[0:TP, 374:375], flip[0:TP, 2:127], hankel[:, gr * 4 + hh, 0:1], start=False, stop=True, skip_group_check=True)
                last.then_inc(fT, 1)

            def pt(b, gr, n):
                after(pe, "front", "A", "p", gr, n, b=b)
                if n == 0:
                    after(pe, "front", "A", "k", gr, b=b)
                else:
                    after(pe, "front", "V" if n % 2 else "A", "ptc", gr, n - 1, b=b)
                for jt in range(NT):
                    last = tr(fb[0:TP, jt * TP:jt * TP + TP], prob[:, n % 2, jt * TP:jt * TP + TP], ident[0:TP, 0:TP])
                last.then_inc(fT, 1)

            def pv_end(b, gr):
                after(pe, "front", "V", "ptc", gr, 10, b=b)
                after(pe, "front", "A", "ptc", gr, 11, b=b)
                pv(gr, 10)
                pv(gr, 11).then_inc(fT, 1)

            def o1t(b):
                after_alone(pe, "front", "V", "o1", 1, b=b)
                for it in range(NT):
                    last = tr(fb[0:64, it * TP:it * TP + TP], o1[:, it, :], ident[0:TP, 0:TP])
                last.then_inc(fT, 1)

            def proj(b):
                after(pe, "front", "A", "o1t", b=b)
                for it in range(NT):
                    last = mm(fa[0:TP, it * DIM:it * DIM + DIM], xnT[:, it * TP:it * TP + TP], w_proj[:, :], start=True, stop=True)
                last.then_inc(fT, 1)

            def qpk(b, gr, p):
                if gr == 0:
                    after(pe, "front", "A", "xnt", 2, b=b)
                else:
                    after(pe, "front", "G", "keep_xn2", b=b)
                    if p == 0:
                        after(pe, "front", "A", "sim", 0, 2, b=b)
                src = (xn2, xn2k)[gr]
                col = p * 256 + gr * 128
                mm(fa2[p][:, 0:PICKED], w_pk[:, col:col + 128], src[:, :], start=True, stop=True).then_inc(fT, 1)

            def sim(b, gr, it):
                after(pe, "front", "A", "qpk", gr, 1, b=b)
                if it == 2:
                    after(pe, "front", "A", "sim", gr, 0, b=b)
                bank = fa2[it % 2]
                for q in range(2):
                    p = 1 - q
                    last = mm(bank[0:TP, q * 256:q * 256 + 256], qpkT[:, p, it * TP:it * TP + TP],
                              w_keys[:, p * 2 + gr].rearrange("p h k -> p (h k)"), start=True, stop=True)
                last.then_inc(fT, 1)

            def combo(b, n):
                wait(pe, combo_done["G"], b * HEADS * COMBOS + n + 1)
                wait(pe, combo_done["V"], b * HEADS * COMBOS + n)
                for it in range(NT):
                    last = tr(combo_bank[:, it * TP:it * TP + TP], quarter[:, n % 2, it, :], ident[0:TP, 0:TP])
                last.then_inc(combo_done["T"], 1)

            def out_mm(b, u):
                h, tile = u // PER_HEAD, u % PER_HEAD
                c, a8 = tile // 8, tile % 8
                if tile == 0:
                    wait(pe, kv_copied, b * HEADS + h)
                    if h == 3:
                        if isinstance(b, int) and b == 0:
                            pe.wait_ge(table_loaded[3], N_TABLE)
                        else:
                            pe.wait_ge(swap_loaded, b * 2 * N_TABLE)
                    elif h == 7:
                        pe.wait_ge(swap_loaded, b * 2 * N_TABLE + N_TABLE)
                    elif isinstance(b, int) and b == 0:
                        pe.wait_ge(table_loaded[h], N_TABLE)
                pe.wait_ge(pair_weights, b * SLOTS + u + 1)
                t = table[:, table_slot(h), c, a8, :]
                mm(kv_bank[:, 0:PICKED], t, weight[:, u % 4, :], start=(tile == 0), stop=(tile == PER_HEAD - 1)).then_inc(pair_sums, 1)

            def dense(b, u):
                n = u // 8
                if u % 8 == 0:
                    pe.wait_ge(combo_done["V"], b * HEADS * COMBOS + n + 1)
                if u < 3:
                    wait(pe, pair_weights, b * SLOTS)
                mm(s_bank[u % 3][:, 0:PICKED], sel[:, u % 8, :], halves[:, n % 2, :], start=True, stop=True).then_inc(pair_scores, 1)
                if u >= 2:
                    out_mm(b, u - 2)

            def flush(b):
                out_mm(b, SLOTS - 2)
                out_mm(b, SLOTS - 1)

            def kvt(b, h):
                wait(pe, kv_copied, b * HEADS + h + 1)
                if h % 2 == 0 and h > 0:
                    after(pe, "back", "V", "acc", h // 2 - 1, b=b)
                elif h == 0:
                    after(pe, "back", "V", "acc", 3, b=b - 1)
                else:
                    after(pe, "back", "V", "o2", h - 1, b=b)
                for it in range(NT):
                    last = tr(back_bank[0:TP, it * 128:it * 128 + 128], kvT[:, it * TP:it * TP + TP], ident[:, :])
                last.then_inc(bT, 1)

            def knt(b, h):
                after(pe, "back", "V", "kvn", h, b=b)
                for it in range(NT):
                    last = tr(back_bank[:, it * TP:it * TP + TP], kv[:, it, :], ident[0:TP, 0:TP])
                last.then_inc(bT, 1)

            def q2(b, j):
                after(pe, "back", "A", "knt", 2 * j, b=b)
                after(pe, "front", "G", "keep_xn2", b=b)
                mm(back_bank[:, 0:PICKED], w_q2[:, j * 128:j * 128 + 128], xn2k[:, :], start=True, stop=True).then_inc(bT, 1)

            def qk2(b, h, r):
                if r == 0:
                    if h % 2 == 0:
                        after(pe, "back", "A", "q2", h // 2, b=b)
                    else:
                        after(pe, "back", "A", "knt", h, b=b)
                else:
                    after(pe, "back", "V", "ptc2", h, 0, b=b)
                rows = slice(64 * (h % 2), 64 * (h % 2) + 64)
                for it, at in (((0, 0), (1, TP)) if r == 0 else ((2, 0),)):
                    n = TP * (it + 1)
                    mm(back_bank[0:TP, at:at + n], q2T[rows, it * TP:it * TP + TP], knT[rows, 0:n], start=True, stop=True)
                    last = mm(back_bank[0:TP, at + n - TP:at + n], identb[0:TP, 0:TP], causal[:, :], start=False, stop=True, skip_group_check=True)
                last.then_inc(bT, 1)

            def pt2(b, h, r):
                after(pe, "back", "A", "p2", h, r, b=b)
                for jt in range(NT):
                    last = tr(back_bank[0:TP, jt * TP:jt * TP + TP], prob2[:, r, jt * TP:jt * TP + TP], ident[0:TP, 0:TP])
                last.then_inc(bT, 1)

            def pv2(b, h):
                after(pe, "back", "A", "ptc2", h, 1, b=b)
                v0 = DIM * (1 - h % 2)
                for it in range(NT):
                    for jt in range(it + 1):
                        p = prob2T[:, 1, jt, :] if it == 2 else prob2T[:, 0, it + jt, :]
                        last = mm(back_bank[0:TP, it * DIM:it * DIM + DIM], p, kv[:, jt, v0:v0 + DIM], start=(jt == 0), stop=(jt == it))
                last.then_inc(bT, 1)

            def o2t(b, j):
                after(pe, "back", "V", "o2", 2 * j + 1, b=b)
                for it in range(NT):
                    last = tr(back_bank[:, it * TP:it * TP + TP], o2[:, it, :], ident[0:TP, 0:TP])
                last.then_inc(bT, 1)

            def wo_mm(b, j):
                after(pe, "back", "A", "o2t", j, b=b)
                for it in range(NT):
                    last = mm(back_bank[0:TP, it * DIM:it * DIM + DIM], o2T[:, it * TP:it * TP + TP], w_o[:, j, :], start=True, stop=True)
                last.then_inc(bT, 1)

            run(pe, "T", {("front", "rowbc"): rowbc, ("front", "pick"): pick, ("front", "xnt"): xnt, ("front", "v"): v,
                          ("front", "q"): qk_proj(0, fa), ("front", "k"): qk_proj(1, fb), ("front", "qk"): qk, ("front", "pt"): pt,
                          ("front", "pv_end"): pv_end, ("front", "o1t"): o1t, ("front", "proj"): proj, ("front", "qpk"): qpk,
                          ("front", "sim"): sim, ("combo", "combo"): combo, ("back", "kvt"): kvt, ("back", "knt"): knt,
                          ("back", "q2"): q2, ("back", "qk2"): qk2, ("back", "pt2"): pt2, ("back", "pv2"): pv2,
                          ("back", "o2t"): o2t, ("back", "wo"): wo_mm}, dense, flush)

        @block.scalar
        def _(act):
            fA, bA = done["front", "A"], done["back", "A"]

            def copy(out, in_, s, scale=1.0):
                nc.scalar.activation(out, in_, ACT.Copy, scale=scale).then_inc(s, 1)

            act.wait_ge(const_pe, 2)
            act.wait_ge(zeroed, 2)
            for q in range(2):
                for gr in range(2):
                    for hh in range(4):
                        at = (q * 2 + gr) * 64
                        last = nc.scalar.activation(w_keys[32 * hh:32 * hh + 32, q * 2 + gr, hh, :], fb[32 * hh:32 * hh + 32, at:at + 64], ACT.Copy)
            last.then_inc(const_act, 1)
            act.wait_ge(const_pool, CONSTS)

            def eneg(b):
                after(act, "front", "V", "score", b=b)
                after(act, "front", "V", "den", b=b - 1)
                nc.scalar.activation(eneg_, score, ACT.Exp, scale=-1.0).then_inc(fA, 1)

            def h1_(b):
                after(act, "front", "T", "pick", b=b)
                after(act, "front", "V", "h2", b=b - 1)
                copy(h1[:, :, :], fa[0:TP, 0:NT * DIM].rearrange("p (t f) -> p t f", t=NT), fA)

            def xnt(b, i):
                after(act, "front", "T", "xnt", i, b=b)
                if i == 1:
                    after(act, "front", "T", "proj", b=b - 1)
                else:
                    after(act, "front", "T", "qpk", 0, 1, b=b - 1)
                    after(act, "front", "G", "keep_xn2", b=b - 1)
                copy((xnT[0:64, :], xn2[:, :])[i - 1], fb[0:64, 0:PICKED], fA)

            def v(b):
                after(act, "front", "T", "v", b=b)
                after(act, "front", "T", "pv_end", 1, b=b - 1)
                copy(vtok[:, :, :], fa[0:TP, 0:NT * DIM].rearrange("p (t f) -> p t f", t=NT), fA)

            def q(b, gr):
                after(act, "front", "T", "q", gr, b=b)
                copy(qT, fa[:, 0:PICKED], fA, scale=-DH ** -0.5)

            def k(b, gr):
                after(act, "front", "T", "k", gr, b=b)
                copy(kT, fb[:, 0:PICKED], fA)

            def p(b, gr, n):
                after(act, "front", "V", "low", gr, n, b=b)
                if n >= 2:
                    after(act, "front", "T", "pt", gr, n - 2, b=b)
                hh, it = n // NT, n % NT
                z = zsum[:, gr * 12 + it * 4 + hh:gr * 12 + it * 4 + hh + 1]
                nc.scalar.activation(prob[:, n % 2, :], fa[0:TP, 0:PICKED], ACT.Exp, bias=low[:, n % 2:n % 2 + 1], scale=-1.0, accum_out=z).then_inc(fA, 1)

            def ptc(b, gr, n):
                after(act, "front", "T", "pt", gr, n, b=b)
                if n >= 2:
                    after(act, "front", "T", "qk", gr, n, b=b)
                copy(probT[:, n % 2, :], fb[0:TP, 0:PICKED], fA)

            def o1t(b):
                after(act, "front", "T", "o1t", b=b)
                copy(xnT[0:64, :], fb[0:64, 0:PICKED], fA)

            def qpk(b, gr, p):
                after(act, "front", "T", "qpk", gr, p, b=b)
                copy(qpkT[:, p, :], fa2[p][:, 0:PICKED], fA)

            def sim(b, gr, it):
                after(act, "front", "T", "sim", gr, it, b=b)
                if it == 0:
                    wait(act, combo_done["G"], (b - 1) * HEADS * COMBOS + 16 * (gr + 1))
                copy(sims[:, gr, it].rearrange("p h q k -> p q h k"), fa2[it % 2][0:TP, :].rearrange("p (q h k) -> p q h k", q=2, h=4), fA)

            def wexp(b, gr):
                after(act, "front", "V", "diff", gr, b=b)
                nc.scalar.activation(wke[:, :, :], wk[:, :, :], ACT.Exp, bias=shift[0:TP, :]).then_inc(fA, 1)

            def combo(b, n):
                wait(act, combo_done["T"], b * HEADS * COMBOS + n + 1)
                copy(hi[:, :], combo_bank[:, 0:PICKED], combo_done["A"])

            def dense(b, u):
                if u % PER_HEAD == 2 and u > 2:
                    kv_copy(b, u // PER_HEAD - 1)
                act.wait_ge(pair_scores, b * SLOTS + u + 1)
                nc.scalar.activation(weight[:, u % 4, :], s_bank[u % 3][:, 0:PICKED], ACT.Exp, bias=shift[:, :]).then_inc(pair_exps, 1)

            def kv_copy(b, h):
                act.wait_ge(pair_sums, b * SLOTS + (h + 1) * PER_HEAD)
                if h == 0:
                    after(act, "back", "T", "kvt", HEADS - 1, b=b - 1)
                else:
                    after(act, "back", "T", "kvt", h - 1, b=b)
                copy(kvT[:, :], kv_bank[:, 0:PICKED], kv_copied)

            def flush(b):
                kv_copy(b, HEADS - 1)

            def knt(b, h):
                after(act, "back", "T", "knt", h, b=b)
                r = slice(64 * (h % 2), 64 * (h % 2) + 64)
                copy(knT[r, :], back_bank[r, 0:PICKED], bA)

            def q2(b, j):
                after(act, "back", "T", "q2", j, b=b)
                copy(q2T[:, :], back_bank[:, 0:PICKED], bA, scale=-DIM ** -0.5)

            def p2(b, h, r):
                after(act, "back", "V", "low2", h, r, b=b)
                for it, at, n in (((0, 0, TP), (1, TP, 2 * TP)) if r == 0 else ((2, 0, 3 * TP),)):
                    last = nc.scalar.activation(prob2[:, r, at:at + n], back_bank[0:TP, at:at + n], ACT.Exp, bias=low2[:, it:it + 1], scale=-1.0,
                                                accum_out=z2[:, it:it + 1])
                last.then_inc(bA, 1)

            def ptc2(b, h, r):
                after(act, "back", "T", "pt2", h, r, b=b)
                copy(prob2T[:, r].rearrange("p j i -> p (j i)"), back_bank[0:TP, 0:PICKED], bA)

            def o2t(b, j):
                after(act, "back", "T", "o2t", j, b=b)
                copy(o2T[:, :], back_bank[:, 0:PICKED], bA)

            eneg_ = small[:, 6:12]
            run(act, "A", {("front", "eneg"): eneg, ("front", "h1"): h1_, ("front", "xnt"): xnt, ("front", "v"): v, ("front", "q"): q,
                           ("front", "k"): k, ("front", "p"): p, ("front", "ptc"): ptc, ("front", "o1t"): o1t, ("front", "qpk"): qpk,
                           ("front", "sim"): sim, ("front", "wexp"): wexp, ("combo", "combo"): combo, ("back", "knt"): knt,
                           ("back", "q2"): q2, ("back", "p2"): p2, ("back", "ptc2"): ptc2, ("back", "o2t"): o2t}, dense, flush)

        @block.vector
        def _(dve):
            V = nc.vector
            fV, bV = done["front", "V"], done["back", "V"]

            dve.wait_ge(const_pe, 1)
            dve.wait_ge(const_pool, CONSTS)
            ext0 = small[0:HEADS, 40:41]
            V.tensor_copy(ext0, fa[0:HEADS, 0:1]).then_inc(const_dve0, 1)
            dve.wait_ge(const_dve0, 1)
            V.tensor_scalar(ext[:, 123:250], fa[0:HEADS, 0:127], ext0, -1.0, ALU.subtract, ALU.mult).then_inc(const_dve, 2)

            def score_mul(b):
                if isinstance(b, int) and b == 0:
                    dve.wait_ge(weights_loaded, N_WEIGHTS)
                dve.wait_ge(x_loaded, b * 16 + 16)
                V.tensor_tensor(xw[:, :, :], xin[:, :, :], w_score[:, :].unsqueeze(1).broadcast_to([TP, XT, DIM]), ALU.mult).then_inc(fV, 1)

            def score_(b):
                after(dve, "front", "V", "score_mul", b=b)
                after(dve, "front", "T", "rowbc", b=b - 1)
                V.tensor_reduce(score, xw[:, :, :], AX.X, ALU.add).then_inc(fV, 1)

            def den_(b):
                after(dve, "front", "A", "eneg", b=b)
                V.tensor_scalar(den, eneg, 1.0, None, ALU.add).then_inc(fV, 1)

            def gate_(b):
                after(dve, "front", "V", "den", b=b)
                V.reciprocal(gate, den).then_inc(fV, 1)

            def xg_(b):
                after(dve, "front", "V", "gate", b=b)
                after(dve, "front", "T", "pick", b=b - 1)
                V.tensor_tensor(xg[:, :, :], xin[:, :, :], gate.unsqueeze(2).broadcast_to([TP, XT, DIM]), ALU.mult).then_inc(fV, 1)

            def rank_(b, t):
                if t == 0:
                    after(dve, "front", "T", "rowbc", b=b)
                else:
                    after(dve, "front", "V", "rank", t - 1, b=b)
                for half_ in range(2):
                    last = V.scalar_tensor_tensor(out=junk[:, half_ * 375:half_ * 375 + 375], in0=fa2[half_][0:TP, 0:375], scalar=score[:, t:t + 1],
                                           in1=ties[:, (5 - t) * TP + half_ * 375:(5 - t) * TP + half_ * 375 + 375],
                                           op0=ALU.subtract, op1=ALU.is_gt, accum_out=rank2[:, half_ * 6 + t:half_ * 6 + t + 1])
                last.then_inc(fV, 1)

            rank2 = small[:, 42:54]

            def hot_(b, t):
                after(dve, "front", "V", "ranks", b=b)
                if t == 0:
                    after(dve, "front", "T", "pv_end", 1, b=b - 1)
                V.tensor_scalar(hot[:, t, :], ranks_row[:, :], rank[:, t:t + 1], None, ALU.is_equal).then_inc(fV, 1)

            def ranks(b):
                after(dve, "front", "V", "rank", XT - 1, b=b)
                V.tensor_tensor(rank, rank2[:, 0:6], rank2[:, 6:12], ALU.add).then_inc(fV, 1)

            def rows(i):
                return (h1, h2)[i - 1]

            def sum_(b, i):
                if i == 1:
                    after(dve, "front", "A", "h1", b=b)
                else:
                    after(dve, "front", "V", "h2", b=b)
                V.tensor_reduce(stat[:, 0, :], rows(i)[:, :, :], AX.X, ALU.add).then_inc(fV, 1)

            def mean(b, i):
                after(dve, "front", "V", "sum", i, b=b)
                V.tensor_scalar(stat[:, 1, :], stat[:, 0, :], 1.0 / DIM, None, ALU.mult).then_inc(fV, 1)

            def wide(ap):
                return ap.unsqueeze(2).broadcast_to([TP, NT, DIM])

            def cen_(b, i):
                after(dve, "front", "V", "mean", i, b=b)
                V.tensor_tensor(cen[:, :, :], rows(i)[:, :, :], wide(stat[:, 1, :]), ALU.subtract).then_inc(fV, 1)

            def sq_(b, i):
                after(dve, "front", "V", "cen", i, b=b)
                V.tensor_tensor(sq[:, :, :], cen[:, :, :], cen[:, :, :], ALU.mult).then_inc(fV, 1)

            def var(b, i):
                after(dve, "front", "V", "sq", i, b=b)
                V.tensor_reduce(stat[:, 2, :], sq[:, :, :], AX.X, ALU.add).then_inc(fV, 1)

            def veps(b, i):
                after(dve, "front", "V", "var", i, b=b)
                V.tensor_scalar(stat[:, 3, :], stat[:, 2, :], 1.0 / DIM, 1e-5, ALU.mult, ALU.add).then_inc(fV, 1)

            def xn_(b, i):
                after(dve, "front", "G", "rstd", i, b=b)
                after(dve, "front", "T", "xnt", 3 - i, b=b - (i == 1))
                V.tensor_tensor(xn[:, :, :], cen[:, :, :], wide(stat[:, 4, :]), ALU.mult).then_inc(fV, 1)

            def low_(b, gr, n):
                after(dve, "front", "T", "qk", gr, n, b=b)
                V.tensor_reduce(low[:, n % 2:n % 2 + 1], fa[0:TP, 0:PICKED], AX.X, ALU.min).then_inc(fV, 1)

            def ptc(b, gr, n):
                after(dve, "front", "T", "pt", gr, n, b=b)
                if n >= 2:
                    after(dve, "front", "T", "qk", gr, n, b=b)
                V.tensor_copy(probT[:, n % 2, :], fb[0:TP, 0:PICKED]).then_inc(fV, 1)

            def rz_(b, gr):
                after(dve, "front", "A", "p", gr, 11, b=b)
                V.reciprocal(rz[:, gr * 12:gr * 12 + 12], zsum[:, gr * 12:gr * 12 + 12]).then_inc(fV, 1)

            def o1_(b, gr):
                after(dve, "front", "T", "pv_end", gr, b=b)
                after(dve, "front", "V", "rz", gr, b=b)
                after(dve, "front", "T", "o1t", b=b - 1)
                V.tensor_tensor(o1[:, :, gr * 32:gr * 32 + 32].rearrange("p t (h d) -> p t h d", h=4),
                                fa[0:TP, 384:480].rearrange("p (t h d) -> p t h d", t=NT, h=4),
                                rz[:, gr * 12:gr * 12 + 12].rearrange("p (t h) -> p t h", t=NT).unsqueeze(3).broadcast_to([TP, NT, 4, DH]),
                                ALU.mult).then_inc(fV, 1)

            def h2_(b):
                after(dve, "front", "T", "proj", b=b)
                after(dve, "back", "G", "keep_h2", b=b - 1)
                V.tensor_tensor(h2[:, :, :], h1[:, :, :], fa[0:TP, 0:NT * DIM].rearrange("p (t f) -> p t f", t=NT), ALU.add).then_inc(fV, 1)

            def group(gr, it, q):
                return sims[:, gr, it].rearrange("p h q k -> p (h q) k")[:, q, :]

            def max_a(b, gr, it, q):
                if q == 0:
                    after_alone(dve, "front", "A", "sim", gr, it, b=b)
                V.max(top[:, it, q, 0:8], group(gr, it, q)).then_inc(fV, 1)

            def cut_a(b, gr, it, q):
                if q == 0:
                    after_alone(dve, "front", "V", "max_a", gr, it, 7, b=b)
                V.match_replace(left[:, q, :], top[:, it, q, 0:8], group(gr, it, q), -3e38).then_inc(fV, 1)

            def max_b(b, gr, it, q):
                if q == 0:
                    after_alone(dve, "front", "V", "cut_a", gr, it, 7, b=b)
                V.max(top[:, it, q, 8:16], left[:, q, :]).then_inc(fV, 1)

            def cut_b(b, gr, it, q):
                if q == 0:
                    after_alone(dve, "front", "V", "max_b", gr, it, 7, b=b)
                V.match_replace(left[:, q, :], top[:, it, q, 8:16], left[:, q, :], -3e38).then_inc(fV, 1)

            def max_c(b, gr, it):
                after(dve, "front", "V", "cut_b", gr, it, 7, b=b)
                V.tensor_reduce(top[:, it, :, 16:17].rearrange("p q o -> p (q o)"), left[:, :, :], AX.X, ALU.max).then_inc(fV, 1)

            CAND_ROWS = [(0, 1, 17), (1, 1, 8), (2, 1, 5), (3, 1, 4), (4, 1, 3), (5, 3, 2), (8, 9, 1)]

            def cand_(b, gr, it, r):
                if r == 0:
                    after(dve, "front", "V", "max_c", gr, it, b=b)
                i0, ni, nj = CAND_ROWS[r]
                at = sum(a * c for _, a, c in CAND_ROWS[:r])
                t4 = top[:, it].rearrange("p (h q) k -> p h q k", q=2)
                o = cand[:, :, at:at + ni * nj].rearrange("p h (i j) -> p h i j", i=ni)
                V.tensor_tensor(o, t4[:, :, 1, i0:i0 + ni].unsqueeze(3).broadcast_to([TP, 4, ni, nj]),
                                t4[:, :, 0, 0:nj].unsqueeze(2).broadcast_to([TP, 4, ni, nj]), ALU.add).then_inc(fV, 1)

            def cmax_a(b, gr, it, q):
                if q == 0:
                    after_alone(dve, "front", "V", "cand", gr, it, 6, b=b)
                V.max(best[:, it, q, 0:8], cand[:, q, :]).then_inc(fV, 1)

            def ccut_a(b, gr, it, q):
                if q == 0:
                    after_alone(dve, "front", "V", "cmax_a", gr, it, 3, b=b)
                V.match_replace(cand[:, q, :], best[:, it, q, 0:8], cand[:, q, :], -3e38).then_inc(fV, 1)

            def cmax_b(b, gr, it, q):
                if q == 0:
                    after_alone(dve, "front", "V", "ccut_a", gr, it, 3, b=b)
                V.max(best[:, it, q, 8:16], cand[:, q, :]).then_inc(fV, 1)

            def ccut_b(b, gr, it, q):
                if q == 0:
                    after_alone(dve, "front", "V", "cmax_b", gr, it, 3, b=b)
                V.match_replace(cand[:, q, :], best[:, it, q, 8:16], cand[:, q, :], -3e38).then_inc(fV, 1)

            def cmax_c(b, gr, it):
                after(dve, "front", "V", "ccut_b", gr, it, 3, b=b)
                V.tensor_reduce(best[:, it, :, 16:17].rearrange("p h o -> p (h o)"), cand[:, :, :], AX.X, ALU.max).then_inc(fV, 1)

            best2 = best[:, :, :, :].rearrange("p t h k -> p (t h) k")
            top2 = top[:, :, :, :].rearrange("p t (h q) k -> p (t h) q k", q=2)

            def mid(b, gr):
                after(dve, "front", "V", "cmax_c", gr, NT - 1, b=b)
                V.tensor_tensor(cut[:, 0, :], best2[:, :, 15], best2[:, :, 16], ALU.add).then_inc(fV, 1)

            def floor(b, gr):
                V.tensor_scalar(cut[:, 1, :], best2[:, :, 0], -SPAN, None, ALU.add).then_inc(fV, 1)

            def thr(b, gr):
                after(dve, "front", "V", "floor", gr, b=b)
                V.scalar_tensor_tensor(out=cut[:, 2, :], in0=cut[:, 0, :], scalar=0.5, in1=cut[:, 1, :], op0=ALU.mult, op1=ALU.max).then_inc(fV, 1)

            def diff(b, gr):
                after(dve, "front", "V", "thr", gr, b=b)
                V.tensor_tensor(wk[:, :, :], best2[:, :, 0:16], cut[:, 2, :].unsqueeze(2).broadcast_to([TP, NT * 4, TOPK]), ALU.subtract).then_inc(fV, 1)

            def zk_(b, gr):
                after(dve, "front", "A", "wexp", gr, b=b)
                V.tensor_reduce(zk[:, :], wke[:, :, :], AX.X, ALU.add).then_inc(fV, 1)

            def rzk_(b, gr):
                after(dve, "front", "V", "zk", gr, b=b)
                after(dve, "back", "V", "kvn", 4 * gr + 3, b=b - 1)
                V.reciprocal(rzk[:, gr, :], zk[:, :]).then_inc(fV, 1)

            def off1(b, gr):
                after(dve, "front", "G", "shift", 1 - gr, NT - 1, b=b - (gr == 0))
                V.tensor_scalar(off[:, :, 0], top2[:, :, 0, 0], -1.0, None, ALU.mult).then_inc(fV, 1)

            def off0(b, gr):
                V.tensor_tensor(off[:, :, 1], top2[:, :, 0, 0], cut[:, 2, :], ALU.subtract).then_inc(fV, 1)

            def combo(b, n):
                wait(dve, combo_done["A"], b * HEADS * COMBOS + n + 1)
                wait(dve, pair_scores, b * SLOTS + 8 * (n - 1))
                V.scalar_tensor_tensor(out=halves[:, n % 2, :], in0=hi[:, :], scalar=neg_lo[:, 0:1], in1=combo_bank[:, 0:PICKED],
                                       op0=ALU.mult, op1=ALU.add).then_inc(combo_done["V"], 1)

            def dense(b, u):
                dve.wait_ge(pair_exps, b * SLOTS + u + 1)
                V.scalar_tensor_tensor(out=weight[:, u % 4, :], in0=s_bank[u % 3][:, 0:PICKED], scalar=0.0, in1=weight[:, u % 4, :],
                                       op0=ALU.is_ge, op1=ALU.mult).then_inc(pair_weights, 1)

            def kvn(b, h):
                after(dve, "back", "T", "kvt", h, b=b)
                after(dve, "front", "V", "rzk", h // 4, b=b)
                if h > 0:
                    after(dve, "back", "T", "pv2", h - 1, b=b)
                else:
                    after(dve, "back", "T", "pv2", HEADS - 1, b=b - 1)
                r = rzk[:, h // 4, :].rearrange("p (t h) -> p t h", t=NT)[:, :, h % 4].unsqueeze(2).broadcast_to([TP, NT, 128])
                V.tensor_tensor(kv[:, :, :], back_bank[0:TP, 0:NT * 128].rearrange("p (t c) -> p t c", t=NT), r, ALU.mult).then_inc(bV, 1)

            def low2_(b, h, r):
                after(dve, "back", "T", "qk2", h, r, b=b)
                if r == 0:
                    V.tensor_reduce(low2[:, 0:1], back_bank[0:TP, 0:TP], AX.X, ALU.min)
                    V.tensor_reduce(low2[:, 1:2], back_bank[0:TP, TP:3 * TP], AX.X, ALU.min).then_inc(bV, 1)
                else:
                    V.tensor_reduce(low2[:, 2:3], back_bank[0:TP, 0:3 * TP], AX.X, ALU.min).then_inc(bV, 1)

            def ptc2(b, h, r):
                after(dve, "back", "T", "pt2", h, r, b=b)
                V.tensor_copy(prob2T[:, r].rearrange("p j i -> p (j i)"), back_bank[0:TP, 0:PICKED]).then_inc(bV, 1)

            def rz2_(b, h):
                after(dve, "back", "A", "p2", h, 1, b=b)
                V.reciprocal(rz2[:, :], z2[:, :]).then_inc(bV, 1)

            def o2_(b, h):
                after(dve, "back", "T", "pv2", h, b=b)
                after(dve, "back", "V", "rz2", h, b=b)
                V.tensor_tensor(o2[:, :, 64 * (h % 2):64 * (h % 2) + 64], back_bank[0:TP, 0:NT * DIM].rearrange("p (t f) -> p t f", t=NT),
                                wide(rz2[:, :]), ALU.mult).then_inc(bV, 1)

            def acc(b, j):
                after(dve, "back", "T", "wo", j, b=b)
                after(dve, "back", "G", "keep_h2", b=b)
                V.tensor_tensor(result[:, :, :], result[:, :, :], back_bank[0:TP, 0:NT * DIM].rearrange("p (t f) -> p t f", t=NT), ALU.add).then_inc(bV, 1)

            run(dve, "V", {("front", "score_mul"): score_mul, ("front", "score"): score_, ("front", "den"): den_, ("front", "gate"): gate_,
                           ("front", "xg"): xg_, ("front", "rank"): rank_, ("front", "ranks"): ranks, ("front", "hot"): hot_,
                           ("front", "sum"): sum_, ("front", "mean"): mean, ("front", "cen"): cen_, ("front", "sq"): sq_,
                           ("front", "var"): var, ("front", "veps"): veps, ("front", "xn"): xn_, ("front", "low"): low_,
                           ("front", "ptc"): ptc, ("front", "rz"): rz_, ("front", "o1"): o1_, ("front", "h2"): h2_,
                           ("front", "max_a"): max_a, ("front", "cut_a"): cut_a, ("front", "max_b"): max_b, ("front", "cut_b"): cut_b,
                           ("front", "max_c"): max_c, ("front", "cand"): cand_, ("front", "cmax_a"): cmax_a, ("front", "ccut_a"): ccut_a,
                           ("front", "cmax_b"): cmax_b, ("front", "ccut_b"): ccut_b, ("front", "cmax_c"): cmax_c, ("front", "mid"): mid,
                           ("front", "floor"): floor, ("front", "thr"): thr, ("front", "diff"): diff, ("front", "zk"): zk_,
                           ("front", "rzk"): rzk_, ("front", "off1"): off1, ("front", "off0"): off0, ("combo", "combo"): combo,
                           ("back", "kvn"): kvn, ("back", "low2"): low2_, ("back", "ptc2"): ptc2, ("back", "rz2"): rz2_,
                           ("back", "o2"): o2_, ("back", "acc"): acc}, dense, lambda b: None)


_INS = ['x', 'L0_tok_score_proj', 'L0_attn_qkv_w', 'L0_attn_qkv_b', 'L0_attn_proj_w', 'L0_attn_proj_b', 'L0_attn_rpb_table',
        'L0_ffn_Wq_pk', 'L0_ffn_pk_keys', 'L0_ffn_Wq', 'kv_table', 'L0_ffn_Wo']
_OUTS = [((16, 375, 64), 'float32')]


def kernel(**inputs):
    import numpy as _np
    import concourse.bacc as _bacc
    from concourse import mybir as _mybir
    from concourse.bass_utils import run_bass_kernel_spmd as _run

    nc = _bacc.Bacc("TRN2", target_bir_lowering=False, num_devices=1)
    laid = dict(inputs)
    k, v = (_np.asarray(inputs[n]).reshape(HEADS, -1, DIM) for n in ('L0_ffn_keys_table', 'L0_ffn_values_table'))
    laid['kv_table'] = _np.concatenate([_np.concatenate([(k, v)[h % 2][h], (v, k)[h % 2][h]], axis=1) for h in range(HEADS)])
    arrays, args = {}, []
    for name in _INS:
        a = _np.ascontiguousarray(laid[name])
        arrays[f"in_{name}_dram"] = a
        args.append(nc.dram_tensor(f"in_{name}_dram", a.shape, _mybir.dt.from_np(a.dtype), kind="ExternalInput").ap())
    for i, (shape, dtype) in enumerate(_OUTS):
        dt = _mybir.dt.from_np(_np.dtype(dtype))
        args.append(nc.dram_tensor(f"out_{i}_dram", shape, dt, kind="ExternalOutput").ap())
    build_kernel(nc, *args)
    r = _run(nc, [arrays], core_ids=[0])
    return r.results[0]["out_0_dram"]
```

```python
BATCH, TOKENS, PICKED, DIM, HEADS = 16, 750, 375, 64, 8
TP = 125
NT = PICKED // TP
XT = TOKENS // TP
DH = DIM // HEADS
LAST_REL = 126
KEYS, KEY_DIM, TOPK = 64, 32, 16
CAND = sum(17 // (i + 1) for i in range(17))
SLOTS = 256
PER_HEAD = SLOTS // HEADS
COMBOS = 4
TIE = 1e-37
SPAN = 100.0
SHIFT = SPAN / 2
SWAP_HEADS = (3, 7)
BIG = 1e30


def table_slot(h):
    return 3 if h in SWAP_HEADS else h


def select_steps():
    s = [("G", ("score_mul",), 1.), ("V", ("score",), .45), ("A", ("eneg",), .2), ("T", ("rowbc",), .4, ("score",)),
         ("V", ("den",), .1, ("eneg",)), ("V", ("gate",), .1), ("G", ("xg",), 1.)]
    s += [("V", ("rank", t, part), .52, ("rowbc",)) for t in range(XT) for part in range(2)] + [("V", ("ranks",), .1)]
    s += [("G", ("hot", t), 1.25) for t in range(XT)]
    s += [("T", ("pick", it), .6, ("hot", XT - 1)) for it in range(NT)] + [("A", ("h1",), .4)]
    s += norm_steps(1)
    s += [("T", ("v",), .3), ("A", ("v",), .4)]
    for g in range(2):
        s += [("T", ("q", g), .63), ("T", ("k", g), .63), ("A", ("q", g), .4, ("q", g)), ("A", ("k", g), .4, ("k", g)),
              ("V", ("q", g), .52, ("q", g)), ("V", ("k", g), .52, ("k", g))]
        for n in range(13):
            if n < 12:
                s += [("T", ("qk", g, n), .8 if n % 3 == 2 else 1.05, ("p", g, n - 1) if n else ("k", g))]
            if n:
                s += [("T", ("pt", g, n - 1), .33, ("p", g, n - 1)), ("A", ("ptc", g, n - 1), .45, ("pt", g, n - 1))]
            if n < 12:
                s += [("V", ("low", g, n), .46, ("qk", g, n)), ("A", ("p", g, n), .55, ("low", g, n))]
        s += [("T", ("pv_end", g), .2, ("ptc", g, 11)), ("V", ("rz", g), .1), ("V", ("o1", g), .25)]
    s += [("T", ("o1t",), .2), ("A", ("o1t",), .45), ("T", ("proj",), .1), ("V", ("h2",), .3)]
    s += norm_steps(2)
    return s


def norm_steps(i):
    return [("V", ("sum", i), .25), ("V", ("mean", i), .1), ("V", ("cen", i), .25), ("G", ("sq", i), .5),
            ("V", ("var", i), .25), ("V", ("veps", i), .1), ("G", ("rstd", i), .85), ("V", ("xn", i), .25),
            ("T", ("xnt", i), .3), ("A", ("xnt", i), .45)]


def topk_steps(g):
    s = [("T", ("qpk", g, p), .63) for p in range(2)] + [("A", ("qpk", g, p), .45, ("qpk", g, p)) for p in range(2)]
    for it in range(NT):
        s += [("T", ("sim", g, it), .86, ("qpk", g, 1)), ("A", ("sim", g, it), .6)]
    for it in range(NT):
        for what in ("max_a", "cut_a", "max_b", "cut_b"):
            s += [("V", (what, g, it, q), .135) + ((("sim", g, it),) if (what, q) == ("max_a", 0) else ()) for q in range(8)]
        s += [("V", ("max_c", g, it), .6)]
        s += [("G", ("cand", g, it, i), .2) for i in range(7)]
        for what in ("cmax_a", "ccut_a", "cmax_b", "ccut_b"):
            s += [("V", (what, g, it, q), .125) for q in range(4)]
        s += [("V", ("cmax_c", g, it), .3)]
    s += [("V", ("mid", g), .1), ("V", ("floor", g), .1), ("V", ("thr", g), .1), ("V", ("diff", g), .3),
          ("V", ("off1", g), .1), ("V", ("off0", g), .1), ("A", ("wexp", g), .4, ("diff", g)), ("V", ("zk", g), .3), ("V", ("rzk", g), .1)]
    s += [("G", ("shift", g, it), 1., ("off0", g)) for it in range(NT)] + [("G", ("clamp", g, it), 1.5) for it in range(NT)]
    return s


def head_steps(h):
    s = [("T", ("kvt", h), .33), ("V", ("kvn", h), .48), ("T", ("knt", h), .35), ("A", ("knt", h), .45)]
    if h % 2 == 0:
        s += [("T", ("q2", h // 2), .63), ("A", ("q2", h // 2), .45)]
    for r in range(2):
        s += [("T", ("qk2", h, r), .75), ("V", ("low2", h, r), .5), ("A", ("p2", h, r), .65), ("T", ("pt2", h, r), .33),
              ("A", ("ptc2", h, r), .45)]
    s += [("T", ("pv2", h), .7), ("V", ("rz2", h), .1), ("V", ("o2", h), .3)]
    if h % 2:
        s += [("T", ("o2t", h // 2), .31), ("A", ("o2t", h // 2), .45), ("T", ("wo", h // 2), .33), ("V", ("acc", h // 2), .3)]
    return s


FRONT = select_steps()
TOP = topk_steps(0) + [("G", ("keep_xn2",), .8)] + topk_steps(1)
BACK = [("G", ("keep_h2",), .4)] + [x for h in range(HEADS) for x in head_steps(h)]


def order(steps, engine):
    return [step[1] for step in steps if step[0] == engine]


SEQ = {thread: {e: order(steps, e) for e in "TVAG"} for thread, steps in (("front", FRONT), ("top", TOP), ("back", BACK))}
COUNT = {(t, e): {name: i + 1 for i, name in enumerate(SEQ[t][e])} for t in SEQ for e in "TVAG"}

LEAD = {"T": .8, "A": .7, "V": 1.2, "G": 0.}
ROOM = {"T": 1.5, "A": 1.2, "V": .8, "G": 2.}
DENSE = {"V": .46, "A": .46}
OVER = .4
HOP = .1


def place(timeline, load, thread, steps, first, last, batch, room=ROOM):
    end, at, previous = {}, dict.fromkeys("TVAG", first), None
    for engine, name, cost, *follows in steps:
        by, ready = end.get(follows[0] if follows else previous, (engine, 0.))
        ready += HOP * (by != engine)
        slot = at[engine]
        start = sum(LEAD["T"] + side for side in load["T"][:slot])
        while True:
            begin = start + LEAD[engine] + load[engine][slot]
            slack = max(LEAD["T"] + load["T"][slot] - DENSE[engine], .3) if engine in "VA" else 9.
            late = ready - begin > (0. if engine in "TG" else slack - load[engine][slot] - cost)
            if slot >= last or not (ready > begin and late or load[engine][slot] and load[engine][slot] + cost > min(room[engine], slack + OVER)):
                break
            start += LEAD["T"] + load["T"][slot]
            slot += 1
        timeline[slot].append((thread, engine, name, batch))
        begin = max(begin, ready)
        load[engine][slot] = begin + cost - start - LEAD[engine]
        end[name] = engine, begin + cost
        at[engine], previous = slot, name
    return max(at.values())


def timeline_of(kind):
    line = [[] for _ in range(SLOTS)]
    load = {e: [0.] * SLOTS for e in "TVAG"}
    for n in range(1, HEADS * COMBOS + (kind != "last")):
        for engine, slot, cost in (("G", -2, 1.4), ("T", 1, .33), ("A", 2, .4), ("V", 4, .52)):
            at = max(8 * (n - 1) + slot, 0)
            line[at].append(("combo", engine, ("combo", n % (HEADS * COMBOS)), n // (HEADS * COMBOS)))
            load[engine][at] += cost
    for h in range(HEADS):
        load["A"][PER_HEAD * h + 2] += .45
    ends = []
    if kind != "first":
        ends.append(place(line, load, "back", head_steps(HEADS - 1), 3, 28, -1))
        line[29].append(("back", "S", ("store",), -1))
    ends.append(place(line, load, "back", BACK[:1], 31, 31, 0))
    for h in range(HEADS - 1):
        ends.append(place(line, load, "back", head_steps(h), PER_HEAD * (h + 1) + 3, PER_HEAD * (h + 2) - 1, 0))
    group1 = [("G", ("keep_xn2",), .8)] + topk_steps(1)
    on_pe = max(i for i, step in enumerate(group1) if step[0] == "T") + 2
    free = place(line, load, "top", group1[:on_pe], 1, SLOTS - 1, 0) + 1
    ends.append(free)
    if kind != "last":
        ends.append(place(line, load, "front", select_steps(), free, SLOTS - 1, 1))
    ends.append(place(line, load, "top", group1[on_pe:], free, 4 * PER_HEAD - 20, 0))
    if kind != "last":
        ends.append(place(line, load, "top", topk_steps(0), max(ends[-2:]) + 1, SLOTS - 10, 1, dict(ROOM, V=.5)))
    return line


def build_kernel(nc, x, score_proj, qkv_w, qkv_b, proj_w, proj_b, rpb, wq_pk, pk_keys, wq, kv_table, wo, out):
    from contextlib import ExitStack
    import concourse.bass as bass
    from concourse import mybir

    F32, F16, BF16 = mybir.dt.float32, mybir.dt.float16, mybir.dt.bfloat16
    ALU, ACT, AX = mybir.AluOpType, mybir.ActivationFunctionType, mybir.AxisListType

    with ExitStack() as ctx:
        def sb(name, shape, dt=F32):
            return ctx.enter_context(nc.sbuf_tensor(name, shape, dt))

        def sem(name):
            return ctx.enter_context(nc.semaphore(name))

        table = sb("table", [128, 7, COMBOS, 8, 2 * DIM])
        sel = sb("sel", [128, 8, 128], F16)
        ident = sb("ident", [128, 128])
        identb = sb("identb", [128, 128], BF16)
        flip = sb("flip", [127, 127])
        causal = sb("causal", [TP, TP], BF16)
        ties = sb("ties", [TP, 11 * TP], BF16)
        ranks_row = sb("ranks_row", [TP, PICKED])
        neg_lo = sb("neg_lo", [128, 1])
        is_lo = sb("is_lo", [128, 2])
        w_score = sb("w_score", [TP, DIM])
        w_qk = sb("w_qk", [65, 2, 2, 4, 32])
        w_v = sb("w_v", [65, DIM])
        w_proj = sb("w_proj", [65, DIM])
        w_pk = sb("w_pk", [64, 512])
        w_q2 = sb("w_q2", [64, 512])
        w_o = sb("w_o", [128, 4, DIM])
        w_keys = sb("w_keys", [128, 4, 4, KEYS])
        hankel = sb("hankel", [TP, HEADS, 126])
        rel_tab = sb("rel_tab", [127, HEADS])

        xin = sb("xin", [TP, XT, DIM])
        xw = sb("xw", [TP, XT, DIM])
        xg = sb("xg", [TP, XT, DIM])
        junk = sb("junk", [TP, TOKENS], BF16)
        small = sb("small", [TP, 64])
        score, eneg, den, gate, rank = (small[:, 6 * i:6 * i + 6] for i in range(5))
        attn = sb("attn", [128, 2250])
        hot = attn[0:TP, :].rearrange("p (t r) -> p t r", t=XT)
        q_hi, qT, k_hi, kT = (attn[:, 0:750].bitcast(F16)[:, i * PICKED:(i + 1) * PICKED] for i in range(4))
        prob = attn[0:TP, 750:1500].rearrange("p (n r) -> p n r", n=2)
        probT = attn[0:TP, 1500:2250].rearrange("p (n r) -> p n r", n=2)
        h1 = sb("h1", [TP, NT, DIM])
        h2 = sb("h2", [TP, NT, DIM])
        cen = sb("cen", [TP, NT, DIM])
        sq = sb("sq", [TP, NT, DIM])
        xn = sb("xn", [TP, NT, DIM])
        stat = sb("stat", [TP, 5, NT])
        half = sb("half", [TP, NT])
        xnT = sb("xnT", [65, PICKED])
        vtok = sb("vtok", [TP, NT, DIM])
        low = sb("low", [TP, 2])
        zsum = sb("zsum", [TP, 24])
        rz = sb("rz", [TP, 24])
        o1 = sb("o1", [TP, NT, DIM])
        xn2 = sb("xn2", [64, PICKED])
        xn2k = sb("xn2k", [64, PICKED])
        qpkT = sb("qpkT", [128, 2, PICKED])
        sims = sb("sims", [TP, 2, NT, 4, 2, KEYS])
        left = sb("left", [TP, 8, KEYS])
        top = sb("top", [TP, NT, 8, 17])
        cand = sb("cand", [TP, 4, CAND])
        best = sb("best", [TP, NT, 4, 17])
        cut = sb("cut", [TP, 3, NT * 4])
        wk = sb("wk", [TP, NT * 4, TOPK])
        wke = sb("wke", [TP, NT * 4, TOPK])
        zk = sb("zk", [TP, NT * 4])
        rzk = sb("rzk", [TP, 2, NT * 4])
        off = sb("off", [TP, NT * 4, 2])

        quarter = sb("quarter", [TP, 2, NT, 2 * KEYS])
        hi = sb("hi", [128, PICKED], F16)
        halves = sb("halves", [128, 2, PICKED], F16)
        weight = sb("weight", [128, 4, PICKED])
        kvT = sb("kvT", [128, PICKED])
        kv = sb("kv", [TP, NT, 128])
        knT = sb("knT", [128, PICKED])
        q2T = sb("q2T", [128, PICKED])
        prob2 = sb("prob2", [TP, 2, PICKED])
        prob2T = sb("prob2T", [TP, 2, NT, TP])
        low2 = sb("low2", [TP, NT])
        z2 = sb("z2", [TP, NT])
        rz2 = sb("rz2", [TP, NT])
        o2 = sb("o2", [TP, NT, 128])
        o2T = knT
        result = sb("result", [TP, NT, DIM])
        shift = sb("shift", [128, 1])

        ext = kvT[0:HEADS, 0:250]

        banks = [ctx.enter_context(nc.psum_tensor(f"bank{i}", [128, 512], F32)) for i in range(8)]
        s_bank, kv_bank, fa, fb, combo_bank, back_bank = banks[0:3], banks[3], banks[4], banks[5], banks[6], banks[7]
        fa2 = [fa, fb]

        def score_bank(u):
            return fb if u == SLOTS - 1 else s_bank[u % 3]

        done = {(t, e): sem(f"{t}_{e}") for t in ("front", "top", "back") for e in "TVAG"}
        combo_done = {e: sem(f"combo_{e}") for e in "GTAV"}
        pair_scores, pair_exps, pair_weights, pair_sums = sem("pair_scores"), sem("pair_exps"), sem("pair_weights"), sem("pair_sums")
        kv_copied = sem("kv_copied")
        x_loaded, stored = sem("x_loaded"), sem("stored")
        weights_loaded, bias_loaded, hankel_loaded, swap_loaded = sem("weights_loaded"), sem("bias_loaded"), sem("hankel_loaded"), sem("swap_loaded")
        table_loaded = [sem(f"table_loaded{h}") for h in range(HEADS)]
        const_pool, zeroed, const_dve, const_pe, const_act = sem("const_pool"), sem("zeroed"), sem("const_dve"), sem("const_pe"), sem("const_act")
        const_dve0 = sem("const_dve0")
        heads_scaled, split_ready = sem("heads_scaled"), sem("split_ready")
        CONSTS = 24

        def reached(thread, engine, *step, b):
            return done[thread, engine], b * len(SEQ[thread][engine]) + COUNT[thread, engine][step]

        def wait(eng, s, value):
            if isinstance(value, int) and value <= 0:
                return
            eng.wait_ge(s, value)

        def wait_alone(eng, s, value):
            if not isinstance(value, int):
                value = eng.to_reg(value)
                eng.wait_ge(const_pool, CONSTS)
            wait(eng, s, value)

        def after_alone(eng, thread, engine, *step, b):
            wait_alone(eng, *reached(thread, engine, *step, b=b))

        def after(eng, thread, engine, *step, b):
            wait(eng, *reached(thread, engine, *step, b=b))

        def load_table(eng, h, s):
            rows = kv_table[h * 4096:(h + 1) * 4096, :].rearrange("(g b ah a t) c -> a g b ah (t c)", g=2, b=32, ah=2, a=4, t=8)
            for a in range(4):
                for g in range(2):
                    eng.dma_start(table[32 * a:32 * a + 32, table_slot(h), 2 * g:2 * g + 2].rearrange("p ah t c -> p ah (t c)"),
                                  rows[a, g]).then_inc(s, 16)

        block = ctx.enter_context(nc.Block())
        TL = {kind: timeline_of(kind) for kind in ("first", "mid", "last")}
        N_TABLE = 8 * 16
        N_WEIGHTS = 16 * 18
        first_batch, last_batch = 0, BATCH - 1

        def side(kind, slot, engine, steps, b):
            for thread, e, name, ahead in TL[kind][slot]:
                if e == engine:
                    steps[thread, name[0]](b + ahead, *name[1:])

        def prologue(engine, steps):
            for thread, part in (("front", select_steps()), ("top", topk_steps(0))):
                for name in order(part, engine):
                    steps[thread, name[0]](0, *name[1:])
            if engine in "GTAV":
                steps["combo", "combo"](0, 0)

        def run(eng, engine, steps, dense, flush, start=None):
            prologue(engine, steps)
            dense_batch(engine, steps, dense, "first", first_batch)
            with eng.Fori(1, last_batch) as b:
                dense_batch(engine, steps, dense, "mid", b)
            dense_batch(engine, steps, dense, "last", last_batch)
            flush(last_batch)
            for name in order(head_steps(HEADS - 1), engine):
                steps["back", name[0]](last_batch, *name[1:])

        def dense_batch(engine, steps, dense, kind, b):
            for u in range(SLOTS):
                dense(b, u)
                side(kind, u, engine, steps, b)

        @block.sync
        def _(sp):
            def load_x(b):
                if not isinstance(b, int) or b > 0:
                    after(sp, "front", "G", "xg", b=b - 1)
                sp.dma_start(xin[:, :, :], x[b].rearrange("(t p) f -> p t f", p=TP)).then_inc(x_loaded, 16)

            def store(b):
                after(sp, "back", "V", "acc", 3, b=b)
                sp.dma_start(out[b].rearrange("(t p) f -> p t f", p=TP), result[:, :, :]).then_inc(stored, 16)

            load_x(0)
            s = weights_loaded
            sp.dma_start(w_score[:, :], score_proj.rearrange("f o -> (o f)").partition_broadcast(TP)).then_inc(s, 16)
            sp.dma_start(rel_tab[:, :], rpb).then_inc(s, 16)
            sp.wait_ge(zeroed, 2)
            qkv = qkv_w.rearrange("c (k g h d) -> c k g h d", k=3, g=2, h=4)
            qkvb = qkv_b.rearrange("(o k g h d) -> o k g h d", o=1, k=3, g=2, h=4)
            for k in range(2):
                for g in range(2):
                    sp.dma_start(w_qk[0:64, k, g, :, 0:DH], qkv[:, k, g]).then_inc(s, 16)
                    sp.dma_start(w_qk[64:65, k, g, :, 0:DH], qkvb[:, k, g]).then_inc(s, 16)
            sp.dma_start(w_v[0:64, :], qkv_w[:, 128:192]).then_inc(s, 16)
            sp.dma_start(w_v[64:65, :], qkv_b.rearrange("(o n) -> o n", o=1)[:, 128:192]).then_inc(s, 16)
            sp.dma_start(w_proj[0:64, :], proj_w).then_inc(s, 16)
            sp.dma_start(w_proj[64:65, :], proj_b.rearrange("(o n) -> o n", o=1)).then_inc(s, 16)
            sp.dma_start(w_pk[:, :], wq_pk).then_inc(s, 16)
            sp.dma_start(w_q2[:, :], wq).then_inc(s, 16)
            sp.dma_start(w_o[:, :, :], wo.rearrange("(j p) n -> p j n", p=128)).then_inc(s, 16)
            sp.dma_start(attn[0:64, 0:512].rearrange("p (q n) -> p q n", q=2), pk_keys.rearrange("q k h d -> k q (h d)")).then_inc(s, 16)
            sp.wait_ge(const_dve, 1)
            for h in range(HEADS):
                row = ext[h:h + 1, :]
                sp.dma_start(hankel[:, h, :], bass.AP(row.tensor, row.offset, [row.ap[0], [1, TP], [1, 126]])).then_inc(hankel_loaded, 16)
            for h in range(HEADS - 1):
                load_table(sp, h, table_loaded[h])

            def batch(kind, b):
                if kind != "last":
                    load_x(b + 1)
                if kind != "first":
                    store(b - 1)
                sp.wait_ge(pair_sums, b * SLOTS + 4 * PER_HEAD)
                load_table(sp, 7, swap_loaded)
                if kind != "last":
                    sp.wait_ge(pair_sums, b * SLOTS + SLOTS)
                    load_table(sp, 3, swap_loaded)

            batch("first", 0)
            with sp.Fori(1, last_batch) as b:
                batch("mid", b)
            batch("last", last_batch)
            store(last_batch)
            sp.wait_ge(stored, 16 * BATCH)

        @block.gpsimd
        def _(pool):
            g = nc.gpsimd
            g.memset(w_qk[:, :, :, :, :], 0.0).then_inc(zeroed, 1)
            g.memset(w_keys[:, :, :, :], 0.0).then_inc(zeroed, 1)
            n = [0]

            def made(ins):
                n[0] += 1
                ins.then_inc(const_pool, 1)
                pool.wait_ge(const_pool, n[0])

            for m in (ident, identb, flip, causal, sel):
                made(g.memset(m[:], 0.0))
            made(g.memset(ties[:, 0:6 * TP], -TIE))
            made(g.memset(ties[:, 6 * TP:], 0.0))
            made(g.memset(neg_lo[:, :], 0.0))
            made(g.memset(neg_lo[32:64, :], -1.0))
            made(g.memset(neg_lo[96:128, :], -1.0))
            made(g.memset(half[:, :], -0.5))
            made(g.memset(shift[:, :], -SHIFT))
            made(g.memset(xnT[64:65, :], 1.0))
            made(g.memset(ext[:, 0:123], 0.0))
            for m in (ident, identb):
                made(g.affine_select(out=m[:, :], in_=m[:, :], compare_op=ALU.not_equal, fill=1.0, base=0,
                                     pattern=[[-1, 128]], channel_multiplier=1))
            made(g.affine_select(out=flip[:, :], in_=flip[:, :], compare_op=ALU.not_equal, fill=1.0, base=-126,
                                 pattern=[[1, 127]], channel_multiplier=1))
            made(g.affine_select(out=causal[:, :], in_=causal[:, :], compare_op=ALU.is_ge, fill=BIG, base=0,
                                 pattern=[[-1, TP]], channel_multiplier=1))
            tri = ties[:, 5 * TP:6 * TP]
            made(g.affine_select(out=tri, in_=tri, compare_op=ALU.is_gt, fill=0.0, base=0,
                                 pattern=[[-1, TP]], channel_multiplier=1))
            for r in (0, 32):
                v = sel[r:r + 32].rearrange("p t (a b) -> p t a b", a=4)
                made(g.affine_select(out=v, in_=v, compare_op=ALU.not_equal, fill=1.0, base=0,
                                     pattern=[[0, 8], [0, 4], [-1, 32]], channel_multiplier=1))
            for r in (64, 96):
                v = sel[r:r + 32].rearrange("p t (a b) -> p t a b", a=4)
                made(g.affine_select(out=v, in_=v, compare_op=ALU.not_equal, fill=1.0, base=0,
                                     pattern=[[-1, 8], [-8, 4], [0, 32]], channel_multiplier=1))
            made(g.iota(ranks_row[:, :], [[1, PICKED]], base=0, channel_multiplier=0, allow_small_or_imprecise_dtypes=True))

            fG, tG = done["front", "G"], done["top", "G"]

            def score_mul(b):
                if isinstance(b, int) and b == 0:
                    pool.wait_ge(weights_loaded, N_WEIGHTS)
                pool.wait_ge(x_loaded, b * 16 + 16)
                g.tensor_tensor(xw[:, :, :], xin[:, :, :], w_score[:, :].unsqueeze(1).broadcast_to([TP, XT, DIM]), ALU.mult).then_inc(fG, 1)

            def xg_(b):
                after(pool, "front", "V", "gate", b=b)
                after(pool, "front", "T", "pick", NT - 1, b=b - 1)
                g.tensor_tensor(xg[:, :, :], xin[:, :, :], gate.unsqueeze(2).broadcast_to([TP, XT, DIM]), ALU.mult).then_inc(fG, 1)

            def hot_(b, t):
                after_alone(pool, "front", "V", "ranks", b=b)
                if t == 0:
                    after_alone(pool, "front", "T", "pv_end", 1, b=b - 1)
                g.tensor_scalar(hot[:, t, :], ranks_row[:, :], rank[:, t:t + 1], None, ALU.is_equal).then_inc(fG, 1)

            def sq_(b, i):
                after(pool, "front", "V", "cen", i, b=b)
                g.tensor_tensor(sq[:, :, :], cen[:, :, :], cen[:, :, :], ALU.mult).then_inc(fG, 1)

            CAND_ROWS = [(0, 1, 17), (1, 1, 8), (2, 1, 5), (3, 1, 4), (4, 1, 3), (5, 3, 2), (8, 9, 1)]

            def cand_(b, gr, it, r):
                if r == 0:
                    after(pool, "top", "V", "max_c", gr, it, b=b)
                i0, ni, nj = CAND_ROWS[r]
                at = sum(a * c for _, a, c in CAND_ROWS[:r])
                t4 = top[:, it].rearrange("p (h q) k -> p h q k", q=2)
                o = cand[:, :, at:at + ni * nj].rearrange("p h (i j) -> p h i j", i=ni)
                g.tensor_tensor(o, t4[:, :, 1, i0:i0 + ni].unsqueeze(3).broadcast_to([TP, 4, ni, nj]),
                                t4[:, :, 0, 0:nj].unsqueeze(2).broadcast_to([TP, 4, ni, nj]), ALU.add).then_inc(tG, 1)

            def rstd(b, i):
                after(pool, "front", "V", "veps", i, b=b)
                g.tensor_tensor(stat[:, 4, :], stat[:, 3, :], half[:, :], ALU.pow).then_inc(done["front", "G"], 1)

            def shift_scores(b, gr, it):
                after(pool, "top", "V", "off0", gr, b=b)
                v = sims[:, gr, it].rearrange("p h q k -> p (h q) k")
                o = off[:, 4 * it:4 * it + 4, :].rearrange("p h q -> p (h q)").unsqueeze(2).broadcast_to([TP, 8, KEYS])
                g.tensor_tensor(v, v, o, ALU.add).then_inc(done["top", "G"], 1)

            def clamp(b, gr, it):
                after_alone(pool, "top", "G", "shift", gr, it, b=b)
                v = sims[:, gr, it].rearrange("p h q k -> p (h q k)")
                g.tensor_scalar(v, v, -60000.0, None, ALU.max).then_inc(done["top", "G"], 1)

            def combo(b, n):
                h, c = n // COMBOS, n % COMBOS
                gk, ah = c // 2, c % 2
                after(pool, "top", "G", "clamp", h // 4, NT - 1, b=b)
                wait_alone(pool, combo_done["T"], b * HEADS * COMBOS + n - 1)
                cols = sims[:, h // 4, :, h % 4].rearrange("p t q (g k) -> p t (q g) k", g=2)
                cols = cols[:, :, gk:2 + ah + 1:2 + ah - gk, :].unsqueeze(3).broadcast_to([TP, NT, 2, 2, 32])
                g.tensor_copy(quarter[:, n % 2].rearrange("p t (q d k) -> p t q d k", q=2, d=2), cols).then_inc(combo_done["G"], 1)

            def keep_xn2(b):
                after(pool, "front", "A", "xnt", 2, b=b)
                after(pool, "top", "T", "qpk", 1, 1, b=b - 1)
                after_alone(pool, "back", "T", "q2", 3, b=b - 1)
                g.tensor_copy(xn2k[:, :], xn2[:, :]).then_inc(done["top", "G"], 1)

            def keep_h2(b):
                after(pool, "front", "V", "h2", b=b)
                wait_alone(pool, stored, b * 16)
                g.tensor_copy(result[:, :, :], h2[:, :, :]).then_inc(done["back", "G"], 1)

            run(pool, "G", {("front", "score_mul"): score_mul, ("front", "xg"): xg_, ("front", "hot"): hot_, ("front", "sq"): sq_, ("top", "cand"): cand_,
                            ("front", "rstd"): rstd, ("top", "shift"): shift_scores, ("top", "clamp"): clamp,
                            ("combo", "combo"): combo, ("top", "keep_xn2"): keep_xn2, ("back", "keep_h2"): keep_h2},
                lambda b, u: None, lambda b: None)

        @block.tensor
        def _(pe):
            mm, tr = nc.tensor.matmul, nc.tensor.transpose
            fT, tT, bT = (done[thread, "T"] for thread in ("front", "top", "back"))

            pe.wait_ge(weights_loaded, N_WEIGHTS)
            pe.wait_ge(const_pool, CONSTS)
            mm(fa[0:HEADS, 0:127], rel_tab[:, :], flip[:, :], start=True, stop=True).then_inc(const_pe, 1)
            for q in range(2):
                for gr in range(2):
                    last = tr(fb[:, (q * 2 + gr) * 64:(q * 2 + gr) * 64 + 64], attn[0:64, q * 256 + gr * 128:q * 256 + gr * 128 + 128], ident[0:64, 0:64])
            last.then_inc(const_pe, 1)
            pe.wait_ge(const_dve, 2)
            pe.wait_ge(const_act, 1)
            pe.wait_ge(hankel_loaded, 16 * HEADS)
            pe.wait_ge(heads_scaled, 6)

            def rowbc(b):
                after(pe, "front", "V", "score", b=b)
                after(pe, "top", "A", "sim", 1, 2, b=b - 1)
                for t in range(XT):
                    last = tr(fa2[t // 3][0:TP, t % 3 * TP:t % 3 * TP + TP], score[:, t:t + 1].broadcast_to([TP, TP]), ident[0:TP, 0:TP])
                last.then_inc(fT, 1)

            def pick(b, it):
                if it == 0:
                    after(pe, "front", "G", "hot", XT - 1, b=b)
                for t in range(XT):
                    last = mm(fa[0:TP, it * DIM:it * DIM + DIM], hot[:, t, it * TP:it * TP + TP], xg[:, t, :], start=(t == 0), stop=(t == XT - 1))
                last.then_inc(fT, 1)

            def xnt(b, i):
                after_alone(pe, "front", "V", "xn", i, b=b)
                for it in range(NT):
                    last = tr(fb[0:64, it * TP:it * TP + TP], xn[:, it, :], ident[0:TP, 0:TP])
                last.then_inc(fT, 1)

            def v(b):
                after(pe, "front", "A", "xnt", 1, b=b)
                for it in range(NT):
                    last = mm(fa[0:TP, it * DIM:it * DIM + DIM], xnT[:, it * TP:it * TP + TP], w_v[:, :], start=True, stop=True)
                last.then_inc(fT, 1)

            def qk_proj(which, bank):
                def f(b, gr):
                    if which == 0:
                        if gr == 0:
                            after(pe, "front", "A", "v", b=b)
                        else:
                            after(pe, "front", "V", "o1", 0, b=b)
                    elif gr == 1:
                        after(pe, "front", "A", "ptc", 0, 11, b=b)
                    mm(bank[:, 0:PICKED], w_qk[:, which, gr].rearrange("p h d -> p (h d)"), xnT[:, :], start=True, stop=True).then_inc(fT, 1)
                return f

            def pv(gr, n):
                hh, it = n // NT, n % NT
                o = fa[0:TP, 384 + it * 32 + hh * DH:384 + it * 32 + hh * DH + DH]
                col = (gr * 4 + hh) * DH
                for jt in range(NT):
                    last = mm(o, probT[:, n % 2, jt * TP:jt * TP + TP], vtok[:, jt, col:col + DH], start=(jt == 0), stop=(jt == NT - 1))
                return last

            def qk(b, gr, n):
                hh, it = n // NT, n % NT
                if n == 0:
                    after(pe, "front", "V", "k", gr, b=b)
                else:
                    after(pe, "front", "A", "p", gr, n - 1, b=b)
                if n >= 2:
                    after(pe, "front", "A", "ptc", gr, n - 2, b=b)
                    pv(gr, n - 2)
                k0 = 32 * hh
                last = mm(fa[0:TP, 0:PICKED], qT[k0:k0 + 3 * DH, it * TP:it * TP + TP], kT[k0:k0 + 3 * DH, :], start=True, stop=True)
                if it == 0:
                    last = mm(fa[0:TP, 249:375], flip[0:TP, 2:127], hankel[:, gr * 4 + hh, :], start=False, stop=True, skip_group_check=True)
                elif it == 1:
                    last = mm(fa[0:TP, 374:375], flip[0:TP, 2:127], hankel[:, gr * 4 + hh, 0:1], start=False, stop=True, skip_group_check=True)
                last.then_inc(fT, 1)

            def pt(b, gr, n):
                after(pe, "front", "A", "p", gr, n, b=b)
                if n == 0:
                    after(pe, "front", "V", "k", gr, b=b)
                else:
                    after(pe, "front", "A", "ptc", gr, n - 1, b=b)
                for jt in range(NT):
                    last = tr(fb[0:TP, jt * TP:jt * TP + TP], prob[:, n % 2, jt * TP:jt * TP + TP], ident[0:TP, 0:TP])
                last.then_inc(fT, 1)

            def pv_end(b, gr):
                after(pe, "front", "A", "ptc", gr, 11, b=b)
                pv(gr, 10)
                pv(gr, 11).then_inc(fT, 1)

            def o1t(b):
                after_alone(pe, "front", "V", "o1", 1, b=b)
                for it in range(NT):
                    last = tr(fb[0:64, it * TP:it * TP + TP], o1[:, it, :], ident[0:TP, 0:TP])
                last.then_inc(fT, 1)

            def proj(b):
                after(pe, "front", "A", "o1t", b=b)
                for it in range(NT):
                    last = mm(fa[0:TP, it * DIM:it * DIM + DIM], xnT[:, it * TP:it * TP + TP], w_proj[:, :], start=True, stop=True)
                last.then_inc(fT, 1)

            def qpk(b, gr, p):
                if gr == 0:
                    after(pe, "front", "A", "xnt", 2, b=b)
                else:
                    after(pe, "top", "G", "keep_xn2", b=b)
                    if p == 0:
                        after(pe, "top", "A", "sim", 0, 2, b=b)
                    else:
                        wait(pe, pair_weights, b * SLOTS)
                src = (xn2, xn2k)[gr]
                col = p * 256 + gr * 128
                mm(fa2[p][:, 0:PICKED], w_pk[:, col:col + 128], src[:, :], start=True, stop=True).then_inc(tT, 1)

            def sim(b, gr, it):
                after(pe, "top", "A", "qpk", gr, 1, b=b)
                if it == 2:
                    after(pe, "top", "A", "sim", gr, 0, b=b)
                bank = fa2[it % 2]
                for q in range(2):
                    p = 1 - q
                    last = mm(bank[0:TP, q * 256:q * 256 + 256], qpkT[:, p, it * TP:it * TP + TP],
                              w_keys[:, p * 2 + gr].rearrange("p h k -> p (h k)"), start=True, stop=True)
                last.then_inc(tT, 1)

            def combo(b, n):
                wait(pe, combo_done["G"], b * HEADS * COMBOS + n + 1)
                wait(pe, combo_done["V"], b * HEADS * COMBOS + n)
                for it in range(NT):
                    last = tr(combo_bank[:, it * TP:it * TP + TP], quarter[:, n % 2, it, :], ident[0:TP, 0:TP])
                last.then_inc(combo_done["T"], 1)

            def out_mm(b, u):
                h, tile = u // PER_HEAD, u % PER_HEAD
                c, a8 = tile // 8, tile % 8
                if tile == 0:
                    wait(pe, kv_copied, b * HEADS + h)
                    if h == 3:
                        if isinstance(b, int) and b == 0:
                            pe.wait_ge(table_loaded[3], N_TABLE)
                        else:
                            pe.wait_ge(swap_loaded, b * 2 * N_TABLE)
                    elif h == 7:
                        pe.wait_ge(swap_loaded, b * 2 * N_TABLE + N_TABLE)
                    elif isinstance(b, int) and b == 0:
                        pe.wait_ge(table_loaded[h], N_TABLE)
                pe.wait_ge(pair_weights, b * SLOTS + u + 1)
                t = table[:, table_slot(h), c, a8, :]
                mm(kv_bank[:, 0:PICKED], t, weight[:, u % 4, :], start=(tile == 0), stop=(tile == PER_HEAD - 1)).then_inc(pair_sums, 1)

            def dense(b, u):
                if u % 8 == 0:
                    pe.wait_ge(combo_done["V"], b * HEADS * COMBOS + u // 8 + 1)
                if u == SLOTS - 1:
                    if isinstance(b, int) and b == last_batch:
                        after(pe, "top", "A", "sim", 1, NT - 1, b=b)
                    else:
                        after(pe, "top", "A", "sim", 0, NT - 1, b=b + 1)
                mm(score_bank(u)[:, 0:PICKED], sel[:, u % 8, :], halves[:, u // 8 % 2, :], start=True, stop=True).then_inc(pair_scores, 1)
                if u >= 2:
                    out_mm(b, u - 2)
                elif not isinstance(b, int) or b > 0:
                    out_mm(b - 1, SLOTS - 2 + u)

            def flush(b):
                out_mm(b, SLOTS - 2)
                out_mm(b, SLOTS - 1)

            def kvt(b, h):
                wait(pe, kv_copied, b * HEADS + h + 1)
                if h % 2 == 0 and h > 0:
                    after(pe, "back", "V", "acc", h // 2 - 1, b=b)
                elif h == 0:
                    after(pe, "back", "V", "acc", 3, b=b - 1)
                else:
                    after(pe, "back", "V", "o2", h - 1, b=b)
                for it in range(NT):
                    last = tr(back_bank[0:TP, it * 128:it * 128 + 128], kvT[:, it * TP:it * TP + TP], ident[:, :])
                last.then_inc(bT, 1)

            def knt(b, h):
                after(pe, "back", "V", "kvn", h, b=b)
                for it in range(NT):
                    last = tr(back_bank[:, it * TP:it * TP + TP], kv[:, it, :], ident[0:TP, 0:TP])
                last.then_inc(bT, 1)

            def q2(b, j):
                after(pe, "back", "A", "knt", 2 * j, b=b)
                after(pe, "top", "G", "keep_xn2", b=b)
                mm(back_bank[:, 0:PICKED], w_q2[:, j * 128:j * 128 + 128], xn2k[:, :], start=True, stop=True).then_inc(bT, 1)

            def qk2(b, h, r):
                if r == 0:
                    if h % 2 == 0:
                        after(pe, "back", "A", "q2", h // 2, b=b)
                    else:
                        after(pe, "back", "A", "knt", h, b=b)
                else:
                    after(pe, "back", "A", "ptc2", h, 0, b=b)
                rows = slice(64 * (h % 2), 64 * (h % 2) + 64)
                for it, at in (((0, 0), (1, TP)) if r == 0 else ((2, 0),)):
                    n = TP * (it + 1)
                    mm(back_bank[0:TP, at:at + n], q2T[rows, it * TP:it * TP + TP], knT[rows, 0:n], start=True, stop=True)
                    last = mm(back_bank[0:TP, at + n - TP:at + n], identb[0:TP, 0:TP], causal[:, :], start=False, stop=True, skip_group_check=True)
                last.then_inc(bT, 1)

            def pt2(b, h, r):
                after(pe, "back", "A", "p2", h, r, b=b)
                for jt in range(NT):
                    last = tr(back_bank[0:TP, jt * TP:jt * TP + TP], prob2[:, r, jt * TP:jt * TP + TP], ident[0:TP, 0:TP])
                last.then_inc(bT, 1)

            def pv2(b, h):
                after(pe, "back", "A", "ptc2", h, 1, b=b)
                v0 = DIM * (1 - h % 2)
                for it in range(NT):
                    for jt in range(it + 1):
                        p = prob2T[:, 1, jt, :] if it == 2 else prob2T[:, 0, it + jt, :]
                        last = mm(back_bank[0:TP, it * DIM:it * DIM + DIM], p, kv[:, jt, v0:v0 + DIM], start=(jt == 0), stop=(jt == it))
                last.then_inc(bT, 1)

            def o2t(b, j):
                after(pe, "back", "V", "o2", 2 * j + 1, b=b)
                for it in range(NT):
                    last = tr(back_bank[:, it * TP:it * TP + TP], o2[:, it, :], ident[0:TP, 0:TP])
                last.then_inc(bT, 1)

            def wo_mm(b, j):
                after(pe, "back", "A", "o2t", j, b=b)
                for it in range(NT):
                    last = mm(back_bank[0:TP, it * DIM:it * DIM + DIM], o2T[:, it * TP:it * TP + TP], w_o[:, j, :], start=True, stop=True)
                last.then_inc(bT, 1)

            run(pe, "T", {("front", "rowbc"): rowbc, ("front", "pick"): pick, ("front", "xnt"): xnt, ("front", "v"): v,
                          ("front", "q"): qk_proj(0, fa), ("front", "k"): qk_proj(1, fb), ("front", "qk"): qk, ("front", "pt"): pt,
                          ("front", "pv_end"): pv_end, ("front", "o1t"): o1t, ("front", "proj"): proj, ("top", "qpk"): qpk,
                          ("top", "sim"): sim, ("combo", "combo"): combo, ("back", "kvt"): kvt, ("back", "knt"): knt,
                          ("back", "q2"): q2, ("back", "qk2"): qk2, ("back", "pt2"): pt2, ("back", "pv2"): pv2,
                          ("back", "o2t"): o2t, ("back", "wo"): wo_mm}, dense, flush)

        @block.scalar
        def _(act):
            fA, tA, bA = (done[thread, "A"] for thread in ("front", "top", "back"))

            def copy(out, in_, s, scale=1.0):
                nc.scalar.activation(out, in_, ACT.Copy, scale=scale).then_inc(s, 1)

            act.wait_ge(const_pe, 2)
            act.wait_ge(zeroed, 2)
            for q in range(2):
                for gr in range(2):
                    for hh in range(4):
                        at = (q * 2 + gr) * 64
                        last = nc.scalar.activation(w_keys[32 * hh:32 * hh + 32, q * 2 + gr, hh, :], fb[32 * hh:32 * hh + 32, at:at + 64], ACT.Copy)
            last.then_inc(const_act, 1)
            act.wait_ge(const_pool, CONSTS)

            def eneg(b):
                after(act, "front", "V", "score", b=b)
                after(act, "front", "V", "den", b=b - 1)
                nc.scalar.activation(eneg_, score, ACT.Exp, scale=-1.0).then_inc(fA, 1)

            def h1_(b):
                after(act, "front", "T", "pick", NT - 1, b=b)
                after(act, "front", "V", "h2", b=b - 1)
                copy(h1[:, :, :], fa[0:TP, 0:NT * DIM].rearrange("p (t f) -> p t f", t=NT), fA)

            def xnt(b, i):
                after(act, "front", "T", "xnt", i, b=b)
                if i == 1:
                    after(act, "front", "T", "proj", b=b - 1)
                else:
                    after(act, "top", "T", "qpk", 0, 1, b=b - 1)
                    after(act, "top", "G", "keep_xn2", b=b - 1)
                copy((xnT[0:64, :], xn2[:, :])[i - 1], fb[0:64, 0:PICKED], fA)

            def v(b):
                after(act, "front", "T", "v", b=b)
                after(act, "front", "T", "pv_end", 1, b=b - 1)
                copy(vtok[:, :, :], fa[0:TP, 0:NT * DIM].rearrange("p (t f) -> p t f", t=NT), fA)

            def q(b, gr):
                after(act, "front", "T", "q", gr, b=b)
                copy(q_hi, fa[:, 0:PICKED], fA)

            def k(b, gr):
                after(act, "front", "T", "k", gr, b=b)
                copy(k_hi, fb[:, 0:PICKED], fA)

            def p(b, gr, n):
                after(act, "front", "V", "low", gr, n, b=b)
                if n >= 2:
                    after(act, "front", "T", "pt", gr, n - 2, b=b)
                hh, it = n // NT, n % NT
                z = zsum[:, gr * 12 + it * 4 + hh:gr * 12 + it * 4 + hh + 1]
                nc.scalar.activation(prob[:, n % 2, :], fa[0:TP, 0:PICKED], ACT.Exp, bias=low[:, n % 2:n % 2 + 1], scale=-1.0, accum_out=z).then_inc(fA, 1)

            def ptc(b, gr, n):
                after(act, "front", "T", "pt", gr, n, b=b)
                if n >= 2:
                    after(act, "front", "T", "qk", gr, n, b=b)
                copy(probT[:, n % 2, :], fb[0:TP, 0:PICKED], fA)

            def o1t(b):
                after(act, "front", "T", "o1t", b=b)
                copy(xnT[0:64, :], fb[0:64, 0:PICKED], fA)

            def qpk(b, gr, p):
                after(act, "top", "T", "qpk", gr, p, b=b)
                copy(qpkT[:, p, :], fa2[p][:, 0:PICKED], tA)

            def sim(b, gr, it):
                after(act, "top", "T", "sim", gr, it, b=b)
                if it == 0:
                    wait(act, combo_done["G"], (b - 1) * HEADS * COMBOS + 16 * (gr + 1))
                copy(sims[:, gr, it].rearrange("p h q k -> p q h k"), fa2[it % 2][0:TP, :].rearrange("p (q h k) -> p q h k", q=2, h=4), tA)

            def wexp(b, gr):
                after(act, "top", "V", "diff", gr, b=b)
                nc.scalar.activation(wke[:, :, :], wk[:, :, :], ACT.Exp, bias=shift[0:TP, :]).then_inc(tA, 1)

            def combo(b, n):
                wait(act, combo_done["T"], b * HEADS * COMBOS + n + 1)
                copy(hi[:, :], combo_bank[:, 0:PICKED], combo_done["A"])

            def dense(b, u):
                if u % PER_HEAD == 2 and u > 2:
                    kv_copy(b, u // PER_HEAD - 1)
                elif u == 2 and (not isinstance(b, int) or b > 0):
                    kv_copy(b - 1, HEADS - 1)
                act.wait_ge(pair_scores, b * SLOTS + u + 1)
                nc.scalar.activation(weight[:, u % 4, :], score_bank(u)[:, 0:PICKED], ACT.Exp, bias=shift[:, :]).then_inc(pair_exps, 1)

            def kv_copy(b, h):
                act.wait_ge(pair_sums, b * SLOTS + (h + 1) * PER_HEAD)
                if h == 0:
                    after(act, "back", "T", "kvt", HEADS - 1, b=b - 1)
                else:
                    after(act, "back", "T", "kvt", h - 1, b=b)
                copy(kvT[:, :], kv_bank[:, 0:PICKED], kv_copied)

            def flush(b):
                kv_copy(b, HEADS - 1)

            def knt(b, h):
                after(act, "back", "T", "knt", h, b=b)
                r = slice(64 * (h % 2), 64 * (h % 2) + 64)
                copy(knT[r, :], back_bank[r, 0:PICKED], bA)

            def q2(b, j):
                after(act, "back", "T", "q2", j, b=b)
                copy(q2T[:, :], back_bank[:, 0:PICKED], bA, scale=-DIM ** -0.5)

            def p2(b, h, r):
                after(act, "back", "V", "low2", h, r, b=b)
                for it, at, n in (((0, 0, TP), (1, TP, 2 * TP)) if r == 0 else ((2, 0, 3 * TP),)):
                    last = nc.scalar.activation(prob2[:, r, at:at + n], back_bank[0:TP, at:at + n], ACT.Exp, bias=low2[:, it:it + 1], scale=-1.0,
                                                accum_out=z2[:, it:it + 1])
                last.then_inc(bA, 1)

            def ptc2(b, h, r):
                after(act, "back", "T", "pt2", h, r, b=b)
                copy(prob2T[:, r].rearrange("p j i -> p (j i)"), back_bank[0:TP, 0:PICKED], bA)

            def o2t(b, j):
                after(act, "back", "T", "o2t", j, b=b)
                copy(o2T[:, :], back_bank[:, 0:PICKED], bA)

            eneg_ = small[:, 6:12]
            run(act, "A", {("front", "eneg"): eneg, ("front", "h1"): h1_, ("front", "xnt"): xnt, ("front", "v"): v, ("front", "q"): q,
                           ("front", "k"): k, ("front", "p"): p, ("front", "ptc"): ptc, ("front", "o1t"): o1t, ("top", "qpk"): qpk,
                           ("top", "sim"): sim, ("top", "wexp"): wexp, ("combo", "combo"): combo, ("back", "knt"): knt,
                           ("back", "q2"): q2, ("back", "p2"): p2, ("back", "ptc2"): ptc2, ("back", "o2t"): o2t}, dense, flush)

        @block.vector
        def _(dve):
            V = nc.vector
            fV, tV, bV = (done[thread, "V"] for thread in ("front", "top", "back"))

            dve.wait_ge(const_pe, 1)
            dve.wait_ge(const_pool, CONSTS)
            ext0 = small[0:HEADS, 40:41]
            V.tensor_copy(ext0, fa[0:HEADS, 0:1]).then_inc(const_dve0, 1)
            dve.wait_ge(const_dve0, 1)
            V.tensor_scalar(ext[:, 123:250], fa[0:HEADS, 0:127], ext0, -1.0, ALU.subtract, ALU.mult).then_inc(const_dve, 2)

            dve.wait_ge(weights_loaded, N_WEIGHTS)
            for k, factor in enumerate((DH ** -0.5, -1.0)):
                first = w_qk[:, k, :, :, 0:DH].rearrange("p g h d -> p (g h) d")
                for copy_ in (1, 2):
                    V.tensor_scalar(w_qk[:, k, :, :, copy_ * DH:copy_ * DH + DH].rearrange("p g h d -> p (g h) d"), first, factor, None, ALU.mult).then_inc(heads_scaled, 1)
            dve.wait_ge(heads_scaled, 4)
            for k, factor in enumerate((DH ** -0.5, -1.0)):
                first = w_qk[:, k, :, :, 0:DH].rearrange("p g h d -> p (g h) d")
                V.tensor_scalar(first, first, factor, None, ALU.mult).then_inc(heads_scaled, 1)
            for k, rows_ in enumerate((2, 1)):
                V.tensor_reduce(is_lo[:, k:k + 1], ident[:, :].rearrange("p (h d) -> p h d", h=4)[:, :, rows_ * DH:rows_ * DH + DH], AX.XY, ALU.add).then_inc(split_ready, 1)
            dve.wait_ge(split_ready, 2)

            def score_(b):
                after(dve, "front", "G", "score_mul", b=b)
                after(dve, "front", "T", "rowbc", b=b - 1)
                V.tensor_reduce(score, xw[:, :, :], AX.X, ALU.add).then_inc(fV, 1)

            def den_(b):
                after(dve, "front", "A", "eneg", b=b)
                V.tensor_scalar(den, eneg, 1.0, None, ALU.add).then_inc(fV, 1)

            def gate_(b):
                after(dve, "front", "V", "den", b=b)
                V.reciprocal(gate, den).then_inc(fV, 1)

            def rank_(b, t, part):
                if (t, part) == (0, 0):
                    after(dve, "front", "T", "rowbc", b=b)
                else:
                    after(dve, "front", "V", "rank", *((t, 0) if part else (t - 1, 1)), b=b)
                at, lag = part * 375, (5 - t) * TP
                V.scalar_tensor_tensor(out=junk[:, at:at + 375], in0=fa2[part][0:TP, 0:375], scalar=score[:, t:t + 1],
                                       in1=ties[:, lag + at:lag + at + 375], op0=ALU.subtract, op1=ALU.is_gt,
                                       accum_out=rank2[:, part * 6 + t:part * 6 + t + 1]).then_inc(fV, 1)

            rank2 = small[:, 42:54]

            def ranks(b):
                after(dve, "front", "V", "rank", XT - 1, 1, b=b)
                V.tensor_tensor(rank, rank2[:, 0:6], rank2[:, 6:12], ALU.add).then_inc(fV, 1)

            def rows(i):
                return (h1, h2)[i - 1]

            def sum_(b, i):
                if i == 1:
                    after(dve, "front", "A", "h1", b=b)
                else:
                    after(dve, "front", "V", "h2", b=b)
                V.tensor_reduce(stat[:, 0, :], rows(i)[:, :, :], AX.X, ALU.add).then_inc(fV, 1)

            def mean(b, i):
                after(dve, "front", "V", "sum", i, b=b)
                V.tensor_scalar(stat[:, 1, :], stat[:, 0, :], 1.0 / DIM, None, ALU.mult).then_inc(fV, 1)

            def wide(ap):
                return ap.unsqueeze(2).broadcast_to([TP, NT, DIM])

            def cen_(b, i):
                after(dve, "front", "V", "mean", i, b=b)
                V.tensor_tensor(cen[:, :, :], rows(i)[:, :, :], wide(stat[:, 1, :]), ALU.subtract).then_inc(fV, 1)

            def var(b, i):
                after(dve, "front", "G", "sq", i, b=b)
                V.tensor_reduce(stat[:, 2, :], sq[:, :, :], AX.X, ALU.add).then_inc(fV, 1)

            def veps(b, i):
                after(dve, "front", "V", "var", i, b=b)
                V.tensor_scalar(stat[:, 3, :], stat[:, 2, :], 1.0 / DIM, 1e-5, ALU.mult, ALU.add).then_inc(fV, 1)

            def xn_(b, i):
                after(dve, "front", "G", "rstd", i, b=b)
                after(dve, "front", "T", "xnt", 3 - i, b=b - (i == 1))
                V.tensor_tensor(xn[:, :, :], cen[:, :, :], wide(stat[:, 4, :]), ALU.mult).then_inc(fV, 1)

            def split(which, bank, hi_, out_):
                def f(b, gr):
                    after(dve, "front", "A", which, gr, b=b)
                    V.scalar_tensor_tensor(out=out_, in0=hi_, scalar=is_lo[:, "qk".index(which):"qk".index(which) + 1], in1=bank[:, 0:PICKED],
                                           op0=ALU.mult, op1=ALU.subtract).then_inc(fV, 1)
                return f

            def low_(b, gr, n):
                after(dve, "front", "T", "qk", gr, n, b=b)
                V.tensor_reduce(low[:, n % 2:n % 2 + 1], fa[0:TP, 0:PICKED], AX.X, ALU.min).then_inc(fV, 1)

            def rz_(b, gr):
                after(dve, "front", "A", "p", gr, 11, b=b)
                V.reciprocal(rz[:, gr * 12:gr * 12 + 12], zsum[:, gr * 12:gr * 12 + 12]).then_inc(fV, 1)

            def o1_(b, gr):
                after(dve, "front", "T", "pv_end", gr, b=b)
                after(dve, "front", "V", "rz", gr, b=b)
                after(dve, "front", "T", "o1t", b=b - 1)
                V.tensor_tensor(o1[:, :, gr * 32:gr * 32 + 32].rearrange("p t (h d) -> p t h d", h=4),
                                fa[0:TP, 384:480].rearrange("p (t h d) -> p t h d", t=NT, h=4),
                                rz[:, gr * 12:gr * 12 + 12].rearrange("p (t h) -> p t h", t=NT).unsqueeze(3).broadcast_to([TP, NT, 4, DH]),
                                ALU.mult).then_inc(fV, 1)

            def h2_(b):
                after(dve, "front", "T", "proj", b=b)
                after(dve, "back", "G", "keep_h2", b=b - 1)
                V.tensor_tensor(h2[:, :, :], h1[:, :, :], fa[0:TP, 0:NT * DIM].rearrange("p (t f) -> p t f", t=NT), ALU.add).then_inc(fV, 1)

            def group(gr, it, q):
                return sims[:, gr, it].rearrange("p h q k -> p (h q) k")[:, q, :]

            def max_a(b, gr, it, q):
                if q == 0:
                    after_alone(dve, "top", "A", "sim", gr, it, b=b)
                V.max(top[:, it, q, 0:8], group(gr, it, q)).then_inc(tV, 1)

            def cut_a(b, gr, it, q):
                if q == 0:
                    after_alone(dve, "top", "V", "max_a", gr, it, 7, b=b)
                V.match_replace(left[:, q, :], top[:, it, q, 0:8], group(gr, it, q), -3e38).then_inc(tV, 1)

            def max_b(b, gr, it, q):
                if q == 0:
                    after_alone(dve, "top", "V", "cut_a", gr, it, 7, b=b)
                V.max(top[:, it, q, 8:16], left[:, q, :]).then_inc(tV, 1)

            def cut_b(b, gr, it, q):
                if q == 0:
                    after_alone(dve, "top", "V", "max_b", gr, it, 7, b=b)
                V.match_replace(left[:, q, :], top[:, it, q, 8:16], left[:, q, :], -3e38).then_inc(tV, 1)

            def max_c(b, gr, it):
                after(dve, "top", "V", "cut_b", gr, it, 7, b=b)
                V.tensor_reduce(top[:, it, :, 16:17].rearrange("p q o -> p (q o)"), left[:, :, :], AX.X, ALU.max).then_inc(tV, 1)

            def cmax_a(b, gr, it, q):
                if q == 0:
                    after_alone(dve, "top", "G", "cand", gr, it, 6, b=b)
                V.max(best[:, it, q, 0:8], cand[:, q, :]).then_inc(tV, 1)

            def ccut_a(b, gr, it, q):
                if q == 0:
                    after_alone(dve, "top", "V", "cmax_a", gr, it, 3, b=b)
                V.match_replace(cand[:, q, :], best[:, it, q, 0:8], cand[:, q, :], -3e38).then_inc(tV, 1)

            def cmax_b(b, gr, it, q):
                if q == 0:
                    after_alone(dve, "top", "V", "ccut_a", gr, it, 3, b=b)
                V.max(best[:, it, q, 8:16], cand[:, q, :]).then_inc(tV, 1)

            def ccut_b(b, gr, it, q):
                if q == 0:
                    after_alone(dve, "top", "V", "cmax_b", gr, it, 3, b=b)
                V.match_replace(cand[:, q, :], best[:, it, q, 8:16], cand[:, q, :], -3e38).then_inc(tV, 1)

            def cmax_c(b, gr, it):
                after(dve, "top", "V", "ccut_b", gr, it, 3, b=b)
                V.tensor_reduce(best[:, it, :, 16:17].rearrange("p h o -> p (h o)"), cand[:, :, :], AX.X, ALU.max).then_inc(tV, 1)

            best2 = best[:, :, :, :].rearrange("p t h k -> p (t h) k")
            top2 = top[:, :, :, :].rearrange("p t (h q) k -> p (t h) q k", q=2)

            def mid(b, gr):
                after(dve, "top", "V", "cmax_c", gr, NT - 1, b=b)
                V.tensor_tensor(cut[:, 0, :], best2[:, :, 15], best2[:, :, 16], ALU.add).then_inc(tV, 1)

            def floor(b, gr):
                V.tensor_scalar(cut[:, 1, :], best2[:, :, 0], -SPAN, None, ALU.add).then_inc(tV, 1)

            def thr(b, gr):
                after(dve, "top", "V", "floor", gr, b=b)
                V.scalar_tensor_tensor(out=cut[:, 2, :], in0=cut[:, 0, :], scalar=0.5, in1=cut[:, 1, :], op0=ALU.mult, op1=ALU.max).then_inc(tV, 1)

            def diff(b, gr):
                after(dve, "top", "V", "thr", gr, b=b)
                V.tensor_tensor(wk[:, :, :], best2[:, :, 0:16], cut[:, 2, :].unsqueeze(2).broadcast_to([TP, NT * 4, TOPK]), ALU.subtract).then_inc(tV, 1)

            def zk_(b, gr):
                after(dve, "top", "A", "wexp", gr, b=b)
                V.tensor_reduce(zk[:, :], wke[:, :, :], AX.X, ALU.add).then_inc(tV, 1)

            def rzk_(b, gr):
                after(dve, "top", "V", "zk", gr, b=b)
                after(dve, "back", "V", "kvn", 4 * gr + 3, b=b - 1)
                V.reciprocal(rzk[:, gr, :], zk[:, :]).then_inc(tV, 1)

            def off1(b, gr):
                after(dve, "top", "G", "shift", 1 - gr, NT - 1, b=b - (gr == 0))
                V.tensor_scalar(off[:, :, 0], top2[:, :, 0, 0], -1.0, None, ALU.mult).then_inc(tV, 1)

            def off0(b, gr):
                V.tensor_tensor(off[:, :, 1], top2[:, :, 0, 0], cut[:, 2, :], ALU.subtract).then_inc(tV, 1)

            def combo(b, n):
                wait(dve, combo_done["A"], b * HEADS * COMBOS + n + 1)
                wait(dve, pair_scores, b * SLOTS + 8 * (n - 1))
                V.scalar_tensor_tensor(out=halves[:, n % 2, :], in0=hi[:, :], scalar=neg_lo[:, 0:1], in1=combo_bank[:, 0:PICKED],
                                       op0=ALU.mult, op1=ALU.add).then_inc(combo_done["V"], 1)

            def dense(b, u):
                dve.wait_ge(pair_exps, b * SLOTS + u + 1)
                V.scalar_tensor_tensor(out=weight[:, u % 4, :], in0=score_bank(u)[:, 0:PICKED], scalar=0.0, in1=weight[:, u % 4, :],
                                       op0=ALU.is_ge, op1=ALU.mult).then_inc(pair_weights, 1)

            def kvn(b, h):
                after(dve, "back", "T", "kvt", h, b=b)
                after(dve, "top", "V", "rzk", h // 4, b=b)
                if h > 0:
                    after(dve, "back", "T", "pv2", h - 1, b=b)
                else:
                    after(dve, "back", "T", "pv2", HEADS - 1, b=b - 1)
                r = rzk[:, h // 4, :].rearrange("p (t h) -> p t h", t=NT)[:, :, h % 4].unsqueeze(2).broadcast_to([TP, NT, 128])
                V.tensor_tensor(kv[:, :, :], back_bank[0:TP, 0:NT * 128].rearrange("p (t c) -> p t c", t=NT), r, ALU.mult).then_inc(bV, 1)

            def low2_(b, h, r):
                after(dve, "back", "T", "qk2", h, r, b=b)
                if r == 0:
                    V.tensor_reduce(low2[:, 0:1], back_bank[0:TP, 0:TP], AX.X, ALU.min)
                    V.tensor_reduce(low2[:, 1:2], back_bank[0:TP, TP:3 * TP], AX.X, ALU.min).then_inc(bV, 1)
                else:
                    V.tensor_reduce(low2[:, 2:3], back_bank[0:TP, 0:3 * TP], AX.X, ALU.min).then_inc(bV, 1)

            def rz2_(b, h):
                after(dve, "back", "A", "p2", h, 1, b=b)
                V.reciprocal(rz2[:, :], z2[:, :]).then_inc(bV, 1)

            def o2_(b, h):
                after(dve, "back", "T", "pv2", h, b=b)
                after(dve, "back", "V", "rz2", h, b=b)
                V.tensor_tensor(o2[:, :, 64 * (h % 2):64 * (h % 2) + 64], back_bank[0:TP, 0:NT * DIM].rearrange("p (t f) -> p t f", t=NT),
                                wide(rz2[:, :]), ALU.mult).then_inc(bV, 1)

            def acc(b, j):
                after(dve, "back", "T", "wo", j, b=b)
                after(dve, "back", "G", "keep_h2", b=b)
                V.tensor_tensor(result[:, :, :], result[:, :, :], back_bank[0:TP, 0:NT * DIM].rearrange("p (t f) -> p t f", t=NT), ALU.add).then_inc(bV, 1)

            run(dve, "V", {("front", "score"): score_, ("front", "den"): den_, ("front", "gate"): gate_,
                           ("front", "rank"): rank_, ("front", "ranks"): ranks, 
                           ("front", "sum"): sum_, ("front", "mean"): mean, ("front", "cen"): cen_, 
                           ("front", "var"): var, ("front", "veps"): veps, ("front", "xn"): xn_, ("front", "low"): low_,
                           ("front", "q"): split("q", fa, q_hi, qT), ("front", "k"): split("k", fb, k_hi, kT), ("front", "rz"): rz_, ("front", "o1"): o1_, ("front", "h2"): h2_,
                           ("top", "max_a"): max_a, ("top", "cut_a"): cut_a, ("top", "max_b"): max_b, ("top", "cut_b"): cut_b,
                           ("top", "max_c"): max_c, ("top", "cmax_a"): cmax_a, ("top", "ccut_a"): ccut_a,
                           ("top", "cmax_b"): cmax_b, ("top", "ccut_b"): ccut_b, ("top", "cmax_c"): cmax_c, ("top", "mid"): mid,
                           ("top", "floor"): floor, ("top", "thr"): thr, ("top", "diff"): diff, ("top", "zk"): zk_,
                           ("top", "rzk"): rzk_, ("top", "off1"): off1, ("top", "off0"): off0, ("combo", "combo"): combo,
                           ("back", "kvn"): kvn, ("back", "low2"): low2_, ("back", "rz2"): rz2_,
                           ("back", "o2"): o2_, ("back", "acc"): acc}, dense, lambda b: None)


_INS = ['x', 'L0_tok_score_proj', 'L0_attn_qkv_w', 'L0_attn_qkv_b', 'L0_attn_proj_w', 'L0_attn_proj_b', 'L0_attn_rpb_table',
        'L0_ffn_Wq_pk', 'L0_ffn_pk_keys', 'L0_ffn_Wq', 'kv_table', 'L0_ffn_Wo']
_OUTS = [((16, 375, 64), 'float32')]


def kernel(**inputs):
    import numpy as _np
    import concourse.bacc as _bacc
    from concourse import mybir as _mybir
    from concourse.bass_utils import run_bass_kernel_spmd as _run

    nc = _bacc.Bacc("TRN2", target_bir_lowering=False, num_devices=1)
    laid = dict(inputs)
    k, v = (_np.asarray(inputs[n]).reshape(HEADS, -1, DIM) for n in ('L0_ffn_keys_table', 'L0_ffn_values_table'))
    laid['kv_table'] = _np.concatenate([_np.concatenate([(k, v)[h % 2][h], (v, k)[h % 2][h]], axis=1) for h in range(HEADS)])
    arrays, args = {}, []
    for name in _INS:
        a = _np.ascontiguousarray(laid[name])
        arrays[f"in_{name}_dram"] = a
        args.append(nc.dram_tensor(f"in_{name}_dram", a.shape, _mybir.dt.from_np(a.dtype), kind="ExternalInput").ap())
    for i, (shape, dtype) in enumerate(_OUTS):
        dt = _mybir.dt.from_np(_np.dtype(dtype))
        args.append(nc.dram_tensor(f"out_{i}_dram", shape, dt, kind="ExternalOutput").ap())
    build_kernel(nc, *args)
    r = _run(nc, [arrays], core_ids=[0])
    return r.results[0]["out_0_dram"]
```

```python
BATCH, TOKENS, PICKED, DIM, HEADS = 16, 750, 375, 64, 8
TP = 125
NT = PICKED // TP
XT = TOKENS // TP
DH = DIM // HEADS
LAST_REL = 126
KEYS, KEY_DIM, TOPK = 64, 32, 16
CAND = sum(17 // (i + 1) for i in range(17))
SLOTS = 256
PER_HEAD = SLOTS // HEADS
COMBOS = 4
TIE = 1e-37
SPAN = 100.0
SHIFT = SPAN / 2
SWAP_HEADS = (3, 7)
BIG = 1e30


def table_slot(h):
    return 3 if h in SWAP_HEADS else h


def select_steps():
    s = [("G", ("score_mul",), 1.), ("V", ("score",), .45), ("A", ("eneg",), .2), ("T", ("rowbc",), .4, ("score",)),
         ("V", ("den",), .1, ("eneg",)), ("V", ("gate",), .1), ("G", ("xg",), 1.)]
    s += [("V", ("rank", t, part), .52, ("rowbc",)) for t in range(XT) for part in range(2)] + [("V", ("ranks",), .1)]
    s += [("G", ("hot", t), 1.25) for t in range(XT)]
    s += [("T", ("pick", it), 1.26, ("hot", XT - 1)) for it in range(NT)] + [("A", ("h1",), .4)]
    s += norm_steps(1)
    s += [("T", ("v",), .3), ("A", ("v",), .3), ("V", ("v_lo",), .3)]
    for g in range(2):
        s += [("T", ("q", g), .63, ("v_lo",) if g == 0 else ("o1", 0, 1)), ("T", ("k", g), .63), ("A", ("q", g), .4, ("q", g)), ("A", ("k", g), .4, ("k", g)),
              ("V", ("q", g), .52, ("q", g)), ("V", ("k", g), .52, ("k", g))]
        for n in range(13):
            if n < 12:
                s += [("T", ("qk", g, n), .5 if n % 3 == 2 else .72, *((("p", g, n - 1), ("pt_lo", g, n - 2)) if n else (("k", g),)))]
            if n:
                s += [("T", ("pt", g, n - 1), .33, ("p", g, n - 1), ("pt_lo", g, n - 2))]
            if n < 12:
                s += [("V", ("low", g, n), .46, ("qk", g, n))]
            if n:
                s += [("A", ("ptc", g, n - 1), .4, ("pt", g, n - 1))]
            if n < 12:
                s += [("A", ("p", g, n), .55, ("low", g, n))]
            if n:
                s += [("V", ("pt_lo", g, n - 1), .45, ("ptc", g, n - 1))]
        s += [("T", ("pv_end", g), .7, ("pt_lo", g, 11)), ("V", ("rz", g), .1)]
        s += [("V", (what, g, pair), .13) for what in ("o1_sum", "o1") for pair in range(2)]
    s += [("T", ("o1t",), .2), ("A", ("o1t",), .45), ("T", ("proj",), .33), ("V", ("h2",), .3)]
    s += norm_steps(2)
    return s


def norm_steps(i):
    return [("V", ("sum", i), .25), ("V", ("mean", i), .1), ("V", ("cen", i), .25), ("G", ("sq", i), .5),
            ("V", ("var", i), .25), ("V", ("veps", i), .1), ("G", ("rstd", i), .85), ("V", ("xn", i), .25),
            ("T", ("xnt", i), .3), ("A", ("xnt", i), .45)]


def topk_steps(g):
    s = [("T", ("qpk", g, p), .63) for p in range(2)] + [("A", ("qpk", g, p), .45, ("qpk", g, p)) for p in range(2)]
    for it in range(NT):
        s += [("T", ("sim", g, it), .86, ("qpk", g, 1)), ("A", ("sim", g, it), .6)]
    for it in range(NT):
        for what in ("max_a", "cut_a", "max_b", "cut_b"):
            s += [("V", (what, g, it, q), .135) + ((("sim", g, it),) if (what, q) == ("max_a", 0) else ()) for q in range(8)]
        s += [("V", ("max_c", g, it), .6)]
        s += [("G", ("cand", g, it, i), .2) for i in range(7)]
        for what in ("cmax_a", "ccut_a", "cmax_b", "ccut_b"):
            s += [("V", (what, g, it, q), .125) for q in range(4)]
        s += [("V", ("cmax_c", g, it), .3)]
        s += [("V", (what, g, it), .08) for what in ("mid", "floor", "thr", "off1", "off0")]
        s += [("G", ("shift", g, it), 1.), ("G", ("clamp", g, it), 1.5), ("A", ("hi", g, it), .6), ("G", ("lo", g, it), 1.1),
              ("A", ("keep_hi", g, it), .6)]
    s += [("V", ("diff", g), .3, ("off0", g, NT - 1)), ("A", ("wexp", g), .4), ("V", ("zk", g), .3), ("V", ("rzk", g), .1)]
    return s


def head_steps(h):
    s = [("T", ("kvt", h), .33), ("V", ("kvn", h), .48), ("T", ("knt", h), .35), ("A", ("knt", h), .45)]
    if h % 2 == 0:
        s += [("T", ("q2", h // 2), .63), ("A", ("q2", h // 2), .45)]
    for r in range(2):
        s += [("T", ("qk2", h, r), .75), ("V", ("low2", h, r), .5), ("A", ("p2", h, r), .65), ("T", ("pt2", h, r), .33),
              ("A", ("ptc2", h, r), .45)]
    s += [("T", ("pv2", h), 1.26), ("V", ("rz2", h), .1), ("V", ("o2", h), .3)]
    if h % 2:
        s += [("T", ("o2t", h // 2), .31), ("A", ("o2t", h // 2), .45), ("T", ("wo", h // 2), .33), ("V", ("acc", h // 2), .3)]
    return s


def head_parts(h):
    steps = head_steps(h)
    cut = [step for _, step, *_ in steps].index(("wo", h // 2) if h % 2 else ("pv2", h))
    return steps[:cut], steps[cut:]


FRONT = select_steps()
TOP = topk_steps(0) + [("G", ("keep_xn2",), .8)] + topk_steps(1)
BACK = [("G", ("keep_h2",), .8)] + [x for h in range(HEADS) for x in head_steps(h)]


def order(steps, engine):
    return [step[1] for step in steps if step[0] == engine]


SEQ = {thread: {e: order(steps, e) for e in "TVAG"} for thread, steps in (("front", FRONT), ("top", TOP), ("back", BACK))}
COUNT = {(t, e): {name: i + 1 for i, name in enumerate(SEQ[t][e])} for t in SEQ for e in "TVAG"}

LEAD = {"T": .8, "A": .7, "V": 1.2, "G": 0.}
ROOM = {"T": 1.6, "A": 1.2, "V": .8, "G": 2.}
DENSE = {"V": .46, "A": .46}
OVER = .3
HOP = .1


def place(timeline, load, thread, steps, first, last, batch, room=ROOM):
    end, at, previous = {}, dict.fromkeys("TVAG", first), None
    for engine, step, cost, *follows in steps:
        before = [end[name] for name in follows or [previous] if name in end]
        ready = max([0.] + [done + HOP * (by != engine) for by, _, done in before])
        slot = max([at[engine]] + [there for _, there, _ in before])
        start = sum(LEAD["T"] + side for side in load["T"][:slot])
        while True:
            begin = start + LEAD[engine] + load[engine][slot]
            slack = max(LEAD["T"] + load["T"][slot] - DENSE[engine], .3) if engine in "VA" else 9.
            late = ready - begin > (0. if engine in "TG" else slack - load[engine][slot] - cost)
            if slot >= last or not (ready > begin and late or load[engine][slot] and load[engine][slot] + cost > min(room[engine], slack + OVER)):
                break
            start += LEAD["T"] + load["T"][slot]
            slot += 1
        timeline[slot].append((thread, engine, step, batch))
        begin = max(begin, ready)
        load[engine][slot] = begin + cost - start - LEAD[engine]
        end[step] = engine, slot, begin + cost
        at[engine], previous = slot, step
    return max(at.values())


def timeline_of(kind):
    line = [[] for _ in range(SLOTS)]
    load = {e: [0.] * SLOTS for e in "TVAG"}
    for n in range(1, HEADS * COMBOS + (kind != "last")):
        for engine, slot, cost in (("G", -2, 1.4), ("T", 1, .17), ("A", 2, .4)):
            at = max(8 * (n - 1) + slot, 0)
            line[at].append(("combo", engine, ("combo", n % (HEADS * COMBOS)), n // (HEADS * COMBOS)))
            load[engine][at] += cost
    for h in range(HEADS):
        load["A"][PER_HEAD * h + 2] += .45
    for h in range(-2 if kind != "first" else 0, HEADS - 1):
        batch = 0 if h >= 0 else -1
        copied = PER_HEAD * (h + 1) + 2
        early, late = head_parts(h % HEADS)
        if h > -2:
            place(line, load, "back", early, copied + 1, copied + PER_HEAD - 3, batch)
        if h < HEADS - 2:
            place(line, load, "back", late, copied + PER_HEAD - 1, copied + PER_HEAD, batch)
        if h == 0:
            place(line, load, "back", BACK[:1], copied + 14, copied + 14, 0)
    group1 = [("G", ("keep_xn2",), .8)] + topk_steps(1)
    on_pe = max(i for i, step in enumerate(group1) if step[0] == "T") + 2
    free = place(line, load, "top", group1[:on_pe], 1, SLOTS - 1, 0) + 1
    picked = 0
    if kind != "last":
        picked = place(line, load, "front", select_steps(), free, SLOTS - 1, 1)
    ready = place(line, load, "top", group1[on_pe:], free, SLOTS // 2 - 11, 0)
    if kind != "last":
        place(line, load, "top", topk_steps(0), max(picked, ready) + 1, SLOTS - 11, 1, dict(ROOM, V=.55))
    return line


def build_kernel(nc, x, score_proj, qkv_w, qkv_b, proj_w, proj_b, rpb, wq_pk, pk_keys, wq, kv_table, wo, out):
    from contextlib import ExitStack
    import concourse.bass as bass
    from concourse import mybir

    F32, F16, BF16 = mybir.dt.float32, mybir.dt.float16, mybir.dt.bfloat16
    ALU, ACT, AX = mybir.AluOpType, mybir.ActivationFunctionType, mybir.AxisListType

    with ExitStack() as ctx:
        def sb(name, shape, dt=F32):
            return ctx.enter_context(nc.sbuf_tensor(name, shape, dt))

        def sem(name):
            return ctx.enter_context(nc.semaphore(name))

        table = sb("table", [128, 7, COMBOS, 8, 2 * DIM])
        sel = sb("sel", [128, 8, 128], F16)
        ident = sb("ident", [128, 128])
        ident16 = sb("ident16", [128, 128], F16)
        identb = sb("identb", [128, 128], BF16)
        flip = sb("flip", [127, 127])
        causal = sb("causal", [TP, TP], BF16)
        ties = sb("ties", [TP, 11 * TP], BF16)
        ranks_row = sb("ranks_row", [TP, PICKED])
        is_lo = sb("is_lo", [128, 2])
        w_score = sb("w_score", [TP, DIM])
        w_qk = sb("w_qk", [65, 2, 2, 4, 32])
        w_v = sb("w_v", [65, DIM])
        w_proj = sb("w_proj", [65, DIM])
        w_pk = sb("w_pk", [64, 512])
        w_q2 = sb("w_q2", [64, 512])
        w_o = sb("w_o", [128, 4, DIM])
        w_keys = sb("w_keys", [128, 4, 4, KEYS])
        hankel = sb("hankel", [TP, HEADS, 126])
        rel_tab = sb("rel_tab", [127, HEADS])

        xin = sb("xin", [TP, XT, DIM])
        xw = sb("xw", [TP, XT, DIM])
        xg = sb("xg", [TP, XT, DIM])
        junk = sb("junk", [TP, TOKENS], BF16)
        small = sb("small", [TP, 64])
        score, eneg, den, gate, rank = (small[:, 6 * i:6 * i + 6] for i in range(5))
        attn = sb("attn", [128, 2250])
        hot = attn[0:TP, :].rearrange("p (t r) -> p t r", t=XT)
        q_hi, qT, k_hi, kT = (attn[:, 0:750].bitcast(F16)[:, i * PICKED:(i + 1) * PICKED] for i in range(4))
        prob = attn[0:TP, 750:1500].rearrange("p (n r) -> p n r", n=2)
        probT = attn[0:TP, 1500:2250].bitcast(F16).rearrange("p (n s r) -> p n s r", n=2, s=2)
        h1 = sb("h1", [TP, NT, DIM])
        h2 = sb("h2", [TP, NT, DIM])
        cen = sb("cen", [TP, NT, DIM])
        sq = sb("sq", [TP, NT, DIM])
        xn = sb("xn", [TP, NT, DIM])
        stat = sb("stat", [TP, 5, NT])
        half = sb("half", [TP, NT])
        xnT = sb("xnT", [65, PICKED])
        vtok = sb("vtok", [TP, NT, HEADS, 2, DH], F16)
        low = sb("low", [TP, 2])
        zsum = sb("zsum", [TP, 24])
        rz = sb("rz", [TP, 24])
        o1 = sb("o1", [TP, NT, DIM])
        o1_whole = sb("o1_whole", [TP, 2, NT, 2, DH])
        xn2 = sb("xn2", [64, PICKED])
        xn2k = sb("xn2k", [64, PICKED])
        qpkT = sb("qpkT", [128, 2, PICKED])
        sims = sb("sims", [TP, 2, NT, 4, 2, KEYS])
        left = sb("left", [TP, 8, KEYS])
        top = sb("top", [TP, NT, 8, 17])
        cand = sb("cand", [TP, 4, CAND])
        best = sb("best", [TP, NT, 4, 17])
        cut = sb("cut", [TP, 3, NT * 4])
        wk = sb("wk", [TP, NT * 4, TOPK])
        wke = sb("wke", [TP, NT * 4, TOPK])
        zk = sb("zk", [TP, NT * 4])
        rzk = sb("rzk", [TP, 2, NT * 4])
        off = sb("off", [TP, NT * 4, 2])

        hi_tile = sb("hi_tile", [TP, 8 * KEYS], F16)
        quarter = sb("quarter", [TP, 2, NT, 2 * KEYS], F16)
        halves = sb("halves", [128, 2, PICKED], F16)
        weight = sb("weight", [128, 4, PICKED])
        kvT = sb("kvT", [128, PICKED])
        kv = sb("kv", [TP, NT, 128])
        knT = sb("knT", [128, PICKED])
        q2T = sb("q2T", [128, PICKED])
        prob2 = sb("prob2", [TP, 2, PICKED])
        prob2T = sb("prob2T", [TP, 2, NT, TP])
        low2 = sb("low2", [TP, NT])
        z2 = sb("z2", [TP, NT])
        rz2 = sb("rz2", [TP, NT])
        o2 = sb("o2", [TP, NT, 128])
        o2T = knT
        result = sb("result", [TP, NT, DIM])
        shift = sb("shift", [128, 1])

        ext = kvT[0:HEADS, 0:250]

        banks = [ctx.enter_context(nc.psum_tensor(f"bank{i}", [128, 512], F32)) for i in range(8)]
        s_bank, kv_bank, fa, fb, combo_bank, back_bank = banks[0:3], banks[3], banks[4], banks[5], banks[6], banks[7]
        fa2 = [fa, fb]

        def score_bank(u):
            return fb if u == SLOTS - 1 else s_bank[u % 3]

        done = {(t, e): sem(f"{t}_{e}") for t in ("front", "top", "back") for e in "TVAG"}
        combo_done = {e: sem(f"combo_{e}") for e in "GTA"}
        pair_scores, pair_exps, pair_weights, pair_sums = sem("pair_scores"), sem("pair_exps"), sem("pair_weights"), sem("pair_sums")
        kv_copied = sem("kv_copied")
        x_loaded, stored = sem("x_loaded"), sem("stored")
        weights_loaded, bias_loaded, hankel_loaded, swap_loaded = sem("weights_loaded"), sem("bias_loaded"), sem("hankel_loaded"), sem("swap_loaded")
        table_loaded = [sem(f"table_loaded{h}") for h in range(HEADS)]
        const_pool, zeroed, const_dve, const_pe, const_act = sem("const_pool"), sem("zeroed"), sem("const_dve"), sem("const_pe"), sem("const_act")
        const_dve0 = sem("const_dve0")
        heads_scaled, split_ready = sem("heads_scaled"), sem("split_ready")
        CONSTS = 23

        def reached(thread, engine, *step, b):
            return done[thread, engine], b * len(SEQ[thread][engine]) + COUNT[thread, engine][step]

        def wait(eng, s, value):
            if isinstance(value, int) and value <= 0:
                return
            eng.wait_ge(s, value)

        def wait_alone(eng, s, value):
            if not isinstance(value, int):
                value = eng.to_reg(value)
                eng.wait_ge(const_pool, CONSTS)
            wait(eng, s, value)

        def after_alone(eng, thread, engine, *step, b):
            wait_alone(eng, *reached(thread, engine, *step, b=b))

        def after(eng, thread, engine, *step, b):
            wait(eng, *reached(thread, engine, *step, b=b))

        def load_table(eng, h, s):
            rows = kv_table[h * 4096:(h + 1) * 4096, :].rearrange("(g b ah a t) c -> a g b ah (t c)", g=2, b=32, ah=2, a=4, t=8)
            for a in range(4):
                for g in range(2):
                    eng.dma_start(table[32 * a:32 * a + 32, table_slot(h), 2 * g:2 * g + 2].rearrange("p ah t c -> p ah (t c)"),
                                  rows[a, g]).then_inc(s, 16)

        block = ctx.enter_context(nc.Block())
        TL = {kind: timeline_of(kind) for kind in ("first", "mid", "last")}
        N_TABLE = 8 * 16
        N_WEIGHTS = 16 * 18
        first_batch, last_batch = 0, BATCH - 1

        def side(kind, slot, engine, steps, b):
            for thread, e, name, ahead in TL[kind][slot]:
                if e == engine:
                    steps[thread, name[0]](b + ahead, *name[1:])

        def prologue(engine, steps):
            for thread, part in (("front", select_steps()), ("top", topk_steps(0))):
                for name in order(part, engine):
                    steps[thread, name[0]](0, *name[1:])
            if engine in "GTA":
                steps["combo", "combo"](0, 0)

        def run(eng, engine, steps, dense, flush, start=None):
            prologue(engine, steps)
            dense_batch(engine, steps, dense, "first", first_batch)
            with eng.Fori(1, last_batch) as b:
                dense_batch(engine, steps, dense, "mid", b)
            dense_batch(engine, steps, dense, "last", last_batch)
            flush(last_batch)
            for name in order(head_parts(HEADS - 2)[1] + head_steps(HEADS - 1), engine):
                steps["back", name[0]](last_batch, *name[1:])

        def dense_batch(engine, steps, dense, kind, b):
            for u in range(SLOTS):
                dense(b, u)
                side(kind, u, engine, steps, b)

        @block.sync
        def _(sp):
            def load_x(b):
                if not isinstance(b, int) or b > 0:
                    after(sp, "front", "G", "xg", b=b - 1)
                sp.dma_start(xin[:, :, :], x[b].rearrange("(t p) f -> p t f", p=TP)).then_inc(x_loaded, 16)

            def store(b):
                after(sp, "back", "V", "acc", 3, b=b)
                sp.dma_start(out[b].rearrange("(t p) f -> p t f", p=TP), result[:, :, :]).then_inc(stored, 16)

            load_x(0)
            s = weights_loaded
            sp.dma_start(w_score[:, :], score_proj.rearrange("f o -> (o f)").partition_broadcast(TP)).then_inc(s, 16)
            sp.dma_start(rel_tab[:, :], rpb).then_inc(s, 16)
            sp.wait_ge(zeroed, 2)
            qkv = qkv_w.rearrange("c (k g h d) -> c k g h d", k=3, g=2, h=4)
            qkvb = qkv_b.rearrange("(o k g h d) -> o k g h d", o=1, k=3, g=2, h=4)
            for k in range(2):
                for g in range(2):
                    sp.dma_start(w_qk[0:64, k, g, :, 0:DH], qkv[:, k, g]).then_inc(s, 16)
                    sp.dma_start(w_qk[64:65, k, g, :, 0:DH], qkvb[:, k, g]).then_inc(s, 16)
            sp.dma_start(w_v[0:64, :], qkv_w[:, 128:192]).then_inc(s, 16)
            sp.dma_start(w_v[64:65, :], qkv_b.rearrange("(o n) -> o n", o=1)[:, 128:192]).then_inc(s, 16)
            sp.dma_start(w_proj[0:64, :], proj_w).then_inc(s, 16)
            sp.dma_start(w_proj[64:65, :], proj_b.rearrange("(o n) -> o n", o=1)).then_inc(s, 16)
            sp.dma_start(w_pk[:, :], wq_pk).then_inc(s, 16)
            sp.dma_start(w_q2[:, :], wq).then_inc(s, 16)
            sp.dma_start(w_o[:, :, :], wo.rearrange("(j p) n -> p j n", p=128)).then_inc(s, 16)
            sp.dma_start(attn[0:64, 0:512].rearrange("p (q n) -> p q n", q=2), pk_keys.rearrange("q k h d -> k q (h d)")).then_inc(s, 16)
            sp.wait_ge(const_dve, 1)
            for h in range(HEADS):
                row = ext[h:h + 1, :]
                sp.dma_start(hankel[:, h, :], bass.AP(row.tensor, row.offset, [row.ap[0], [1, TP], [1, 126]])).then_inc(hankel_loaded, 16)
            for h in range(HEADS - 1):
                load_table(sp, h, table_loaded[h])

            def batch(kind, b):
                if kind != "last":
                    load_x(b + 1)
                if kind != "first":
                    store(b - 1)
                sp.wait_ge(pair_sums, b * SLOTS + 4 * PER_HEAD)
                load_table(sp, 7, swap_loaded)
                if kind != "last":
                    sp.wait_ge(pair_sums, b * SLOTS + SLOTS)
                    load_table(sp, 3, swap_loaded)

            batch("first", 0)
            with sp.Fori(1, last_batch) as b:
                batch("mid", b)
            batch("last", last_batch)
            store(last_batch)
            sp.wait_ge(stored, 16 * BATCH)

        @block.gpsimd
        def _(pool):
            g = nc.gpsimd
            g.memset(w_qk[:, :, :, :, :], 0.0).then_inc(zeroed, 1)
            g.memset(w_keys[:, :, :, :], 0.0).then_inc(zeroed, 1)
            n = [0]

            def made(ins):
                n[0] += 1
                ins.then_inc(const_pool, 1)
                pool.wait_ge(const_pool, n[0])

            for m in (ident, ident16, identb, flip, causal, sel):
                made(g.memset(m[:], 0.0))
            made(g.memset(ties[:, 0:6 * TP], -TIE))
            made(g.memset(ties[:, 6 * TP:], 0.0))
            made(g.memset(half[:, :], -0.5))
            made(g.memset(shift[:, :], -SHIFT))
            made(g.memset(xnT[64:65, :], 1.0))
            made(g.memset(ext[:, 0:123], 0.0))
            for m in (ident, ident16, identb):
                made(g.affine_select(out=m[:, :], in_=m[:, :], compare_op=ALU.not_equal, fill=1.0, base=0,
                                     pattern=[[-1, 128]], channel_multiplier=1))
            made(g.affine_select(out=flip[:, :], in_=flip[:, :], compare_op=ALU.not_equal, fill=1.0, base=-126,
                                 pattern=[[1, 127]], channel_multiplier=1))
            made(g.affine_select(out=causal[:, :], in_=causal[:, :], compare_op=ALU.is_ge, fill=BIG, base=0,
                                 pattern=[[-1, TP]], channel_multiplier=1))
            tri = ties[:, 5 * TP:6 * TP]
            made(g.affine_select(out=tri, in_=tri, compare_op=ALU.is_gt, fill=0.0, base=0,
                                 pattern=[[-1, TP]], channel_multiplier=1))
            for r in (0, 32):
                v = sel[r:r + 32].rearrange("p t (a b) -> p t a b", a=4)
                made(g.affine_select(out=v, in_=v, compare_op=ALU.not_equal, fill=1.0, base=0,
                                     pattern=[[0, 8], [0, 4], [-1, 32]], channel_multiplier=1))
            for r in (64, 96):
                v = sel[r:r + 32].rearrange("p t (a b) -> p t a b", a=4)
                made(g.affine_select(out=v, in_=v, compare_op=ALU.not_equal, fill=1.0, base=0,
                                     pattern=[[-1, 8], [-8, 4], [0, 32]], channel_multiplier=1))
            made(g.iota(ranks_row[:, :], [[1, PICKED]], base=0, channel_multiplier=0, allow_small_or_imprecise_dtypes=True))

            fG, tG = done["front", "G"], done["top", "G"]

            def score_mul(b):
                if isinstance(b, int) and b == 0:
                    pool.wait_ge(weights_loaded, N_WEIGHTS)
                pool.wait_ge(x_loaded, b * 16 + 16)
                g.tensor_tensor(xw[:, :, :], xin[:, :, :], w_score[:, :].unsqueeze(1).broadcast_to([TP, XT, DIM]), ALU.mult).then_inc(fG, 1)

            def xg_(b):
                after(pool, "front", "V", "gate", b=b)
                after(pool, "front", "T", "pick", NT - 1, b=b - 1)
                g.tensor_tensor(xg[:, :, :], xin[:, :, :], gate.unsqueeze(2).broadcast_to([TP, XT, DIM]), ALU.mult).then_inc(fG, 1)

            def hot_(b, t):
                after_alone(pool, "front", "V", "ranks", b=b)
                if t == 0:
                    after_alone(pool, "front", "T", "pv_end", 1, b=b - 1)
                g.tensor_scalar(hot[:, t, :], ranks_row[:, :], rank[:, t:t + 1], None, ALU.is_equal).then_inc(fG, 1)

            def sq_(b, i):
                after(pool, "front", "V", "cen", i, b=b)
                g.tensor_tensor(sq[:, :, :], cen[:, :, :], cen[:, :, :], ALU.mult).then_inc(fG, 1)

            CAND_ROWS = [(0, 1, 17), (1, 1, 8), (2, 1, 5), (3, 1, 4), (4, 1, 3), (5, 3, 2), (8, 9, 1)]

            def cand_(b, gr, it, r):
                if r == 0:
                    after(pool, "top", "V", "max_c", gr, it, b=b)
                i0, ni, nj = CAND_ROWS[r]
                at = sum(a * c for _, a, c in CAND_ROWS[:r])
                t4 = top[:, it].rearrange("p (h q) k -> p h q k", q=2)
                o = cand[:, :, at:at + ni * nj].rearrange("p h (i j) -> p h i j", i=ni)
                g.tensor_tensor(o, t4[:, :, 1, i0:i0 + ni].unsqueeze(3).broadcast_to([TP, 4, ni, nj]),
                                t4[:, :, 0, 0:nj].unsqueeze(2).broadcast_to([TP, 4, ni, nj]), ALU.add).then_inc(tG, 1)

            def rstd(b, i):
                after(pool, "front", "V", "veps", i, b=b)
                g.tensor_tensor(stat[:, 4, :], stat[:, 3, :], half[:, :], ALU.pow).then_inc(done["front", "G"], 1)

            def shift_scores(b, gr, it):
                after(pool, "top", "V", "off0", gr, it, b=b)
                v = sims[:, gr, it].rearrange("p h q k -> p (h q) k")
                o = off[:, 4 * it:4 * it + 4, :].rearrange("p h q -> p (h q)").unsqueeze(2).broadcast_to([TP, 8, KEYS])
                g.tensor_tensor(v, v, o, ALU.add).then_inc(done["top", "G"], 1)

            def clamp(b, gr, it):
                after_alone(pool, "top", "G", "shift", gr, it, b=b)
                v = sims[:, gr, it].rearrange("p h q k -> p (h q k)")
                g.tensor_scalar(v, v, -60000.0, None, ALU.max).then_inc(done["top", "G"], 1)

            def tile_scores(gr, it):
                return sims[:, gr, it].rearrange("p h q k -> p (h q k)")

            def lo(b, gr, it):
                after(pool, "top", "A", "hi", gr, it, b=b)
                g.tensor_tensor(tile_scores(gr, it).bitcast(F16).rearrange("p (n s) -> p n s", s=2)[:, :, 1], tile_scores(gr, it), hi_tile[:, :],
                                ALU.subtract).then_inc(tG, 1)

            def combo(b, n):
                h, c = n // COMBOS, n % COMBOS
                gk, ah = c // 2, c % 2
                after(pool, "top", "A", "keep_hi", h // 4, NT - 1, b=b)
                wait_alone(pool, combo_done["T"], b * HEADS * COMBOS + n - 1)
                cols = sims[:, h // 4, :, h % 4].rearrange("p t q k -> p t (q k)").bitcast(F16).rearrange("p t (q g k s) -> p t (q g) s k", q=2, g=2, s=2)
                cols = cols[:, :, gk:2 + ah + 1:2 + ah - gk, :, :]
                g.tensor_copy(quarter[:, n % 2].rearrange("p t (q s k) -> p t q s k", q=2, s=2), cols).then_inc(combo_done["G"], 1)

            def keep_xn2(b):
                after(pool, "front", "A", "xnt", 2, b=b)
                after(pool, "top", "T", "qpk", 1, 1, b=b - 1)
                after_alone(pool, "back", "T", "q2", 3, b=b - 1)
                g.tensor_copy(xn2k[:, :], xn2[:, :]).then_inc(done["top", "G"], 1)

            def keep_h2(b):
                after(pool, "front", "V", "h2", b=b)
                wait_alone(pool, stored, b * 16)
                g.tensor_copy(result[:, :, :], h2[:, :, :]).then_inc(done["back", "G"], 1)

            run(pool, "G", {("front", "score_mul"): score_mul, ("front", "xg"): xg_, ("front", "hot"): hot_, ("front", "sq"): sq_, ("top", "cand"): cand_,
                            ("front", "rstd"): rstd, ("top", "shift"): shift_scores, ("top", "clamp"): clamp, ("top", "lo"): lo,
                            ("combo", "combo"): combo, ("top", "keep_xn2"): keep_xn2, ("back", "keep_h2"): keep_h2},
                lambda b, u: None, lambda b: None)

        @block.tensor
        def _(pe):
            mm, tr = nc.tensor.matmul, nc.tensor.transpose
            fT, tT, bT = (done[thread, "T"] for thread in ("front", "top", "back"))

            pe.wait_ge(weights_loaded, N_WEIGHTS)
            pe.wait_ge(const_pool, CONSTS)
            mm(fa[0:HEADS, 0:127], rel_tab[:, :], flip[:, :], start=True, stop=True).then_inc(const_pe, 1)
            for q in range(2):
                for gr in range(2):
                    last = tr(fb[:, (q * 2 + gr) * 64:(q * 2 + gr) * 64 + 64], attn[0:64, q * 256 + gr * 128:q * 256 + gr * 128 + 128], ident[0:64, 0:64])
            last.then_inc(const_pe, 1)
            pe.wait_ge(const_dve, 2)
            pe.wait_ge(const_act, 1)
            pe.wait_ge(hankel_loaded, 16 * HEADS)
            pe.wait_ge(heads_scaled, 6)

            def rowbc(b):
                after(pe, "front", "V", "score", b=b)
                after(pe, "top", "A", "sim", 1, 2, b=b - 1)
                for t in range(XT):
                    last = tr(fa2[t // 3][0:TP, t % 3 * TP:t % 3 * TP + TP], score[:, t:t + 1].broadcast_to([TP, TP]), ident[0:TP, 0:TP])
                last.then_inc(fT, 1)

            def pick(b, it):
                if it == 0:
                    after(pe, "front", "G", "hot", XT - 1, b=b)
                for t in range(XT):
                    last = mm(fa[0:TP, it * DIM:it * DIM + DIM], hot[:, t, it * TP:it * TP + TP], xg[:, t, :], start=(t == 0), stop=(t == XT - 1))
                last.then_inc(fT, 1)

            def xnt(b, i):
                after_alone(pe, "front", "V", "xn", i, b=b)
                for it in range(NT):
                    last = tr(fb[0:64, it * TP:it * TP + TP], xn[:, it, :], ident[0:TP, 0:TP])
                last.then_inc(fT, 1)

            def v(b):
                after(pe, "front", "A", "xnt", 1, b=b)
                for it in range(NT):
                    last = mm(fa[0:TP, it * DIM:it * DIM + DIM], xnT[:, it * TP:it * TP + TP], w_v[:, :], start=True, stop=True)
                last.then_inc(fT, 1)

            def qk_proj(which, bank):
                def f(b, gr):
                    if which == 0:
                        if gr == 0:
                            after(pe, "front", "V", "v_lo", b=b)
                        else:
                            after(pe, "front", "V", "o1_sum", 0, 1, b=b)
                    elif gr == 1:
                        after(pe, "front", "V", "pt_lo", 0, 11, b=b)
                    mm(bank[:, 0:PICKED], w_qk[:, which, gr].rearrange("p h d -> p (h d)"), xnT[:, :], start=True, stop=True).then_inc(fT, 1)
                return f

            def pv(gr, n):
                hh, it = n // NT, n % NT
                at = 384 + it * 32 + hh % 2 * 2 * DH
                o = fa2[hh // 2][0:TP, at:at + 2 * DH]
                for jt in range(NT):
                    mm(o, probT[:, n % 2, 0, jt * TP:jt * TP + TP], vtok[:, jt, gr * 4 + hh].rearrange("p s d -> p (s d)"), start=(jt == 0), stop=(jt == NT - 1))
                for jt in range(NT):
                    last = mm(o[:, 0:DH], probT[:, n % 2, 1, jt * TP:jt * TP + TP], vtok[:, jt, gr * 4 + hh, 0, :], start=False, stop=True, skip_group_check=True)
                return last

            def qk(b, gr, n):
                hh, it = n // NT, n % NT
                if n == 0:
                    after(pe, "front", "V", "k", gr, b=b)
                else:
                    after(pe, "front", "A", "p", gr, n - 1, b=b)
                if n >= 2:
                    after(pe, "front", "V", "pt_lo", gr, n - 2, b=b)
                    pv(gr, n - 2)
                k0 = 32 * hh
                last = mm(fa[0:TP, 0:PICKED], qT[k0:k0 + 3 * DH, it * TP:it * TP + TP], kT[k0:k0 + 3 * DH, :], start=True, stop=True)
                if it == 0:
                    last = mm(fa[0:TP, 249:375], flip[0:TP, 2:127], hankel[:, gr * 4 + hh, :], start=False, stop=True, skip_group_check=True)
                elif it == 1:
                    last = mm(fa[0:TP, 374:375], flip[0:TP, 2:127], hankel[:, gr * 4 + hh, 0:1], start=False, stop=True, skip_group_check=True)
                last.then_inc(fT, 1)

            def pt(b, gr, n):
                after(pe, "front", "A", "p", gr, n, b=b)
                if n == 0:
                    after(pe, "front", "V", "k", gr, b=b)
                else:
                    after(pe, "front", "V", "pt_lo", gr, n - 1, b=b)
                for jt in range(NT):
                    last = tr(fb[0:TP, jt * TP:jt * TP + TP], prob[:, n % 2, jt * TP:jt * TP + TP], ident[0:TP, 0:TP])
                last.then_inc(fT, 1)

            def pv_end(b, gr):
                after(pe, "front", "V", "pt_lo", gr, 11, b=b)
                pv(gr, 10)
                pv(gr, 11).then_inc(fT, 1)

            def o1t(b):
                after_alone(pe, "front", "V", "o1", 1, 1, b=b)
                for it in range(NT):
                    last = tr(fb[0:64, it * TP:it * TP + TP], o1[:, it, :], ident[0:TP, 0:TP])
                last.then_inc(fT, 1)

            def proj(b):
                after(pe, "front", "A", "o1t", b=b)
                for it in range(NT):
                    last = mm(fa[0:TP, it * DIM:it * DIM + DIM], xnT[:, it * TP:it * TP + TP], w_proj[:, :], start=True, stop=True)
                last.then_inc(fT, 1)

            def qpk(b, gr, p):
                if gr == 0:
                    after(pe, "front", "A", "xnt", 2, b=b)
                else:
                    after(pe, "top", "G", "keep_xn2", b=b)
                    if p == 0:
                        after(pe, "top", "A", "sim", 0, 2, b=b)
                    else:
                        wait(pe, pair_weights, b * SLOTS)
                src = (xn2, xn2k)[gr]
                col = p * 256 + gr * 128
                mm(fa2[p][:, 0:PICKED], w_pk[:, col:col + 128], src[:, :], start=True, stop=True).then_inc(tT, 1)

            def sim(b, gr, it):
                after(pe, "top", "A", "qpk", gr, 1, b=b)
                if it == 2:
                    after(pe, "top", "A", "sim", gr, 0, b=b)
                bank = fa2[it % 2]
                for q in range(2):
                    p = 1 - q
                    last = mm(bank[0:TP, q * 256:q * 256 + 256], qpkT[:, p, it * TP:it * TP + TP],
                              w_keys[:, p * 2 + gr].rearrange("p h k -> p (h k)"), start=True, stop=True)
                last.then_inc(tT, 1)

            def combo(b, n):
                wait(pe, combo_done["G"], b * HEADS * COMBOS + n + 1)
                wait(pe, combo_done["A"], b * HEADS * COMBOS + n)
                for it in range(NT):
                    last = mm(combo_bank[:, it * TP:it * TP + TP], quarter[:, n % 2, it, :], ident16[0:TP, 0:TP], start=True, stop=True)
                last.then_inc(combo_done["T"], 1)

            def out_mm(b, u):
                h, tile = u // PER_HEAD, u % PER_HEAD
                c, a8 = tile // 8, tile % 8
                if tile == 0:
                    wait(pe, kv_copied, b * HEADS + h)
                    if h == 3:
                        if isinstance(b, int) and b == 0:
                            pe.wait_ge(table_loaded[3], N_TABLE)
                        else:
                            pe.wait_ge(swap_loaded, b * 2 * N_TABLE)
                    elif h == 7:
                        pe.wait_ge(swap_loaded, b * 2 * N_TABLE + N_TABLE)
                    elif isinstance(b, int) and b == 0:
                        pe.wait_ge(table_loaded[h], N_TABLE)
                pe.wait_ge(pair_weights, b * SLOTS + u + 1)
                t = table[:, table_slot(h), c, a8, :]
                mm(kv_bank[:, 0:PICKED], t, weight[:, u % 4, :], start=(tile == 0), stop=(tile == PER_HEAD - 1)).then_inc(pair_sums, 1)

            def dense(b, u):
                if u % 8 == 0:
                    pe.wait_ge(combo_done["A"], b * HEADS * COMBOS + u // 8 + 1)
                if u == SLOTS - 1:
                    if isinstance(b, int) and b == last_batch:
                        after(pe, "top", "A", "sim", 1, NT - 1, b=b)
                    else:
                        after(pe, "top", "A", "sim", 0, NT - 1, b=b + 1)
                mm(score_bank(u)[:, 0:PICKED], sel[:, u % 8, :], halves[:, u // 8 % 2, :], start=True, stop=True).then_inc(pair_scores, 1)
                if u >= 2:
                    out_mm(b, u - 2)
                elif not isinstance(b, int) or b > 0:
                    out_mm(b - 1, SLOTS - 2 + u)

            def flush(b):
                out_mm(b, SLOTS - 2)
                out_mm(b, SLOTS - 1)

            def kvt(b, h):
                wait(pe, kv_copied, b * HEADS + h + 1)
                if h % 2 == 0 and h > 0:
                    after(pe, "back", "V", "acc", h // 2 - 1, b=b)
                elif h == 0:
                    after(pe, "back", "V", "acc", 3, b=b - 1)
                else:
                    after(pe, "back", "V", "o2", h - 1, b=b)
                for it in range(NT):
                    last = tr(back_bank[0:TP, it * 128:it * 128 + 128], kvT[:, it * TP:it * TP + TP], ident[:, :])
                last.then_inc(bT, 1)

            def knt(b, h):
                after(pe, "back", "V", "kvn", h, b=b)
                for it in range(NT):
                    last = tr(back_bank[:, it * TP:it * TP + TP], kv[:, it, :], ident[0:TP, 0:TP])
                last.then_inc(bT, 1)

            def q2(b, j):
                after(pe, "back", "A", "knt", 2 * j, b=b)
                after(pe, "top", "G", "keep_xn2", b=b)
                mm(back_bank[:, 0:PICKED], w_q2[:, j * 128:j * 128 + 128], xn2k[:, :], start=True, stop=True).then_inc(bT, 1)

            def qk2(b, h, r):
                if r == 0:
                    if h % 2 == 0:
                        after(pe, "back", "A", "q2", h // 2, b=b)
                    else:
                        after(pe, "back", "A", "knt", h, b=b)
                else:
                    after(pe, "back", "A", "ptc2", h, 0, b=b)
                rows = slice(64 * (h % 2), 64 * (h % 2) + 64)
                for it, at in (((0, 0), (1, TP)) if r == 0 else ((2, 0),)):
                    n = TP * (it + 1)
                    mm(back_bank[0:TP, at:at + n], q2T[rows, it * TP:it * TP + TP], knT[rows, 0:n], start=True, stop=True)
                    last = mm(back_bank[0:TP, at + n - TP:at + n], identb[0:TP, 0:TP], causal[:, :], start=False, stop=True, skip_group_check=True)
                last.then_inc(bT, 1)

            def pt2(b, h, r):
                after(pe, "back", "A", "p2", h, r, b=b)
                for jt in range(NT):
                    last = tr(back_bank[0:TP, jt * TP:jt * TP + TP], prob2[:, r, jt * TP:jt * TP + TP], ident[0:TP, 0:TP])
                last.then_inc(bT, 1)

            def pv2(b, h):
                after(pe, "back", "A", "ptc2", h, 1, b=b)
                v0 = DIM * (1 - h % 2)
                for it in range(NT):
                    for jt in range(it + 1):
                        p = prob2T[:, 1, jt, :] if it == 2 else prob2T[:, 0, it + jt, :]
                        last = mm(back_bank[0:TP, it * DIM:it * DIM + DIM], p, kv[:, jt, v0:v0 + DIM], start=(jt == 0), stop=(jt == it))
                last.then_inc(bT, 1)

            def o2t(b, j):
                after(pe, "back", "V", "o2", 2 * j + 1, b=b)
                for it in range(NT):
                    last = tr(back_bank[:, it * TP:it * TP + TP], o2[:, it, :], ident[0:TP, 0:TP])
                last.then_inc(bT, 1)

            def wo_mm(b, j):
                after(pe, "back", "A", "o2t", j, b=b)
                for it in range(NT):
                    last = mm(back_bank[0:TP, it * DIM:it * DIM + DIM], o2T[:, it * TP:it * TP + TP], w_o[:, j, :], start=True, stop=True)
                last.then_inc(bT, 1)

            run(pe, "T", {("front", "rowbc"): rowbc, ("front", "pick"): pick, ("front", "xnt"): xnt, ("front", "v"): v,
                          ("front", "q"): qk_proj(0, fa), ("front", "k"): qk_proj(1, fb), ("front", "qk"): qk, ("front", "pt"): pt,
                          ("front", "pv_end"): pv_end, ("front", "o1t"): o1t, ("front", "proj"): proj, ("top", "qpk"): qpk,
                          ("top", "sim"): sim, ("combo", "combo"): combo, ("back", "kvt"): kvt, ("back", "knt"): knt,
                          ("back", "q2"): q2, ("back", "qk2"): qk2, ("back", "pt2"): pt2, ("back", "pv2"): pv2,
                          ("back", "o2t"): o2t, ("back", "wo"): wo_mm}, dense, flush)

        @block.scalar
        def _(act):
            fA, tA, bA = (done[thread, "A"] for thread in ("front", "top", "back"))

            def copy(out, in_, s, scale=1.0):
                nc.scalar.activation(out, in_, ACT.Copy, scale=scale).then_inc(s, 1)

            act.wait_ge(const_pe, 2)
            act.wait_ge(zeroed, 2)
            for q in range(2):
                for gr in range(2):
                    for hh in range(4):
                        at = (q * 2 + gr) * 64
                        last = nc.scalar.activation(w_keys[32 * hh:32 * hh + 32, q * 2 + gr, hh, :], fb[32 * hh:32 * hh + 32, at:at + 64], ACT.Copy)
            last.then_inc(const_act, 1)
            act.wait_ge(const_pool, CONSTS)

            def eneg(b):
                after(act, "front", "V", "score", b=b)
                after(act, "front", "V", "den", b=b - 1)
                nc.scalar.activation(eneg_, score, ACT.Exp, scale=-1.0).then_inc(fA, 1)

            def h1_(b):
                after(act, "front", "T", "pick", NT - 1, b=b)
                after(act, "front", "V", "h2", b=b - 1)
                copy(h1[:, :, :], fa[0:TP, 0:NT * DIM].rearrange("p (t f) -> p t f", t=NT), fA)

            def xnt(b, i):
                after(act, "front", "T", "xnt", i, b=b)
                if i == 1:
                    after(act, "front", "T", "proj", b=b - 1)
                else:
                    after(act, "top", "T", "qpk", 0, 1, b=b - 1)
                    after(act, "top", "G", "keep_xn2", b=b - 1)
                copy((xnT[0:64, :], xn2[:, :])[i - 1], fb[0:64, 0:PICKED], fA)

            def v(b):
                after(act, "front", "T", "v", b=b)
                after(act, "front", "T", "pv_end", 1, b=b - 1)
                copy(vtok[:, :, :, 0, :].rearrange("p t h d -> p (t h) d"), fa[0:TP, 0:NT * DIM].rearrange("p (n d) -> p n d", d=DH), fA)

            def q(b, gr):
                after(act, "front", "T", "q", gr, b=b)
                copy(q_hi, fa[:, 0:PICKED], fA)

            def k(b, gr):
                after(act, "front", "T", "k", gr, b=b)
                copy(k_hi, fb[:, 0:PICKED], fA)

            def p(b, gr, n):
                after(act, "front", "V", "low", gr, n, b=b)
                if n >= 2:
                    after(act, "front", "T", "pt", gr, n - 2, b=b)
                hh, it = n // NT, n % NT
                z = zsum[:, gr * 12 + it * 4 + hh:gr * 12 + it * 4 + hh + 1]
                nc.scalar.activation(prob[:, n % 2, :], fa[0:TP, 0:PICKED], ACT.Exp, bias=low[:, n % 2:n % 2 + 1], scale=-1.0, accum_out=z).then_inc(fA, 1)

            def ptc(b, gr, n):
                after(act, "front", "T", "pt", gr, n, b=b)
                if n >= 2:
                    after(act, "front", "T", "qk", gr, n, b=b)
                copy(probT[:, n % 2, 0, :], fb[0:TP, 0:PICKED], fA)

            def o1t(b):
                after(act, "front", "T", "o1t", b=b)
                copy(xnT[0:64, :], fb[0:64, 0:PICKED], fA)

            def qpk(b, gr, p):
                after(act, "top", "T", "qpk", gr, p, b=b)
                copy(qpkT[:, p, :], fa2[p][:, 0:PICKED], tA)

            def sim(b, gr, it):
                after(act, "top", "T", "sim", gr, it, b=b)
                if it == 0:
                    wait(act, combo_done["G"], (b - 1) * HEADS * COMBOS + 16 * (gr + 1))
                copy(sims[:, gr, it].rearrange("p h q k -> p q h k"), fa2[it % 2][0:TP, :].rearrange("p (q h k) -> p q h k", q=2, h=4), tA)

            def hi(b, gr, it):
                after(act, "top", "G", "clamp", gr, it, b=b)
                if it:
                    after(act, "top", "A", "keep_hi", gr, it - 1, b=b)
                else:
                    after(act, "top", "A", "keep_hi", 1 - gr, NT - 1, b=b - (gr == 0))
                copy(hi_tile[:, :], sims[:, gr, it].rearrange("p h q k -> p (h q k)"), tA)

            def keep_hi(b, gr, it):
                after(act, "top", "G", "lo", gr, it, b=b)
                words = sims[:, gr, it].rearrange("p h q k -> p (h q k)").bitcast(F16).rearrange("p (n s) -> p n s", s=2)
                copy(words[:, :, 0], hi_tile[:, :], tA)

            def wexp(b, gr):
                after(act, "top", "V", "diff", gr, b=b)
                nc.scalar.activation(wke[:, :, :], wk[:, :, :], ACT.Exp, bias=shift[0:TP, :]).then_inc(tA, 1)

            def combo(b, n):
                wait(act, combo_done["T"], b * HEADS * COMBOS + n + 1)
                wait(act, pair_scores, b * SLOTS + 8 * (n - 1))
                copy(halves[:, n % 2, :], combo_bank[:, 0:PICKED], combo_done["A"])

            def dense(b, u):
                if u % PER_HEAD == 2 and u > 2:
                    kv_copy(b, u // PER_HEAD - 1)
                elif u == 2 and (not isinstance(b, int) or b > 0):
                    kv_copy(b - 1, HEADS - 1)
                act.wait_ge(pair_scores, b * SLOTS + u + 1)
                nc.scalar.activation(weight[:, u % 4, :], score_bank(u)[:, 0:PICKED], ACT.Exp, bias=shift[:, :]).then_inc(pair_exps, 1)

            def kv_copy(b, h):
                act.wait_ge(pair_sums, b * SLOTS + (h + 1) * PER_HEAD)
                if h == 0:
                    after(act, "back", "T", "kvt", HEADS - 1, b=b - 1)
                else:
                    after(act, "back", "T", "kvt", h - 1, b=b)
                copy(kvT[:, :], kv_bank[:, 0:PICKED], kv_copied)

            def flush(b):
                kv_copy(b, HEADS - 1)

            def knt(b, h):
                after(act, "back", "T", "knt", h, b=b)
                r = slice(64 * (h % 2), 64 * (h % 2) + 64)
                copy(knT[r, :], back_bank[r, 0:PICKED], bA)

            def q2(b, j):
                after(act, "back", "T", "q2", j, b=b)
                copy(q2T[:, :], back_bank[:, 0:PICKED], bA, scale=-DIM ** -0.5)

            def p2(b, h, r):
                after(act, "back", "V", "low2", h, r, b=b)
                for it, at, n in (((0, 0, TP), (1, TP, 2 * TP)) if r == 0 else ((2, 0, 3 * TP),)):
                    last = nc.scalar.activation(prob2[:, r, at:at + n], back_bank[0:TP, at:at + n], ACT.Exp, bias=low2[:, it:it + 1], scale=-1.0,
                                                accum_out=z2[:, it:it + 1])
                last.then_inc(bA, 1)

            def ptc2(b, h, r):
                after(act, "back", "T", "pt2", h, r, b=b)
                copy(prob2T[:, r].rearrange("p j i -> p (j i)"), back_bank[0:TP, 0:PICKED], bA)

            def o2t(b, j):
                after(act, "back", "T", "o2t", j, b=b)
                copy(o2T[:, :], back_bank[:, 0:PICKED], bA)

            eneg_ = small[:, 6:12]
            run(act, "A", {("front", "eneg"): eneg, ("front", "h1"): h1_, ("front", "xnt"): xnt, ("front", "v"): v, ("front", "q"): q,
                           ("front", "k"): k, ("front", "p"): p, ("front", "ptc"): ptc, ("front", "o1t"): o1t, ("top", "qpk"): qpk,
                           ("top", "sim"): sim, ("top", "wexp"): wexp, ("top", "hi"): hi, ("top", "keep_hi"): keep_hi, ("combo", "combo"): combo, ("back", "knt"): knt,
                           ("back", "q2"): q2, ("back", "p2"): p2, ("back", "ptc2"): ptc2, ("back", "o2t"): o2t}, dense, flush)

        @block.vector
        def _(dve):
            V = nc.vector
            fV, tV, bV = (done[thread, "V"] for thread in ("front", "top", "back"))

            dve.wait_ge(const_pe, 1)
            dve.wait_ge(const_pool, CONSTS)
            ext0 = small[0:HEADS, 40:41]
            V.tensor_copy(ext0, fa[0:HEADS, 0:1]).then_inc(const_dve0, 1)
            dve.wait_ge(const_dve0, 1)
            V.tensor_scalar(ext[:, 123:250], fa[0:HEADS, 0:127], ext0, -1.0, ALU.subtract, ALU.mult).then_inc(const_dve, 2)

            dve.wait_ge(weights_loaded, N_WEIGHTS)
            for k, factor in enumerate((DH ** -0.5, -1.0)):
                first = w_qk[:, k, :, :, 0:DH].rearrange("p g h d -> p (g h) d")
                for copy_ in (1, 2):
                    V.tensor_scalar(w_qk[:, k, :, :, copy_ * DH:copy_ * DH + DH].rearrange("p g h d -> p (g h) d"), first, factor, None, ALU.mult).then_inc(heads_scaled, 1)
            dve.wait_ge(heads_scaled, 4)
            for k, factor in enumerate((DH ** -0.5, -1.0)):
                first = w_qk[:, k, :, :, 0:DH].rearrange("p g h d -> p (g h) d")
                V.tensor_scalar(first, first, factor, None, ALU.mult).then_inc(heads_scaled, 1)
            for k, rows_ in enumerate((2, 1)):
                V.tensor_reduce(is_lo[:, k:k + 1], ident[:, :].rearrange("p (h d) -> p h d", h=4)[:, :, rows_ * DH:rows_ * DH + DH], AX.XY, ALU.add).then_inc(split_ready, 1)
            dve.wait_ge(split_ready, 2)

            def score_(b):
                after(dve, "front", "G", "score_mul", b=b)
                after(dve, "front", "T", "rowbc", b=b - 1)
                V.tensor_reduce(score, xw[:, :, :], AX.X, ALU.add).then_inc(fV, 1)

            def den_(b):
                after(dve, "front", "A", "eneg", b=b)
                V.tensor_scalar(den, eneg, 1.0, None, ALU.add).then_inc(fV, 1)

            def gate_(b):
                after(dve, "front", "V", "den", b=b)
                V.reciprocal(gate, den).then_inc(fV, 1)

            def rank_(b, t, part):
                if (t, part) == (0, 0):
                    after(dve, "front", "T", "rowbc", b=b)
                else:
                    after(dve, "front", "V", "rank", *((t, 0) if part else (t - 1, 1)), b=b)
                at, lag = part * 375, (5 - t) * TP
                V.scalar_tensor_tensor(out=junk[:, at:at + 375], in0=fa2[part][0:TP, 0:375], scalar=score[:, t:t + 1],
                                       in1=ties[:, lag + at:lag + at + 375], op0=ALU.subtract, op1=ALU.is_gt,
                                       accum_out=rank2[:, part * 6 + t:part * 6 + t + 1]).then_inc(fV, 1)

            rank2 = small[:, 42:54]

            def ranks(b):
                after(dve, "front", "V", "rank", XT - 1, 1, b=b)
                V.tensor_tensor(rank, rank2[:, 0:6], rank2[:, 6:12], ALU.add).then_inc(fV, 1)

            def rows(i):
                return (h1, h2)[i - 1]

            def sum_(b, i):
                if i == 1:
                    after(dve, "front", "A", "h1", b=b)
                else:
                    after(dve, "front", "V", "h2", b=b)
                V.tensor_reduce(stat[:, 0, :], rows(i)[:, :, :], AX.X, ALU.add).then_inc(fV, 1)

            def mean(b, i):
                after(dve, "front", "V", "sum", i, b=b)
                V.tensor_scalar(stat[:, 1, :], stat[:, 0, :], 1.0 / DIM, None, ALU.mult).then_inc(fV, 1)

            def wide(ap):
                return ap.unsqueeze(2).broadcast_to([TP, NT, DIM])

            def cen_(b, i):
                after(dve, "front", "V", "mean", i, b=b)
                V.tensor_tensor(cen[:, :, :], rows(i)[:, :, :], wide(stat[:, 1, :]), ALU.subtract).then_inc(fV, 1)

            def var(b, i):
                after(dve, "front", "G", "sq", i, b=b)
                V.tensor_reduce(stat[:, 2, :], sq[:, :, :], AX.X, ALU.add).then_inc(fV, 1)

            def veps(b, i):
                after(dve, "front", "V", "var", i, b=b)
                V.tensor_scalar(stat[:, 3, :], stat[:, 2, :], 1.0 / DIM, 1e-5, ALU.mult, ALU.add).then_inc(fV, 1)

            def xn_(b, i):
                after(dve, "front", "G", "rstd", i, b=b)
                after(dve, "front", "T", "xnt", 3 - i, b=b - (i == 1))
                V.tensor_tensor(xn[:, :, :], cen[:, :, :], wide(stat[:, 4, :]), ALU.mult).then_inc(fV, 1)

            def split(which, bank, hi_, out_):
                def f(b, gr):
                    after(dve, "front", "A", which, gr, b=b)
                    V.scalar_tensor_tensor(out=out_, in0=hi_, scalar=is_lo[:, "qk".index(which):"qk".index(which) + 1], in1=bank[:, 0:PICKED],
                                           op0=ALU.mult, op1=ALU.subtract).then_inc(fV, 1)
                return f

            def low_(b, gr, n):
                after(dve, "front", "T", "qk", gr, n, b=b)
                V.tensor_reduce(low[:, n % 2:n % 2 + 1], fa[0:TP, 0:PICKED], AX.X, ALU.min).then_inc(fV, 1)

            def rz_(b, gr):
                after(dve, "front", "A", "p", gr, 11, b=b)
                V.reciprocal(rz[:, gr * 12:gr * 12 + 12], zsum[:, gr * 12:gr * 12 + 12]).then_inc(fV, 1)

            def v_lo(b):
                after(dve, "front", "A", "v", b=b)
                V.tensor_tensor(vtok[:, :, :, 1, :].rearrange("p t h d -> p (t h) d"), fa[0:TP, 0:NT * DIM].rearrange("p (n d) -> p n d", d=DH),
                                vtok[:, :, :, 0, :].rearrange("p t h d -> p (t h) d"), ALU.subtract).then_inc(fV, 1)

            def pt_lo(b, gr, n):
                after(dve, "front", "A", "ptc", gr, n, b=b)
                V.tensor_tensor(probT[:, n % 2, 1, :], fb[0:TP, 0:PICKED], probT[:, n % 2, 0, :], ALU.subtract).then_inc(fV, 1)

            def o1_sum(b, gr, pair):
                after(dve, "front", "T", "pv_end", gr, b=b)
                after(dve, "front", "V", "o1", 1 - gr, pair, b=b - (gr == 0))
                parts = fa2[pair][0:TP, 384:480].rearrange("p (n s d) -> p n d s", s=2, d=DH)
                V.tensor_reduce(o1_whole[:, pair].rearrange("p t h d -> p (t h) d"), parts, AX.X, ALU.add).then_inc(fV, 1)

            def o1_(b, gr, pair):
                after(dve, "front", "V", "o1_sum", gr, pair, b=b)
                after(dve, "front", "V", "rz", gr, b=b)
                after(dve, "front", "T", "o1t", b=b - 1)
                at = gr * 32 + pair * 2 * DH
                V.tensor_tensor(o1[:, :, at:at + 2 * DH].rearrange("p t (h d) -> p t h d", h=2), o1_whole[:, pair],
                                rz[:, gr * 12:gr * 12 + 12].rearrange("p (t h) -> p t h", t=NT)[:, :, 2 * pair:2 * pair + 2].unsqueeze(3).broadcast_to([TP, NT, 2, DH]),
                                ALU.mult).then_inc(fV, 1)

            def h2_(b):
                after(dve, "front", "T", "proj", b=b)
                after(dve, "back", "G", "keep_h2", b=b - 1)
                V.tensor_tensor(h2[:, :, :], h1[:, :, :], fa[0:TP, 0:NT * DIM].rearrange("p (t f) -> p t f", t=NT), ALU.add).then_inc(fV, 1)

            def group(gr, it, q):
                return sims[:, gr, it].rearrange("p h q k -> p (h q) k")[:, q, :]

            def max_a(b, gr, it, q):
                if q == 0:
                    after_alone(dve, "top", "A", "sim", gr, it, b=b)
                V.max(top[:, it, q, 0:8], group(gr, it, q)).then_inc(tV, 1)

            def cut_a(b, gr, it, q):
                if q == 0:
                    after_alone(dve, "top", "V", "max_a", gr, it, 7, b=b)
                V.match_replace(left[:, q, :], top[:, it, q, 0:8], group(gr, it, q), -3e38).then_inc(tV, 1)

            def max_b(b, gr, it, q):
                if q == 0:
                    after_alone(dve, "top", "V", "cut_a", gr, it, 7, b=b)
                V.max(top[:, it, q, 8:16], left[:, q, :]).then_inc(tV, 1)

            def cut_b(b, gr, it, q):
                if q == 0:
                    after_alone(dve, "top", "V", "max_b", gr, it, 7, b=b)
                V.match_replace(left[:, q, :], top[:, it, q, 8:16], left[:, q, :], -3e38).then_inc(tV, 1)

            def max_c(b, gr, it):
                after(dve, "top", "V", "cut_b", gr, it, 7, b=b)
                V.tensor_reduce(top[:, it, :, 16:17].rearrange("p q o -> p (q o)"), left[:, :, :], AX.X, ALU.max).then_inc(tV, 1)

            def cmax_a(b, gr, it, q):
                if q == 0:
                    after_alone(dve, "top", "G", "cand", gr, it, 6, b=b)
                V.max(best[:, it, q, 0:8], cand[:, q, :]).then_inc(tV, 1)

            def ccut_a(b, gr, it, q):
                if q == 0:
                    after_alone(dve, "top", "V", "cmax_a", gr, it, 3, b=b)
                V.match_replace(cand[:, q, :], best[:, it, q, 0:8], cand[:, q, :], -3e38).then_inc(tV, 1)

            def cmax_b(b, gr, it, q):
                if q == 0:
                    after_alone(dve, "top", "V", "ccut_a", gr, it, 3, b=b)
                V.max(best[:, it, q, 8:16], cand[:, q, :]).then_inc(tV, 1)

            def ccut_b(b, gr, it, q):
                if q == 0:
                    after_alone(dve, "top", "V", "cmax_b", gr, it, 3, b=b)
                V.match_replace(cand[:, q, :], best[:, it, q, 8:16], cand[:, q, :], -3e38).then_inc(tV, 1)

            def cmax_c(b, gr, it):
                after(dve, "top", "V", "ccut_b", gr, it, 3, b=b)
                V.tensor_reduce(best[:, it, :, 16:17].rearrange("p h o -> p (h o)"), cand[:, :, :], AX.X, ALU.max).then_inc(tV, 1)

            best2 = best[:, :, :, :].rearrange("p t h k -> p (t h) k")
            top2 = top[:, :, :, :].rearrange("p t (h q) k -> p (t h) q k", q=2)

            def heads_of(it):
                return slice(4 * it, 4 * it + 4)

            def mid(b, gr, it):
                after(dve, "top", "V", "cmax_c", gr, it, b=b)
                V.tensor_tensor(cut[:, 0, heads_of(it)], best2[:, heads_of(it), 15], best2[:, heads_of(it), 16], ALU.add).then_inc(tV, 1)

            def floor(b, gr, it):
                V.tensor_scalar(cut[:, 1, heads_of(it)], best2[:, heads_of(it), 0], -SPAN, None, ALU.add).then_inc(tV, 1)

            def thr(b, gr, it):
                after(dve, "top", "V", "floor", gr, it, b=b)
                V.scalar_tensor_tensor(out=cut[:, 2, heads_of(it)], in0=cut[:, 0, heads_of(it)], scalar=0.5, in1=cut[:, 1, heads_of(it)],
                                       op0=ALU.mult, op1=ALU.max).then_inc(tV, 1)

            def off1(b, gr, it):
                after(dve, "top", "G", "shift", 1 - gr, it, b=b - (gr == 0))
                V.tensor_scalar(off[:, heads_of(it), 0], top2[:, heads_of(it), 0, 0], -1.0, None, ALU.mult).then_inc(tV, 1)

            def off0(b, gr, it):
                after(dve, "top", "V", "thr", gr, it, b=b)
                V.tensor_tensor(off[:, heads_of(it), 1], top2[:, heads_of(it), 0, 0], cut[:, 2, heads_of(it)], ALU.subtract).then_inc(tV, 1)

            def diff(b, gr):
                after(dve, "top", "V", "thr", gr, NT - 1, b=b)
                V.tensor_tensor(wk[:, :, :], best2[:, :, 0:16], cut[:, 2, :].unsqueeze(2).broadcast_to([TP, NT * 4, TOPK]), ALU.subtract).then_inc(tV, 1)

            def zk_(b, gr):
                after(dve, "top", "A", "wexp", gr, b=b)
                V.tensor_reduce(zk[:, :], wke[:, :, :], AX.X, ALU.add).then_inc(tV, 1)

            def rzk_(b, gr):
                after(dve, "top", "V", "zk", gr, b=b)
                after(dve, "back", "V", "kvn", 4 * gr + 3, b=b - 1)
                V.reciprocal(rzk[:, gr, :], zk[:, :]).then_inc(tV, 1)

            def dense(b, u):
                dve.wait_ge(pair_exps, b * SLOTS + u + 1)
                V.scalar_tensor_tensor(out=weight[:, u % 4, :], in0=score_bank(u)[:, 0:PICKED], scalar=0.0, in1=weight[:, u % 4, :],
                                       op0=ALU.is_ge, op1=ALU.mult).then_inc(pair_weights, 1)

            def kvn(b, h):
                after(dve, "back", "T", "kvt", h, b=b)
                after(dve, "top", "V", "rzk", h // 4, b=b)
                if h > 0:
                    after(dve, "back", "T", "pv2", h - 1, b=b)
                else:
                    after(dve, "back", "T", "pv2", HEADS - 1, b=b - 1)
                r = rzk[:, h // 4, :].rearrange("p (t h) -> p t h", t=NT)[:, :, h % 4].unsqueeze(2).broadcast_to([TP, NT, 128])
                V.tensor_tensor(kv[:, :, :], back_bank[0:TP, 0:NT * 128].rearrange("p (t c) -> p t c", t=NT), r, ALU.mult).then_inc(bV, 1)

            def low2_(b, h, r):
                after(dve, "back", "T", "qk2", h, r, b=b)
                if r == 0:
                    V.tensor_reduce(low2[:, 0:1], back_bank[0:TP, 0:TP], AX.X, ALU.min)
                    V.tensor_reduce(low2[:, 1:2], back_bank[0:TP, TP:3 * TP], AX.X, ALU.min).then_inc(bV, 1)
                else:
                    V.tensor_reduce(low2[:, 2:3], back_bank[0:TP, 0:3 * TP], AX.X, ALU.min).then_inc(bV, 1)

            def rz2_(b, h):
                after(dve, "back", "A", "p2", h, 1, b=b)
                V.reciprocal(rz2[:, :], z2[:, :]).then_inc(bV, 1)

            def o2_(b, h):
                after(dve, "back", "T", "pv2", h, b=b)
                after(dve, "back", "V", "rz2", h, b=b)
                V.tensor_tensor(o2[:, :, 64 * (h % 2):64 * (h % 2) + 64], back_bank[0:TP, 0:NT * DIM].rearrange("p (t f) -> p t f", t=NT),
                                wide(rz2[:, :]), ALU.mult).then_inc(bV, 1)

            def acc(b, j):
                after(dve, "back", "T", "wo", j, b=b)
                after(dve, "back", "G", "keep_h2", b=b)
                V.tensor_tensor(result[:, :, :], result[:, :, :], back_bank[0:TP, 0:NT * DIM].rearrange("p (t f) -> p t f", t=NT), ALU.add).then_inc(bV, 1)

            run(dve, "V", {("front", "score"): score_, ("front", "den"): den_, ("front", "gate"): gate_,
                           ("front", "rank"): rank_, ("front", "ranks"): ranks, 
                           ("front", "sum"): sum_, ("front", "mean"): mean, ("front", "cen"): cen_, 
                           ("front", "var"): var, ("front", "veps"): veps, ("front", "xn"): xn_, ("front", "low"): low_,
                           ("front", "q"): split("q", fa, q_hi, qT), ("front", "k"): split("k", fb, k_hi, kT), ("front", "rz"): rz_, ("front", "v_lo"): v_lo, ("front", "pt_lo"): pt_lo, ("front", "o1_sum"): o1_sum, ("front", "o1"): o1_, ("front", "h2"): h2_,
                           ("top", "max_a"): max_a, ("top", "cut_a"): cut_a, ("top", "max_b"): max_b, ("top", "cut_b"): cut_b,
                           ("top", "max_c"): max_c, ("top", "cmax_a"): cmax_a, ("top", "ccut_a"): ccut_a,
                           ("top", "cmax_b"): cmax_b, ("top", "ccut_b"): ccut_b, ("top", "cmax_c"): cmax_c, ("top", "mid"): mid,
                           ("top", "floor"): floor, ("top", "thr"): thr, ("top", "diff"): diff, ("top", "zk"): zk_,
                           ("top", "rzk"): rzk_, ("top", "off1"): off1, ("top", "off0"): off0,
                           ("back", "kvn"): kvn, ("back", "low2"): low2_, ("back", "rz2"): rz2_,
                           ("back", "o2"): o2_, ("back", "acc"): acc}, dense, lambda b: None)


_INS = ['x', 'L0_tok_score_proj', 'L0_attn_qkv_w', 'L0_attn_qkv_b', 'L0_attn_proj_w', 'L0_attn_proj_b', 'L0_attn_rpb_table',
        'L0_ffn_Wq_pk', 'L0_ffn_pk_keys', 'L0_ffn_Wq', 'kv_table', 'L0_ffn_Wo']
_OUTS = [((16, 375, 64), 'float32')]


def kernel(**inputs):
    import numpy as _np
    import concourse.bacc as _bacc
    from concourse import mybir as _mybir
    from concourse.bass_utils import run_bass_kernel_spmd as _run

    nc = _bacc.Bacc("TRN2", target_bir_lowering=False, num_devices=1)
    laid = dict(inputs)
    k, v = (_np.asarray(inputs[n]).reshape(HEADS, -1, DIM) for n in ('L0_ffn_keys_table', 'L0_ffn_values_table'))
    laid['kv_table'] = _np.concatenate([_np.concatenate([(k, v)[h % 2][h], (v, k)[h % 2][h]], axis=1) for h in range(HEADS)])
    arrays, args = {}, []
    for name in _INS:
        a = _np.ascontiguousarray(laid[name])
        arrays[f"in_{name}_dram"] = a
        args.append(nc.dram_tensor(f"in_{name}_dram", a.shape, _mybir.dt.from_np(a.dtype), kind="ExternalInput").ap())
    for i, (shape, dtype) in enumerate(_OUTS):
        dt = _mybir.dt.from_np(_np.dtype(dtype))
        args.append(nc.dram_tensor(f"out_{i}_dram", shape, dt, kind="ExternalOutput").ap())
    build_kernel(nc, *args)
    r = _run(nc, [arrays], core_ids=[0])
    return r.results[0]["out_0_dram"]
```
